# Optimizing a Trainium2 kernel written in Bass

```python
import numpy as np
import jax
import jax.numpy as jnp

def _softmax(x, axis=-1):
    return jax.nn.softmax(x, axis=axis)

def _gelu(x):
    return jax.nn.gelu(x, approximate=True)

def _silu(x):
    return jax.nn.silu(x)

def _sigmoid(x):
    return jax.nn.sigmoid(x)

def _layernorm(x, axis=-1, eps=1e-05):
    m = jnp.mean(x, axis=axis, keepdims=True)
    v = jnp.var(x, axis=axis, keepdims=True)
    return (x - m) / jnp.sqrt(v + eps)

def _scatter_add(tgt, idx, src, axis=0):
    return tgt.at[idx].add(src)

def _segment_sum(src, seg, n):
    return jax.ops.segment_sum(src, seg, n)
kernel_name = 'mk_seq_preln_d2_jaxref_r8_b22186'

def setup_inputs(seed: int=0):
    np.random.seed(seed)
    _w = jnp.asarray

    def _L0_attn_setup():
        import jax, jax.numpy as jnp
        import numpy as np
        B, S, D = (2, 256, 128)
        H, DH = (16, 64)
        DQL, DKVL = (64, 64)
        DR = 64
        TOPK = 64
        LN_EPS = 1e-05
        ROPE_BASE = 10000.0

        def _rope_tables(seq_len, dim):
            inv_freq = 1.0 / ROPE_BASE ** (np.arange(0, dim, 2, dtype=np.float32) / dim)
            t = np.arange(seq_len, dtype=np.float32)
            freqs = np.outer(t, inv_freq)
            cos = np.concatenate([np.cos(freqs), np.cos(freqs)], -1)[:, ::2]
            sin = np.concatenate([np.sin(freqs), np.sin(freqs)], -1)[:, ::2]
            return (jnp.asarray(cos), jnp.asarray(sin))

        def _apply_rope_subspace(x, d_rope):
            s = x.shape[-2]
            cos, sin = _rope_tables(s, d_rope)
            xr, xp = (x[..., :d_rope], x[..., d_rope:])
            e, o = (xr[..., 0::2], xr[..., 1::2])
            rot = jnp.stack([e * cos - o * sin, e * sin + o * cos], axis=-1).reshape(xr.shape)
            return jnp.concatenate([rot, xp], axis=-1)

        def _reference_tuple_inner(x, w_down_q, w_down_kv, w_up_q, w_up_k, w_up_v, w_out, ln_scale, ln_bias):
            b, s, d = x.shape
            residual = x
            mu = jnp.mean(x, axis=-1, keepdims=True)
            var = jnp.mean((x - mu) ** 2, axis=-1, keepdims=True)
            h = (x - mu) * jax.lax.rsqrt(var + LN_EPS) * ln_scale + ln_bias
            c_q = h @ w_down_q.T
            c_kv = h @ w_down_kv.T
            q = (c_q @ w_up_q.T).reshape(b, s, H, DH).transpose(0, 2, 1, 3)
            k = (c_kv @ w_up_k.T).reshape(b, s, H, DH).transpose(0, 2, 1, 3)
            v = (c_kv @ w_up_v.T).reshape(b, s, H, DH).transpose(0, 2, 1, 3)
            q = _apply_rope_subspace(q, DR)
            k = _apply_rope_subspace(k, DR)
            scale = 1.0 / np.sqrt(DH).astype(np.float32)
            scores = jnp.einsum('bhqd,bhkd->bhqk', q, k) * scale
            _, indices = jax.lax.top_k(scores, min(TOPK, s))
            attn = jax.nn.softmax(scores, axis=-1)
            out = jnp.einsum('bhqk,bhkd->bhqd', attn, v)
            out = out.transpose(0, 2, 1, 3).reshape(b, s, H * DH)
            out = out @ w_out.T + residual
            return (out, indices.astype(jnp.int64))
        key = jax.random.key(seed)
        ks = jax.random.split(key, 7)
        init = lambda k, shape: jax.random.normal(k, shape, jnp.float32) * 0.02
        return {'x': jax.random.normal(ks[0], (B, S, D), jnp.float32), 'w_down_q': init(ks[1], (DQL, D)), 'w_down_kv': init(ks[2], (DKVL, D)), 'w_up_q': init(ks[3], (H * DH, DQL)), 'w_up_k': init(ks[4], (H * DH, DKVL)), 'w_up_v': init(ks[5], (H * DH, DKVL)), 'w_out': init(ks[6], (D, H * DH)), 'ln_scale': jnp.ones((D,), jnp.float32), 'ln_bias': jnp.zeros((D,), jnp.float32)}
    _L0_attn_in = _L0_attn_setup()

    def _L0_ffn_setup():
        import jax, jax.numpy as jnp
        import numpy as np
        TOPK = 4
        N_GROUPS = 4
        TOPK_GROUPS = 2
        ROUTE_SCALE = 2.5

        def _gate(x2, Wg):
            T = x2.shape[0]
            E = Wg.shape[0]
            scores = x2 @ Wg.T
            s = jax.nn.sigmoid(scores)
            g = s.reshape(T, N_GROUPS, E // N_GROUPS)
            group_scores = g.max(axis=-1)
            _, gidx = jax.lax.top_k(group_scores, TOPK_GROUPS)
            group_mask = jnp.any(jax.nn.one_hot(gidx, N_GROUPS, dtype=jnp.bool_), axis=1)
            masked = jnp.where(group_mask[:, :, None], g, -jnp.inf).reshape(T, E)
            _, idx = jax.lax.top_k(masked, TOPK)
            w = jnp.take_along_axis(s, idx, axis=1)
            w = w / jnp.sum(w, axis=-1, keepdims=True)
            w = w * ROUTE_SCALE
            return (w.astype(x2.dtype), idx)
        key = jax.random.key(seed)
        ks = jax.random.split(key, 6)
        B, S, D, I, E = (2, 256, 128, 128, 16)
        scale = 0.02
        return {'x': jax.random.normal(ks[0], (B, S, D), dtype=jnp.float32), 'Wg': jax.random.normal(ks[1], (E, D), dtype=jnp.float32) * scale, 'W1': jax.random.normal(ks[2], (E, I, D), dtype=jnp.float32) * scale, 'b1': jnp.zeros((E, I), dtype=jnp.float32), 'W2': jax.random.normal(ks[3], (E, D, I), dtype=jnp.float32) * scale, 'b2': jnp.zeros((E, D), dtype=jnp.float32), 'W3': jax.random.normal(ks[4], (E, I, D), dtype=jnp.float32) * scale, 'b3': jnp.zeros((E, I), dtype=jnp.float32)}
    _L0_ffn_in = _L0_ffn_setup()

    def _L1_attn_setup():
        import jax, jax.numpy as jnp
        import numpy as np
        B, L = (2, 128)
        D_MODEL, D_CKV, D_CQ = (128, 32, 64)
        N_HEAD, D_HEAD, D_ROPE = (8, 64, 32)
        N_IDX_HEAD = 4
        K_TS, LW = (96, 64)
        ROPE_BASE = 10000.0

        def _pope(x, angles):
            cos, sin = (jnp.cos(angles), jnp.sin(angles))
            mu1, mu2 = jnp.split(jax.nn.softplus(x), 2, axis=-1)
            return jnp.concatenate([mu1 * cos - mu2 * sin, mu1 * sin + mu2 * cos], axis=-1)

        def _forward(x, W_dkv, W_uk, W_uv, W_dq, W_uq, W_qr, W_kr, W_out, idx_wq, idx_wk, idx_w, raw_delta):
            B_, L_, _ = x.shape
            c_kv = x @ W_dkv
            q_i = (x @ idx_wq).reshape(B_, L_, N_IDX_HEAD, D_HEAD)
            k_i = x @ idx_wk
            s_i = jax.nn.relu(jnp.einsum('bthd,bsd->bths', q_i, k_i))
            I = jnp.einsum('bths,h->bts', s_i, idx_w)
            qpos = jnp.arange(L_)[:, None]
            kpos = jnp.arange(L_)[None, :]
            local = (kpos >= qpos - LW + 1) & (kpos <= qpos)
            causal = kpos > qpos
            I = jnp.where(local[None], jnp.inf, I)
            I = jnp.where(causal[None], -jnp.inf, I)
            kk = min(K_TS, L_)
            _, idx = jax.lax.top_k(I, kk)
            bi = jnp.arange(B_)[:, None, None]
            key_c = (c_kv @ W_uk)[bi, idx].reshape(B_, L_, kk, N_HEAD, D_HEAD)
            value = (c_kv @ W_uv)[bi, idx].reshape(B_, L_, kk, N_HEAD, D_HEAD)
            c_q = x @ W_dq
            query_c = (c_q @ W_uq).reshape(B_, L_, N_HEAD, D_HEAD)
            half = D_ROPE // 2
            theta = 1.0 / ROPE_BASE ** (2.0 * jnp.arange(half, dtype=jnp.float32) / D_ROPE)
            delta = -2.0 * jnp.pi * jax.nn.sigmoid(raw_delta)
            angles_q = jnp.arange(L_, dtype=jnp.float32)[:, None] * theta[None, :] + delta
            query_r = _pope((c_q @ W_qr).reshape(B_, L_, N_HEAD, D_ROPE), angles_q[None, :, None, :])
            kr_sel = (x @ W_kr)[bi, idx]
            angles_k = jnp.arange(kk, dtype=jnp.float32)[:, None] * theta[None, :] + delta
            key_r = _pope(kr_sel, angles_k[None, None, :, :])
            scale = (D_HEAD + D_ROPE) ** (-0.5)
            q_c = query_c.transpose(0, 2, 1, 3)
            q_r = query_r.transpose(0, 2, 1, 3)
            k_c = key_c.transpose(0, 3, 1, 2, 4)
            v = value.transpose(0, 3, 1, 2, 4)
            scores = (jnp.einsum('bhld,bhlkd->bhlk', q_c, k_c) + jnp.einsum('bhld,blkd->bhlk', q_r, key_r)) * scale
            attn = jax.nn.softmax(scores.astype(jnp.float32), axis=-1).astype(v.dtype)
            out = jnp.einsum('bhlk,bhlkd->bhld', attn, v)
            out = out.transpose(0, 2, 1, 3).reshape(B_, L_, N_HEAD * D_HEAD)
            return out @ W_out
        key = jax.random.key(seed)
        ks = jax.random.split(key, 14)

        def w(k, shape, fan_in):
            return jax.random.normal(k, shape, dtype=jnp.float32) * fan_in ** (-0.5)
        return {'x': jax.random.normal(ks[0], (B, L, D_MODEL), dtype=jnp.float32), 'W_dkv': w(ks[1], (D_MODEL, D_CKV), D_MODEL), 'W_uk': w(ks[2], (D_CKV, N_HEAD * D_HEAD), D_CKV), 'W_uv': w(ks[3], (D_CKV, N_HEAD * D_HEAD), D_CKV), 'W_dq': w(ks[4], (D_MODEL, D_CQ), D_MODEL), 'W_uq': w(ks[5], (D_CQ, N_HEAD * D_HEAD), D_CQ), 'W_qr': w(ks[6], (D_CQ, N_HEAD * D_ROPE), D_CQ), 'W_kr': w(ks[7], (D_MODEL, D_ROPE), D_MODEL), 'W_out': w(ks[8], (N_HEAD * D_HEAD, D_MODEL), N_HEAD * D_HEAD), 'idx_wq': w(ks[9], (D_MODEL, N_IDX_HEAD * D_HEAD), D_MODEL), 'idx_wk': w(ks[10], (D_MODEL, D_HEAD), D_MODEL), 'idx_w': jnp.ones((N_IDX_HEAD,), dtype=jnp.float32), 'raw_delta': jax.random.normal(ks[11], (D_ROPE // 2,), dtype=jnp.float32) * 0.1}
    _L1_attn_in = _L1_attn_setup()

    def _L1_ffn_setup():
        import jax, jax.numpy as jnp
        import numpy as np
        E = 8
        TOPK = 2
        PRIME = 11
        HASH_OFF = 7919
        N_SHARED = 1
        key = jax.random.key(seed)
        ks = jax.random.split(key, 8)
        B, T, C, Hs, Hr = (4, 1024, 128, 256, 128)
        sc = lambda k, shape, fan: jax.random.normal(k, shape, jnp.float32) * fan ** (-0.5)
        return {'x': jax.random.normal(ks[0], (B, T, C), jnp.float32), 't_emb': jax.random.normal(ks[1], (B, C), jnp.float32), 'sw1': sc(ks[2], (C, Hs), C), 'sb1': jnp.zeros((Hs,), jnp.float32), 'sw3': sc(ks[3], (C, Hs), C), 'sb3': jnp.zeros((Hs,), jnp.float32), 'sw2': sc(ks[4], (Hs, C), Hs), 'sb2': jnp.zeros((C,), jnp.float32), 'w1': sc(ks[5], (E, C, Hr), C), 'b1': jnp.zeros((E, Hr), jnp.float32), 'w2': sc(ks[6], (E, Hr, C), Hr), 'b2': jnp.zeros((E, C), jnp.float32)}
    _L1_ffn_in = _L1_ffn_setup()
    _d = {'L0_attn_x': _L0_attn_in['x'], 'L0_attn_w_down_q': _L0_attn_in['w_down_q'], 'L0_attn_w_down_kv': _L0_attn_in['w_down_kv'], 'L0_attn_w_up_q': _L0_attn_in['w_up_q'], 'L0_attn_w_up_k': _L0_attn_in['w_up_k'], 'L0_attn_w_up_v': _L0_attn_in['w_up_v'], 'L0_attn_w_out': _L0_attn_in['w_out'], 'L0_attn_ln_scale': _L0_attn_in['ln_scale'], 'L0_attn_ln_bias': _L0_attn_in['ln_bias'], 'L0_ffn_Wg': _L0_ffn_in['Wg'], 'L0_ffn_W1': _L0_ffn_in['W1'], 'L0_ffn_b1': _L0_ffn_in['b1'], 'L0_ffn_W2': _L0_ffn_in['W2'], 'L0_ffn_b2': _L0_ffn_in['b2'], 'L0_ffn_W3': _L0_ffn_in['W3'], 'L0_ffn_b3': _L0_ffn_in['b3'], 'L1_attn_W_dkv': _L1_attn_in['W_dkv'], 'L1_attn_W_uk': _L1_attn_in['W_uk'], 'L1_attn_W_uv': _L1_attn_in['W_uv'], 'L1_attn_W_dq': _L1_attn_in['W_dq'], 'L1_attn_W_uq': _L1_attn_in['W_uq'], 'L1_attn_W_qr': _L1_attn_in['W_qr'], 'L1_attn_W_kr': _L1_attn_in['W_kr'], 'L1_attn_W_out': _L1_attn_in['W_out'], 'L1_attn_idx_wq': _L1_attn_in['idx_wq'], 'L1_attn_idx_wk': _L1_attn_in['idx_wk'], 'L1_attn_idx_w': _L1_attn_in['idx_w'], 'L1_attn_raw_delta': _L1_attn_in['raw_delta'], 'L1_ffn_t_emb': _L1_ffn_in['t_emb'], 'L1_ffn_sw1': _L1_ffn_in['sw1'], 'L1_ffn_sb1': _L1_ffn_in['sb1'], 'L1_ffn_sw3': _L1_ffn_in['sw3'], 'L1_ffn_sb3': _L1_ffn_in['sb3'], 'L1_ffn_sw2': _L1_ffn_in['sw2'], 'L1_ffn_sb2': _L1_ffn_in['sb2'], 'L1_ffn_w1': _L1_ffn_in['w1'], 'L1_ffn_b1': _L1_ffn_in['b1'], 'L1_ffn_w2': _L1_ffn_in['w2'], 'L1_ffn_b2': _L1_ffn_in['b2']}
    _x0 = _d['L0_attn_x']
    _d['L0_attn_x'] = jax.random.normal(jax.random.fold_in(jax.random.key(seed), 1), (1, 2048, 128), dtype=_x0.dtype)
    del _x0
    return _d

def reference(L0_attn_x, L0_attn_w_down_q, L0_attn_w_down_kv, L0_attn_w_up_q, L0_attn_w_up_k, L0_attn_w_up_v, L0_attn_w_out, L0_attn_ln_scale, L0_attn_ln_bias, L0_ffn_Wg, L0_ffn_W1, L0_ffn_b1, L0_ffn_W2, L0_ffn_b2, L0_ffn_W3, L0_ffn_b3, L1_attn_W_dkv, L1_attn_W_uk, L1_attn_W_uv, L1_attn_W_dq, L1_attn_W_uq, L1_attn_W_qr, L1_attn_W_kr, L1_attn_W_out, L1_attn_idx_wq, L1_attn_idx_wk, L1_attn_idx_w, L1_attn_raw_delta, L1_ffn_t_emb, L1_ffn_sw1, L1_ffn_sb1, L1_ffn_sw3, L1_ffn_sb3, L1_ffn_sw2, L1_ffn_sb2, L1_ffn_w1, L1_ffn_b1, L1_ffn_w2, L1_ffn_b2):

    def _L0_attn_ref(x, w_down_q, w_down_kv, w_up_q, w_up_k, w_up_v, w_out, ln_scale, ln_bias):
        import jax, jax.numpy as jnp
        import numpy as np
        B, S, D = (2, 256, 128)
        H, DH = (16, 64)
        DQL, DKVL = (64, 64)
        DR = 64
        TOPK = 64
        LN_EPS = 1e-05
        ROPE_BASE = 10000.0

        def _rope_tables(seq_len, dim):
            inv_freq = 1.0 / ROPE_BASE ** (np.arange(0, dim, 2, dtype=np.float32) / dim)
            t = np.arange(seq_len, dtype=np.float32)
            freqs = np.outer(t, inv_freq)
            cos = np.concatenate([np.cos(freqs), np.cos(freqs)], -1)[:, ::2]
            sin = np.concatenate([np.sin(freqs), np.sin(freqs)], -1)[:, ::2]
            return (jnp.asarray(cos), jnp.asarray(sin))

        def _apply_rope_subspace(x, d_rope):
            s = x.shape[-2]
            cos, sin = _rope_tables(s, d_rope)
            xr, xp = (x[..., :d_rope], x[..., d_rope:])
            e, o = (xr[..., 0::2], xr[..., 1::2])
            rot = jnp.stack([e * cos - o * sin, e * sin + o * cos], axis=-1).reshape(xr.shape)
            return jnp.concatenate([rot, xp], axis=-1)

        def _reference_tuple_inner(x, w_down_q, w_down_kv, w_up_q, w_up_k, w_up_v, w_out, ln_scale, ln_bias):
            b, s, d = x.shape
            residual = x
            mu = jnp.mean(x, axis=-1, keepdims=True)
            var = jnp.mean((x - mu) ** 2, axis=-1, keepdims=True)
            h = (x - mu) * jax.lax.rsqrt(var + LN_EPS) * ln_scale + ln_bias
            c_q = h @ w_down_q.T
            c_kv = h @ w_down_kv.T
            q = (c_q @ w_up_q.T).reshape(b, s, H, DH).transpose(0, 2, 1, 3)
            k = (c_kv @ w_up_k.T).reshape(b, s, H, DH).transpose(0, 2, 1, 3)
            v = (c_kv @ w_up_v.T).reshape(b, s, H, DH).transpose(0, 2, 1, 3)
            q = _apply_rope_subspace(q, DR)
            k = _apply_rope_subspace(k, DR)
            scale = 1.0 / np.sqrt(DH).astype(np.float32)
            scores = jnp.einsum('bhqd,bhkd->bhqk', q, k) * scale
            _, indices = jax.lax.top_k(scores, min(TOPK, s))
            attn = jax.nn.softmax(scores, axis=-1)
            out = jnp.einsum('bhqk,bhkd->bhqd', attn, v)
            out = out.transpose(0, 2, 1, 3).reshape(b, s, H * DH)
            out = out @ w_out.T + residual
            return (out, indices.astype(jnp.int64))
        return _reference_tuple_inner(x, w_down_q, w_down_kv, w_up_q, w_up_k, w_up_v, w_out, ln_scale, ln_bias)[0]

    def _L0_ffn_ref(x, Wg, W1, b1, W2, b2, W3, b3):
        import jax, jax.numpy as jnp
        import numpy as np
        TOPK = 4
        N_GROUPS = 4
        TOPK_GROUPS = 2
        ROUTE_SCALE = 2.5

        def _gate(x2, Wg):
            T = x2.shape[0]
            E = Wg.shape[0]
            scores = x2 @ Wg.T
            s = jax.nn.sigmoid(scores)
            g = s.reshape(T, N_GROUPS, E // N_GROUPS)
            group_scores = g.max(axis=-1)
            _, gidx = jax.lax.top_k(group_scores, TOPK_GROUPS)
            group_mask = jnp.any(jax.nn.one_hot(gidx, N_GROUPS, dtype=jnp.bool_), axis=1)
            masked = jnp.where(group_mask[:, :, None], g, -jnp.inf).reshape(T, E)
            _, idx = jax.lax.top_k(masked, TOPK)
            w = jnp.take_along_axis(s, idx, axis=1)
            w = w / jnp.sum(w, axis=-1, keepdims=True)
            w = w * ROUTE_SCALE
            return (w.astype(x2.dtype), idx)
        shape = x.shape
        D = shape[-1]
        x2 = x.reshape(-1, D)
        weights, indices = _gate(x2, Wg)
        E = Wg.shape[0]
        y = jnp.zeros_like(x2)
        for e in range(E):
            we = jnp.sum(weights * (indices == e), axis=-1)
            h = jax.nn.silu(x2 @ W1[e].T + b1[e]) * (x2 @ W3[e].T + b3[e])
            y = y + (h @ W2[e].T + b2[e]) * we[:, None]
        return y.reshape(shape)

    def _L1_attn_ref(x, W_dkv, W_uk, W_uv, W_dq, W_uq, W_qr, W_kr, W_out, idx_wq, idx_wk, idx_w, raw_delta):
        import jax, jax.numpy as jnp
        import numpy as np
        B, L = (2, 128)
        D_MODEL, D_CKV, D_CQ = (128, 32, 64)
        N_HEAD, D_HEAD, D_ROPE = (8, 64, 32)
        N_IDX_HEAD = 4
        K_TS, LW = (96, 64)
        ROPE_BASE = 10000.0

        def _pope(x, angles):
            cos, sin = (jnp.cos(angles), jnp.sin(angles))
            mu1, mu2 = jnp.split(jax.nn.softplus(x), 2, axis=-1)
            return jnp.concatenate([mu1 * cos - mu2 * sin, mu1 * sin + mu2 * cos], axis=-1)

        def _forward(x, W_dkv, W_uk, W_uv, W_dq, W_uq, W_qr, W_kr, W_out, idx_wq, idx_wk, idx_w, raw_delta):
            B_, L_, _ = x.shape
            c_kv = x @ W_dkv
            q_i = (x @ idx_wq).reshape(B_, L_, N_IDX_HEAD, D_HEAD)
            k_i = x @ idx_wk
            s_i = jax.nn.relu(jnp.einsum('bthd,bsd->bths', q_i, k_i))
            I = jnp.einsum('bths,h->bts', s_i, idx_w)
            qpos = jnp.arange(L_)[:, None]
            kpos = jnp.arange(L_)[None, :]
            local = (kpos >= qpos - LW + 1) & (kpos <= qpos)
            causal = kpos > qpos
            I = jnp.where(local[None], jnp.inf, I)
            I = jnp.where(causal[None], -jnp.inf, I)
            kk = min(K_TS, L_)
            _, idx = jax.lax.top_k(I, kk)
            bi = jnp.arange(B_)[:, None, None]
            key_c = (c_kv @ W_uk)[bi, idx].reshape(B_, L_, kk, N_HEAD, D_HEAD)
            value = (c_kv @ W_uv)[bi, idx].reshape(B_, L_, kk, N_HEAD, D_HEAD)
            c_q = x @ W_dq
            query_c = (c_q @ W_uq).reshape(B_, L_, N_HEAD, D_HEAD)
            half = D_ROPE // 2
            theta = 1.0 / ROPE_BASE ** (2.0 * jnp.arange(half, dtype=jnp.float32) / D_ROPE)
            delta = -2.0 * jnp.pi * jax.nn.sigmoid(raw_delta)
            angles_q = jnp.arange(L_, dtype=jnp.float32)[:, None] * theta[None, :] + delta
            query_r = _pope((c_q @ W_qr).reshape(B_, L_, N_HEAD, D_ROPE), angles_q[None, :, None, :])
            kr_sel = (x @ W_kr)[bi, idx]
            angles_k = jnp.arange(kk, dtype=jnp.float32)[:, None] * theta[None, :] + delta
            key_r = _pope(kr_sel, angles_k[None, None, :, :])
            scale = (D_HEAD + D_ROPE) ** (-0.5)
            q_c = query_c.transpose(0, 2, 1, 3)
            q_r = query_r.transpose(0, 2, 1, 3)
            k_c = key_c.transpose(0, 3, 1, 2, 4)
            v = value.transpose(0, 3, 1, 2, 4)
            scores = (jnp.einsum('bhld,bhlkd->bhlk', q_c, k_c) + jnp.einsum('bhld,blkd->bhlk', q_r, key_r)) * scale
            attn = jax.nn.softmax(scores.astype(jnp.float32), axis=-1).astype(v.dtype)
            out = jnp.einsum('bhlk,bhlkd->bhld', attn, v)
            out = out.transpose(0, 2, 1, 3).reshape(B_, L_, N_HEAD * D_HEAD)
            return out @ W_out
        return _forward(x, W_dkv, W_uk, W_uv, W_dq, W_uq, W_qr, W_kr, W_out, idx_wq, idx_wk, idx_w, raw_delta)

    def _L1_ffn_ref(x, t_emb, sw1, sb1, sw3, sb3, sw2, sb2, w1, b1, w2, b2):
        import jax, jax.numpy as jnp
        import numpy as np
        E = 8
        TOPK = 2
        PRIME = 11
        HASH_OFF = 7919
        N_SHARED = 1
        B, T, C = x.shape
        N = B * T
        xf = x.reshape(N, C)
        shared = jax.nn.silu(xf @ sw1 + sb1) * (xf @ sw3 + sb3) @ sw2 + sb2
        tok = jnp.arange(N)
        out = jnp.zeros((N, C), x.dtype)
        for k in range(TOPK):
            exp_ids = (tok * PRIME + k * HASH_OFF) % E
            sort_idx = jnp.argsort(exp_ids)
            xs = xf[sort_idx].reshape(E, N // E, C)
            h = jax.nn.gelu(jnp.einsum('enc,ech->enh', xs, w1) + b1[:, None, :], approximate=False)
            y = jnp.einsum('enh,ehc->enc', h, w2) + b2[:, None, :]
            out = out.at[sort_idx].add(y.reshape(N, C))
        out = out / TOPK
        return ((shared + out) / (N_SHARED + 1)).reshape(B, T, C)
    x = L0_attn_x
    x = x + _L0_attn_ref(_layernorm(x, axis=-1), L0_attn_w_down_q, L0_attn_w_down_kv, L0_attn_w_up_q, L0_attn_w_up_k, L0_attn_w_up_v, L0_attn_w_out, L0_attn_ln_scale, L0_attn_ln_bias)
    x = x + _L0_ffn_ref(_layernorm(x, axis=-1), L0_ffn_Wg, L0_ffn_W1, L0_ffn_b1, L0_ffn_W2, L0_ffn_b2, L0_ffn_W3, L0_ffn_b3)
    x = x + _L1_attn_ref(_layernorm(x, axis=-1), L1_attn_W_dkv, L1_attn_W_uk, L1_attn_W_uv, L1_attn_W_dq, L1_attn_W_uq, L1_attn_W_qr, L1_attn_W_kr, L1_attn_W_out, L1_attn_idx_wq, L1_attn_idx_wk, L1_attn_idx_w, L1_attn_raw_delta)
    x = x + _L1_ffn_ref(_layernorm(x, axis=-1), L1_ffn_t_emb, L1_ffn_sw1, L1_ffn_sb1, L1_ffn_sw3, L1_ffn_sb3, L1_ffn_sw2, L1_ffn_sb2, L1_ffn_w1, L1_ffn_b1, L1_ffn_w2, L1_ffn_b2)
    return x

_drawn_inputs = setup_inputs


def setup_inputs(seed=0):
    import zlib

    import numpy as np

    out = dict(_drawn_inputs(seed))
    spreads = {'L0_attn_ln_scale': (1.0, 0.6),
     'L0_attn_ln_bias': (0.0, 0.8),
     'L0_ffn_b1': (0.0, 0.8),
     'L0_ffn_b2': (0.0, 0.8),
     'L0_ffn_b3': (0.0, 0.8),
     'L1_attn_idx_w': (1.0, 0.6),
     'L1_ffn_sb1': (0.0, 2.0),
     'L1_ffn_sb3': (0.0, 2.0),
     'L1_ffn_sb2': (0.0, 2.0),
     'L1_ffn_b1': (0.0, 2.0),
     'L1_ffn_b2': (0.0, 2.0)}
    factors = {'L0_attn_w_down_q': 8.0,
     'L0_attn_w_down_kv': 8.0,
     'L0_attn_w_up_q': 8.0,
     'L0_attn_w_up_k': 8.0,
     'L0_attn_w_up_v': 8.0,
     'L0_attn_w_out': 8.0,
     'L0_ffn_W1': 8.0,
     'L0_ffn_W2': 8.0,
     'L0_ffn_W3': 8.0,
     'L1_attn_W_qr': 24.896,
     'L1_attn_raw_delta': 64.0,
     'L1_attn_W_uk': 6.783,
     'L1_attn_W_dq': 5.874,
     'L1_attn_W_uq': 6.84,
     'L1_attn_W_kr': 8.0,
     'L1_attn_idx_wq': 8.0,
     'L1_attn_idx_wk': 8.0,
     'L1_ffn_sw1': 3.372,
     'L1_ffn_sw3': 3.124,
     'L1_ffn_sw2': 2.803,
     'L1_ffn_w1': 4.884,
     'L1_ffn_w2': 3.793}
    for name, (base, spread) in spreads.items():
        noise = np.random.default_rng([zlib.crc32(name.encode()), seed]).standard_normal(out[name].shape)
        drawn = base * np.exp(spread * noise) if base else spread * noise
        out[name] = jnp.asarray(drawn.astype(out[name].dtype))
    for name, factor in factors.items():
        out[name] = (out[name] * factor).astype(out[name].dtype)
    return out
```

```python
from contextlib import ExitStack

import numpy as np

import concourse.bass as bass
from concourse import mybir

F32 = mybir.dt.float32
F16 = mybir.dt.float16
U32 = mybir.dt.uint32
ALU = mybir.AluOpType
ACT = mybir.ActivationFunctionType
AX = mybir.AxisListType

P = 128
T = 2048
NT = T // P
D = 128
CH = 512
NCH = T // CH
LN_EPS = 1e-5

H0 = 16
DH0 = 64
LAT0 = 64
E0 = 16
TOPK0 = 4
GROUPS0 = 4
TOPG0 = 2
ROUTE_SCALE = 2.5
H1 = 8
DH1 = 64
CKV = 32
CQ = 64
ROPE1 = 32
HALF1 = ROPE1 // 2
NIDX = 4
KTS = 96
LW = 64
FAR = KTS - LW
SCALE1 = float((DH1 + ROPE1) ** -0.5)
E1 = 8
HS = 256
HR = 128


class Order:

    def __init__(self, eng, sem):
        self.eng, self.sem, self.n = eng, sem, 0

    def mark(self, ins):
        ins.then_inc(self.sem, 1)
        self.n += 1

    def wait(self):
        self.eng.wait_ge(self.sem, self.n)

    def link(self, ins):
        self.mark(ins)
        self.wait()


def layer_norm(dve, own, src, dst, work, var_ready, std_ready, k):
    stats, mv, var, std, rec, t, rstd = work
    for i in range(NT):
        own.mark(dve.bn_stats(stats[:, i, :], src[:, i, :]))
    own.wait()
    for i in range(NT):
        own.mark(dve.bn_aggr(mv[:, i, :], stats[:, i, :]))
    own.wait()
    dve.tensor_scalar(var[:], mv[:, :, 1], LN_EPS, None, ALU.add).then_inc(var_ready, 1)
    dve.wait_ge(std_ready, k + 1)
    own.link(dve.reciprocal(rec[:], std[:]))
    own.link(dve.tensor_tensor(t[:], rec[:], rec[:], ALU.mult))
    own.link(dve.tensor_tensor(t[:], t[:], var[:], ALU.mult))
    own.link(dve.tensor_scalar(t[:], t[:], -0.5, 1.5, ALU.mult, ALU.add))
    own.link(dve.tensor_tensor(rstd[:], rec[:], t[:], ALU.mult))
    for i in range(NT):
        own.mark(dve.tensor_scalar(dst[:, i, :], src[:, i, :], mv[:, i, 0:1], rstd[:, i:i + 1],
                                   ALU.subtract, ALU.mult))
    own.wait()


def norm_work(sb, tag):
    return (sb(f"stats{tag}", [P, NT, 6], F32), sb(f"mv{tag}", [P, NT, 2], F32),
            *(sb(f"{n}{tag}", [P, NT], F32) for n in ("var", "std", "rec", "newton", "rstd")))


def allocators(nc, ctx):
    return (lambda n, s, d: ctx.enter_context(nc.sbuf_tensor(n, s, d)),
            lambda n, s, d: ctx.enter_context(nc.psum_tensor(n, s, d)),
            lambda n: ctx.enter_context(nc.semaphore(n)))


def latents(nc, dram, x, ident, keep):
    with ExitStack() as ctx:
        sb, ps, sem = allocators(nc, ctx)
        xa = sb("xa", [P, NT, D], F32)
        xh = sb("xh", [P, NT, D], F32)
        hT = sb("hT", [P, T], F32)
        scale = sb("ln_scale", [P, 1], F32)
        bias = sb("ln_bias", [P, 1], F32)
        wdq = sb("wdq", [P, P], F32)
        wdkv = sb("wdkv", [P, P], F32)
        stage = [sb(f"w_stage{i}", [P, H0 * P], F32) for i in range(2)]
        work = norm_work(sb, "0")
        bank = [ps(f"lat_bank{i}", [P, CH], F32) for i in range(2)]
        x_in, small_in = sem("x_in"), sem("small_in")
        w_in = [sem(f"w_in{i}") for i in range(2)]
        w_split, rope_in = sem("w_split"), keep["rope_in"]
        var0, std0, own_sem = sem("var0"), sem("std0"), sem("dve_own0")
        xh_ready, hT_bank, hT_ready, lat_bank, lat_ready = (
            sem(n) for n in ("xh_ready", "hT_bank", "hT_ready", "lat_bank_full", "lat_ready"))
        weights = ["wq", "wq_sw", "wk", "wk_sw"]

        with nc.Block() as block:
            @block.sync
            def _(sp):
                sp.dma_start(x[:], dram["x"].rearrange("(t p) d -> p t d", p=P)).then_inc(x_in, 16)
                for dst, src in ((ident, "ident"), (scale, "ln_scale"), (bias, "ln_bias"), (wdq, "wdq"),
                                 (wdkv, "wdkv")):
                    sp.dma_start(dst[:], dram[src]).then_inc(small_in, 16)
                for i, w in enumerate(weights):
                    if i >= 2:
                        sp.wait_ge(w_split, i - 1)
                    sp.dma_start(stage[i % 2][:], dram[w]).then_inc(w_in[i % 2], 16)
                sp.dma_start(keep["cos"][:], dram["cos0"]).then_inc(rope_in, 16)
                sp.dma_start(keep["sin"][:], dram["sin0"]).then_inc(rope_in, 16)

            @block.scalar
            def _(act):
                for k in range(2):
                    act.wait_ge(var0, k + 1)
                    act.activation(work[3][:], work[2][:], ACT.Sqrt).then_inc(std0, 1)

            @block.vector
            def _(dve):
                own = Order(dve, own_sem)
                dve.wait_ge(x_in, 16)
                layer_norm(dve, own, x, xa, work, var0, std0, 0)
                layer_norm(dve, own, xa, xh, work, var0, std0, 1)
                own.mark(dve.tensor_tensor(x[:], x[:], xa[:], ALU.add))
                dve.wait_ge(own_sem, own.n)
                dve.memset(keep["yT"][:], 0.0).then_inc(xh_ready, 1)
                dve.wait_ge(small_in, 5 * 16)
                for c in range(NCH):
                    dve.wait_ge(hT_bank, c + 1)
                    dve.tensor_scalar(hT[:, c * CH:(c + 1) * CH], bank[c % 2][:], scale[:], bias[:], ALU.mult,
                                      ALU.add).then_inc(hT_ready, 1)
                for i in range(2 * NCH):
                    c, kv = i % NCH, i // NCH
                    hi, lo = (keep["ck1"], keep["ck2"]) if kv else (keep["cq1"], keep["cq2"])
                    cols = slice(c * CH, (c + 1) * CH)
                    dve.wait_ge(lat_bank, i + 1)
                    if kv:
                        own.mark(dve.tensor_copy(keep["ckv"][:, cols], bank[i % 2][0:LAT0, :]))
                    own.link(dve.tensor_copy(hi[:, cols], bank[i % 2][:]))
                    dve.tensor_tensor(lo[:, cols], bank[i % 2][:], hi[:, cols], ALU.subtract).then_inc(lat_ready, 1)
                for m in range(2):
                    dve.memset(keep["k_b"][m][LAT0:LAT0 + 2, :], 1.0)
                    dve.memset(keep["v"][m][:, :, DH0:DH0 + 1], 1.0)
                dve.memset(keep["ones_row"][DH0:DH0 + 1, :], 1.0)

            @block.gpsimd
            def _(pool):
                own = 0
                for i, w in enumerate(weights):
                    pool.wait_ge(w_in[i % 2], 16 * (i // 2 + 1))
                    if i:
                        pool.wait_ge(w_split, i)
                    pool.tensor_copy(keep[w][:], stage[i % 2][:]).then_inc(keep["pool_own"], 1)
                    own += 1
                    pool.wait_ge(keep["pool_own"], own)
                    pool.tensor_tensor(keep[w][LAT0:P, :], stage[i % 2][LAT0:P, :], keep[w][LAT0:P, :],
                                       ALU.subtract).then_inc(w_split, 1)

            @block.tensor
            def _(pe):
                pe.wait_ge(small_in, 5 * 16)
                pe.wait_ge(xh_ready, 1)
                for c in range(NCH):
                    if c >= 2:
                        pe.wait_ge(hT_ready, c - 1)
                    for j in range(4):
                        ins = pe.transpose(bank[c % 2][:, j * P:(j + 1) * P], xh[:, 4 * c + j, :], ident[:])
                    ins.then_inc(hT_bank, 1)
                pe.wait_ge(hT_ready, NCH)
                for i in range(2 * NCH):
                    c, kv = i % NCH, i // NCH
                    if i >= 2:
                        pe.wait_ge(lat_ready, i - 1)
                    pe.matmul(bank[i % 2][:], (wdkv if kv else wdq)[:], hT[:, c * CH:(c + 1) * CH], start=True,
                              stop=True).then_inc(lat_bank, 1)


KT0 = T // P
QH = T // 2
STEPS = 2 * KT0


def aux_prepare():
    plan = []
    for j in range(2 * NCH):
        plan += [(j, "rope", (j, 0)), (j, "rope", (j, 1))]
    plan += [(2 * NCH + 1 + n // 4, "max", (n // NCH, n % NCH)) for n in range(NT * NCH)]
    plan += [(2 * NCH + NT + 1, "v", 0), (2 * NCH + NT + 2, "v", 1)]
    plan += [(2 * NCH + NT + 3, "shift", 0), (2 * NCH + NT + 3, "shift", 1)]
    return plan


def aux_finish(half, step):
    step += 4
    return [(step, "bcast", (half, 0)), (step, "bcast", (half, 1)), (step + 2, "out", (half, 0)),
            (step + 2, "out", (half, 1))]


def aux_plan(first, last):
    plan = ([] if first else aux_finish(1, 1)) + aux_finish(0, KT0 + 1) + ([] if last else aux_prepare())
    return sorted(plan, key=lambda u: u[0])


PRO = len(aux_prepare())
BODY = len(aux_plan(False, False))
FIRST_SHORT = BODY - len(aux_plan(True, False))


def aux_base(h):
    return PRO + h * BODY - (FIRST_SHORT if not (isinstance(h, int) and h == 0) else 0)


def heads(nc, dram, keep):
    with ExitStack() as ctx:
        sb, ps, sem = allocators(nc, ctx)
        qa = [sb(f"q_a{i}", [P, T], F16) for i in range(2)]
        qb = [sb(f"q_b{i}", [LAT0 + 2, T], F16) for i in range(2)]
        ka = [sb(f"k_a{i}", [P, T], F16) for i in range(2)]
        kb = keep["k_b"]
        v, ones_row = keep["v"], keep["ones_row"]
        probs = sb("probs", [P, 4, QH], F32)
        term = [[sb(f"rope_term{i}{j}", [P, CH], F32) for j in range(2)] for i in range(2)]
        roped = [sb(f"roped{i}", [P, CH], F32) for i in range(2)]
        part_max = sb("part_max", [P, NT, NCH], F32)
        row_max = sb("row_max", [P, NT], F32)
        shift16 = sb("shift16", [P, NT], F16)
        shift = sb("shift", [P, 2, NT], F32)
        shift_row = sb("shift_row", [NT, 2, P], F16)
        unnorm = sb("unnorm", [DH0 + 1, QH], F32)
        den_col = sb("den_col", [P, QH // P], F32)
        inv_col = sb("inv_col", [P, QH // P], F32)
        inv_row = sb("inv_row", [DH0 + 1, QH], F32)
        normed = sb("normed", [DH0, QH], F32)
        w_v = [sb(f"w_v{i}", [LAT0, DH0], F32) for i in range(2)]
        w_out = [sb(f"w_out{i}", [DH0, D], F32) for i in range(2)]
        scores = [ps(f"scores{i}", [P, QH], F32) for i in range(2)]
        acc = ps("acc", [P, QH], F32)
        aux = ps("aux", [P, 2, CH], F32)
        (aux_full, aux_free, rope_sum, hi_ready, lo_ready, shift_ready, shift_in, scores_ready, probs_ready,
         probs_used, acc_copied, den_in, inv_ready, inv_in, dve_own) = (
            sem(n) for n in ("aux_full", "aux_free", "rope_sum", "hi_ready", "lo_ready", "shift_ready", "shift_in",
                             "scores_ready", "probs_ready", "probs_used", "acc_copied", "den_in",
                             "inv_ready", "inv_in", "dve_own1"))
        w_in = [sem(f"w_head_in{i}") for i in range(2)]
        ident = keep["ident"]
        prepare = aux_prepare()

        def index(plan, kind, arg):
            return [(k, a) for _, k, a in plan].index((kind, arg))

        def prepared_in(hp):
            if isinstance(hp, int) and hp == 0:
                return 0, prepare
            return aux_base(hp - 1), aux_plan(isinstance(hp, int) and hp == 1, False)

        def every_head(eng, body):
            body(0, 0, True, False)
            body(1, 1, False, False)
            with eng.Fori(1, H0 // 2 - 1) as pair:
                body(pair * 2, 0, False, False)
                body(pair * 2 + 1, 1, False, False)
            body(H0 - 2, 0, False, False)
            body(H0 - 1, 1, False, True)

        with nc.Block() as block:
            @block.sync
            def _(sp):
                def load_weights(h, m):
                    sp.dma_start(w_v[m][:], dram["wv"][bass.ds(h, 1), :, :].rearrange("a c d -> (a c) d")
                                 ).then_inc(w_in[m], 16)
                    sp.dma_start(w_out[m][:], dram["w_out"][bass.ds(h, 1), :, :].rearrange("a d n -> (a d) n")
                                 ).then_inc(w_in[m], 16)

                def send_shift(hp, m):
                    base, plan = prepared_in(hp)
                    sp.wait_ge(aux_free, base + index(plan, "shift", 1) + 1)
                    for i in range(2):
                        sp.dma_start(qb[m][LAT0 + i:LAT0 + i + 1, :].rearrange("a (t p) -> a t p", p=P),
                                     shift_row[:, i, :]).then_inc(shift_in, 16)

                def spread_den(half_index):
                    sp.wait_ge(acc_copied, half_index + 1)
                    sp.dma_start(den_col[:], unnorm[DH0:DH0 + 1, :].rearrange("a (p j) -> a p j", p=P)
                                 ).then_inc(den_in, 16)
                    sp.wait_ge(inv_ready, half_index + 1)
                    sp.dma_start(inv_row[DH0:DH0 + 1, :].rearrange("a (p j) -> a p j", p=P), inv_col[:]
                                 ).then_inc(inv_in, 16)

                load_weights(0, 0)
                send_shift(0, 0)

                def body(h, m, first, last):
                    if not first:
                        spread_den(h * 2 - 1)
                    if not last:
                        if not first:
                            sp.wait_ge(aux_free, aux_base(h) + index(aux_plan(first, last), "out", (1, 1)) + 1)
                        load_weights(h + 1, 1 - m)
                    spread_den(h * 2)
                    if not last:
                        send_shift(h + 1, 1 - m)

                every_head(sp, body)
                spread_den(2 * H0 - 1)

            @block.gpsimd
            def _(pool):
                def prepare_head(hp, m):
                    for j in range(2 * NCH):
                        cols = slice((j % NCH) * CH, (j % NCH + 1) * CH)
                        n = hp * (2 * NCH) + j
                        base, plan = prepared_in(hp)
                        pool.wait_ge(aux_free, base + index(plan, "rope", (j, 1)) + 1)
                        if not (isinstance(n, int) and n < 2):
                            pool.wait_ge(hi_ready, n - 1)
                        if not (isinstance(n, int) and n < 1):
                            pool.wait_ge(lo_ready, n)
                        pool.tensor_tensor(roped[j % 2][:], term[j % 2][0][:], term[j % 2][1][:],
                                           ALU.add).then_inc(rope_sum, 1)
                        pool.wait_ge(hi_ready, n + 1)
                        if j < NCH:
                            pool.tensor_tensor(qb[m][0:LAT0, cols], roped[j % 2][0:LAT0, :], qa[m][0:LAT0, cols],
                                               ALU.subtract).then_inc(lo_ready, 1)
                        else:
                            pool.tensor_tensor(ka[m][LAT0:P, cols], roped[j % 2][LAT0:P, :], ka[m][LAT0:P, cols],
                                               ALU.subtract).then_inc(lo_ready, 1)

                prepare_head(0, 0)

                def body(h, m, first, last):
                    if not last:
                        prepare_head(h + 1, 1 - m)

                every_head(pool, body)

            @block.scalar
            def _(act):
                def high_halves(hp, m, j):
                    n = hp * (2 * NCH) + j
                    cols = slice((j % NCH) * CH, (j % NCH + 1) * CH)
                    act.wait_ge(rope_sum, n + 1)
                    if j < NCH:
                        act.activation(qa[m][:, cols], roped[j % 2][:], ACT.Copy).then_inc(hi_ready, 1)
                    else:
                        act.activation(kb[m][0:LAT0, cols], roped[j % 2][0:LAT0, :], ACT.Copy)
                        act.activation(ka[m][:, cols], roped[j % 2][:], ACT.Copy).then_inc(hi_ready, 1)

                def copy_acc(half_index, before):
                    act.wait_ge(probs_used, half_index * KT0 + KT0)
                    if before is not None:
                        act.wait_ge(aux_free, before)
                    act.activation(unnorm[:], acc[0:DH0 + 1, :], ACT.Copy).then_inc(acc_copied, 1)

                for j in range(2 * NCH):
                    high_halves(0, 0, j)

                def body(h, m, first, last):
                    for st in range(STEPS):
                        if st == 1 and not first:
                            plan = aux_plan(isinstance(h, int) and h == 1, False)
                            copy_acc(h * 2 - 1, aux_base(h - 1) + index(plan, "bcast", (0, 1)) + 1)
                        if st == KT0 + 1:
                            plan = aux_plan(first, last)
                            copy_acc(h * 2, None if first else aux_base(h) + index(plan, "bcast", (1, 1)) + 1)
                        n = h * STEPS + st
                        act.wait_ge(scores_ready, n + 1)
                        if not (isinstance(n, int) and n < 4):
                            act.wait_ge(probs_used, n - 3)
                        act.activation(probs[:, st % 4, :], scores[st % 2][:], ACT.Exp,
                                       scale=float(DH0) ** -0.5).then_inc(probs_ready, 1)
                        if not last and 2 <= st < 2 + 2 * NCH:
                            high_halves(h + 1, 1 - m, st - 2)

                every_head(act, body)
                copy_acc(2 * H0 - 1, aux_base(H0 - 1) + index(aux_plan(False, True), "bcast", (0, 1)) + 1)

            @block.vector
            def _(dve):
                def empty(u, kind, arg, hp, m, h):
                    bank = aux[:, arg[-1] % 2 if isinstance(arg, tuple) else arg, :]
                    dve.wait_ge(aux_full, u + 1)
                    if kind == "rope":
                        j, part = arg
                        cols = slice((j % NCH) * CH, (j % NCH + 1) * CH)
                        if not (isinstance(hp, int) and hp == 0 and j < 2):
                            dve.wait_ge(rope_sum, hp * (2 * NCH) + j - 1)
                        table = keep["sin"] if part else keep["cos"]
                        dve.tensor_tensor(term[j % 2][part][:], bank, table[:, cols], ALU.mult).then_inc(aux_free, 1)
                    elif kind == "v":
                        dve.tensor_copy(v[m][:, 8 * arg:8 * arg + 8, 0:DH0],
                                        bank.rearrange("p (t d) -> p t d", d=DH0)).then_inc(aux_free, 1)
                    elif kind == "max":
                        t, c = arg
                        dve.tensor_reduce(part_max[:, t, c:c + 1], bank, AX.X, ALU.max).then_inc(aux_free, 1)
                    elif kind == "shift":
                        if not (isinstance(hp, int) and hp == 0):
                            dve.wait_ge(shift_in, hp * 32)
                        dve.tensor_copy(shift_row[:, arg, :], bank[0:NT, 0:P]).then_inc(aux_free, 1)
                    elif kind == "bcast":
                        half, c = arg
                        cols = slice(c * CH, (c + 1) * CH)
                        dve.wait_ge(acc_copied, h * 2 + half + 1)
                        dve.tensor_tensor(normed[:, cols], unnorm[0:DH0, cols], bank[0:DH0, :],
                                          ALU.mult).then_inc(aux_free, 1)
                    elif kind == "out":
                        half, c = arg
                        q0 = half * QH + c * CH
                        dve.tensor_tensor(keep["yT"][:, q0:q0 + CH], keep["yT"][:, q0:q0 + CH], bank,
                                          ALU.add).then_inc(aux_free, 1)

                def row_maxima(base, plan, hp):
                    dve.wait_ge(aux_free, base + index(plan, "max", (NT - 1, NCH - 1)) + 1)
                    step = hp * 3
                    dve.tensor_reduce(row_max[:], part_max[:], AX.X, ALU.max).then_inc(dve_own, 1)
                    dve.wait_ge(dve_own, step + 1)
                    dve.tensor_scalar(shift16[:], row_max[:], -1.0, None, ALU.mult).then_inc(dve_own, 1)
                    dve.wait_ge(dve_own, step + 2)
                    dve.tensor_copy(shift[:, 0, :], shift16[:]).then_inc(dve_own, 1)
                    dve.wait_ge(dve_own, step + 3)
                    dve.scalar_tensor_tensor(shift[:, 1, :], row_max[:], -1.0, shift[:, 0, :], ALU.mult,
                                             ALU.subtract).then_inc(shift_ready, 1)

                dve.wait_ge(keep["rope_in"], 2 * 16)
                for u, (_, kind, arg) in enumerate(prepare):
                    if kind == "shift" and arg == 0:
                        row_maxima(0, prepare, 0)
                    empty(u, kind, arg, 0, 0, None)

                def body(h, m, first, last):
                    plan = aux_plan(first, last)
                    base = aux_base(h)
                    done = [first, False]
                    for u, (at, kind, arg) in enumerate(plan):
                        for i, half_index in enumerate((h * 2 - 1, h * 2)):
                            if at >= 3 + i * KT0 and not done[i]:
                                invert(half_index)
                                done[i] = True
                        if kind == "shift" and arg == 0:
                            row_maxima(base, plan, h + 1)
                        hh = h - 1 if kind in ("bcast", "out") and arg[0] == 1 else h
                        empty(base + u, kind, arg, h + 1, 1 - m, hh)

                def invert(half_index):
                    dve.wait_ge(den_in, half_index * 16 + 16)
                    if not (isinstance(half_index, int) and half_index == 0):
                        dve.wait_ge(inv_in, half_index * 16)
                    dve.reciprocal(inv_col[:], den_col[:]).then_inc(inv_ready, 1)

                every_head(dve, body)
                invert(2 * H0 - 1)
                base = aux_base(H0 - 1) + len(aux_plan(False, True))
                for u, (_, kind, arg) in enumerate(aux_finish(1, 0)):
                    empty(base + u, kind, arg, None, None, H0 - 1)

            @block.tensor
            def _(pe):
                def fill(u, kind, arg, hp, m, h, mh):
                    slot = arg[-1] % 2 if isinstance(arg, tuple) else arg
                    bank = aux[:, slot, :]
                    if not (isinstance(u, int) and u < 2):
                        pe.wait_ge(aux_free, u - 1)
                    if kind == "rope":
                        j, part = arg
                        q = j < NCH
                        w = keep[("wq", "wq_sw", "wk", "wk_sw")[2 * (not q) + part]]
                        hi, lo = (keep["cq1"], keep["cq2"]) if q else (keep["ck1"], keep["ck2"])
                        cols = slice((j % NCH) * CH, (j % NCH + 1) * CH)
                        w = w[:, bass.ds(hp * P, P)]
                        pe.matmul(bank, w, hi[:, cols], start=True, stop=False)
                        ins = pe.matmul(bank, w, lo[:, cols], start=False, stop=True)
                    elif kind == "v":
                        pe.wait_ge(w_in[m], (hp - m) * 16 + 32)
                        for t in range(8):
                            tok = (8 * arg + t) * P
                            ins = pe.matmul(bank[:, t * DH0:(t + 1) * DH0], keep["ckv"][:, tok:tok + P],
                                            w_v[m][:], start=True, stop=True)
                    elif kind == "max":
                        t, c = arg
                        if t == 0 and c == 0:
                            pe.wait_ge(hi_ready, (hp + 1) * (2 * NCH))
                        ins = pe.matmul(bank, qa[m][0:LAT0, t * P:(t + 1) * P], ka[m][0:LAT0, c * CH:(c + 1) * CH],
                                        start=True, stop=True)
                    elif kind == "shift":
                        pe.wait_ge(shift_ready, hp + 1)
                        ins = pe.transpose(bank[0:NT, 0:P], shift[:, arg, :], ident[:])
                    elif kind == "bcast":
                        half, c = arg
                        pe.wait_ge(inv_in, (h * 2 + half) * 16 + 16)
                        ins = pe.matmul(bank[0:DH0, :], ones_row[DH0:DH0 + 1, :],
                                        inv_row[DH0:DH0 + 1, c * CH:(c + 1) * CH], start=True, stop=True)
                    elif kind == "out":
                        half, c = arg
                        pe.wait_ge(aux_free, u - 1)
                        pe.wait_ge(w_in[mh], (h - mh) * 16 + 32)
                        ins = pe.matmul(bank, w_out[mh][:], normed[:, c * CH:(c + 1) * CH], start=True, stop=True)
                    ins.then_inc(aux_full, 1)

                def score(h, m, st):
                    half, kt = st // KT0, st % KT0
                    n = h * STEPS + st
                    if st == 0:
                        pe.wait_ge(lo_ready, (h + 1) * (2 * NCH))
                        pe.wait_ge(shift_in, (h + 1) * 32)
                    if not (isinstance(n, int) and n < 2):
                        pe.wait_ge(probs_ready, n - 1)
                    for c in range(2):
                        q0 = half * QH + c * CH
                        out = scores[st % 2][:, c * CH:(c + 1) * CH]
                        pe.matmul(out, ka[m][:, kt * P:(kt + 1) * P], qa[m][:, q0:q0 + CH], start=True, stop=False)
                        ins = pe.matmul(out, kb[m][:, kt * P:(kt + 1) * P], qb[m][:, q0:q0 + CH], start=False,
                                        stop=True)
                    ins.then_inc(scores_ready, 1)

                def weigh(h, m, st, v_base, half_index):
                    kt = st % KT0
                    n = h * STEPS + st
                    if st == 0:
                        pe.wait_ge(aux_free, v_base)
                    if kt == 0 and not (isinstance(half_index, int) and half_index == 0):
                        pe.wait_ge(acc_copied, half_index)
                    pe.wait_ge(probs_ready, n + 1)
                    for c in range(2):
                        cols = slice(c * CH, (c + 1) * CH)
                        ins = pe.matmul(acc[0:DH0 + 1, cols], v[m][:, kt, :], probs[:, st % 4, cols],
                                        start=(kt == 0), stop=(kt == KT0 - 1))
                    ins.then_inc(probs_used, 1)

                for u, (_, kind, arg) in enumerate(prepare):
                    fill(u, kind, arg, 0, 0, None, None)

                def body(h, m, first, last):
                    plan = aux_plan(first, last)
                    base = aux_base(h)
                    v_base, before = prepared_in(h)
                    v_base += index(before, "v", 1) + 1
                    for st in range(STEPS):
                        score(h, m, st)
                        if st == 0 and not first:
                            weigh(h - 1, 1 - m, STEPS - 1, None, h * 2 - 1)
                        elif st:
                            weigh(h, m, st - 1, v_base, h * 2 + (st - 1) // KT0)
                        for u, (at, kind, arg) in enumerate(plan):
                            if at == st:
                                old = kind in ("bcast", "out") and arg[0] == 1
                                fill(base + u, kind, arg, h + 1, 1 - m, h - 1 if old else h, 1 - m if old else m)

                every_head(pe, body)
                weigh(H0 - 1, 1, STEPS - 1, None, 2 * H0 - 1)
                base = aux_base(H0 - 1) + len(aux_plan(False, True))
                for u, (_, kind, arg) in enumerate(aux_finish(1, 0)):
                    fill(base + u, kind, arg, None, None, H0 - 1, 1)


def layer0_attention(nc, dram, x, ident, yT):
    with ExitStack() as ctx:
        sb, _, sem = allocators(nc, ctx)
        keep = {"ident": ident, "yT": yT}
        for n in ("cos", "sin"):
            keep[n] = sb(n, [P, T], F32)
        for n in ("wq", "wq_sw", "wk", "wk_sw"):
            keep[n] = sb(n, [P, H0 * P], F16)
        for n in ("cq1", "cq2", "ck1", "ck2"):
            keep[n] = sb(n, [P, T], F16)
        keep["ckv"] = sb("ckv", [LAT0, T], F32)
        keep["ones_row"] = sb("ones_row", [DH0 + 1, DH0], F32)
        keep["k_b"] = [sb(f"k_b{i}", [LAT0 + 2, T], F16) for i in range(2)]
        keep["v"] = [sb(f"v{i}", [P, KT0, DH0 + 1], F32) for i in range(2)]
        for n in ("rope_in", "pool_own"):
            keep[n] = sem(n)
        latents(nc, dram, x, ident, keep)
        heads(nc, dram, keep)


def add_transposed(dve, pe, x, yT, ident, bank, turned, added):
    def turn():
        for c in range(NCH):
            if c >= 2:
                pe.wait_ge(added, c - 1)
            for j in range(4):
                t = 4 * c + j
                ins = pe.transpose(bank[c % 2][:, j * P:(j + 1) * P], yT[:, t * P:(t + 1) * P], ident[:])
            ins.then_inc(turned, 1)

    def add():
        for c in range(NCH):
            dve.wait_ge(turned, c + 1)
            rows = x[:, 4 * c:4 * c + 4, :].rearrange("p t d -> p (t d)")
            dve.tensor_tensor(rows, rows, bank[c % 2][:], ALU.add).then_inc(added, 1)

    return turn if dve is None else add


def layer0_experts(nc, dram, x, ident, yT):
    with ExitStack() as ctx:
        sb, ps, sem = allocators(nc, ctx)
        xn = sb("e0_xn", [P, NT, D], F32)
        xnT = sb("e0_xnT", [P, T], F32)
        wg = sb("wg", [P, E0], F32)
        b2 = sb("e0_b2", [E0, D], F32)
        iota = sb("iota", [P, E0], F32)
        s = sb("gate_s", [P, NT, E0], F32)
        best_of = sb("best_of_group", [P, NT, 8], F32)
        top = sb("gate_top", [P, NT, 8], F32)
        at = sb("gate_at", [P, NT, 8], U32)
        atf = sb("gate_atf", [P, NT, 8], F32)
        gmask = sb("group_mask", [P, NT, GROUPS0], F32)
        hit = sb("gate_hit", [P, NT, E0], F32)
        chosen = sb("gate_chosen", [P, NT, E0], F32)
        total = sb("gate_total", [P, NT], F32)
        weT = sb("gate_wT", [E0, T], F32)
        w = [sb(f"e0_w{i}", [P, 3, P], F32) for i in range(2)]
        b13 = [sb(f"e0_b13{i}", [P, 2], F32) for i in range(2)]
        silu = [sb(f"e0_silu{i}", [P, CH], F32) for i in range(2)]
        hid = [sb(f"e0_hid{i}", [P, CH], F32) for i in range(2)]
        work = norm_work(sb, "1")
        bank = [ps(f"e0_bank{i}", [P, CH], F32) for i in range(2)]
        up = [ps(f"e0_up{i}", [P, CH], F32) for i in range(2)]
        gate = [ps(f"e0_gate{i}", [P, CH], F32) for i in range(2)]
        down = [ps(f"e0_down{i}", [P, 4, D], F32) for i in range(2)]
        (small_in, turned, added, var, std, own_sem, normed, xnT_full, xnT_ready, logits, gated, weT_full, weT_ready,
         bias_full, bias_added, chosen_ready, up_full, silu_ready, hid_ready, down_full, down_added) = (
            sem("e0_" + n) for n in (
                "small_in", "turned", "added", "var", "std", "own", "normed", "xnT_full", "xnT_ready", "logits",
                "gated", "weT_full", "weT_ready", "bias_full", "bias_added", "chosen_ready", "up_full", "silu_ready",
                "hid_ready", "down_full", "down_added"))
        w_in = [sem(f"e0_w_in{i}") for i in range(2)]
        SMALL = 3

        with nc.Block() as block:
            @block.sync
            def _(sp):
                for dst, src in ((wg, "wg"), (b2, "e0_b2"), (iota, "iota")):
                    sp.dma_start(dst[:], dram[src]).then_inc(small_in, 16)

                def load(e, m):
                    for j, n in enumerate(("e0_w1", "e0_w3", "e0_w2")):
                        sp.dma_start(w[m][:, j, :], dram[n][bass.ds(e, 1), :, :].rearrange("a d i -> (a d) i")
                                     ).then_inc(w_in[m], 16)
                    sp.dma_start(b13[m][:], dram["e0_b13"][bass.ds(e, 1), :, :].rearrange("a i j -> (a i) j")
                                 ).then_inc(w_in[m], 16)

                load(0, 0)
                load(1, 1)
                with sp.Fori(1, E0 // 2) as pair:
                    for m in range(2):
                        e = pair * 2 + m
                        sp.wait_ge(down_full, (e - 1) * NCH)
                        load(e, m)

            @block.scalar
            def _(act):
                act.wait_ge(var, 1)
                act.activation(work[3][:], work[2][:], ACT.Sqrt).then_inc(std, 1)
                act.wait_ge(logits, 1)
                act.activation(s[:].rearrange("p t e -> p (t e)"), bank[0][:, 0:NT * E0], ACT.Sigmoid
                               ).then_inc(gated, 1)

                def expert(e, m):
                    act.wait_ge(w_in[m], (e - m) * 32 + 64)
                    for c in range(NCH):
                        n = e * NCH + c
                        act.wait_ge(up_full, n + 1)
                        if not (isinstance(n, int) and n < 2):
                            act.wait_ge(hid_ready, n - 1)
                        act.activation(silu[c % 2][:], up[c % 2][:], ACT.Silu, bias=b13[m][:, 0:1]
                                       ).then_inc(silu_ready, 1)

                expert(0, 0)
                expert(1, 1)
                with act.Fori(1, E0 // 2) as pair:
                    expert(pair * 2, 0)
                    expert(pair * 2 + 1, 1)

            @block.vector
            def _(dve):
                own = Order(dve, own_sem)
                add_transposed(dve, None, x, yT, ident, bank, turned, added)()
                dve.wait_ge(added, NCH)
                layer_norm(dve, own, x, xn, work, var, std, 0)
                dve.memset(best_of[:], -1.0).then_inc(normed, 1)
                for c in range(NCH):
                    dve.wait_ge(xnT_full, c + 1)
                    dve.tensor_copy(xnT[:, c * CH:(c + 1) * CH], bank[c % 2][:]).then_inc(xnT_ready, 1)

                def top8(values):
                    for t in range(NT):
                        own.mark(dve.max(top[:, t, :], values[:, t, :]))
                    own.wait()
                    for t in range(NT):
                        own.mark(dve.max_index(at[:, t, :], top[:, t, :], values[:, t, :]))
                    own.wait()
                    own.link(dve.tensor_copy(atf[:], at[:]))

                def mark(mask, n, count):
                    places = iota[:, 0:n].unsqueeze(1).broadcast_to([P, NT, n])
                    for k in range(count):
                        own.link(dve.tensor_tensor(hit[:, :, 0:n] if k else mask, places,
                                                   atf[:, :, k:k + 1].broadcast_to([P, NT, n]), ALU.is_equal))
                        if k:
                            own.link(dve.tensor_tensor(mask, mask, hit[:, :, 0:n], ALU.add))

                dve.wait_ge(small_in, SMALL * 16)
                dve.wait_ge(gated, 1)
                dve.wait_ge(normed, 1)
                own.link(dve.tensor_reduce(best_of[:, :, 0:GROUPS0],
                                           s[:].rearrange("p t (g k) -> p t g k", g=GROUPS0), AX.X, ALU.max))
                top8(best_of)
                mark(gmask[:], GROUPS0, TOPG0)
                per_expert = gmask[:].unsqueeze(3).broadcast_to([P, NT, GROUPS0, E0 // GROUPS0])
                own.link(dve.tensor_tensor(hit[:].rearrange("p t (g k) -> p t g k", g=GROUPS0),
                                           s[:].rearrange("p t (g k) -> p t g k", g=GROUPS0), per_expert, ALU.mult))
                own.link(dve.tensor_scalar(gmask[:], gmask[:], -1.0, None, ALU.add))
                own.link(dve.tensor_tensor(chosen[:].rearrange("p t (g k) -> p t g k", g=GROUPS0),
                                           hit[:].rearrange("p t (g k) -> p t g k", g=GROUPS0), per_expert, ALU.add))
                top8(chosen)
                mark(chosen[:], E0, TOPK0)
                own.link(dve.tensor_tensor(s[:], s[:], chosen[:], ALU.mult))
                own.link(dve.tensor_reduce(total[:], s[:], AX.X, ALU.add))
                own.link(dve.reciprocal(total[:], total[:]))
                own.link(dve.tensor_tensor(s[:], s[:], total[:].unsqueeze(2).broadcast_to([P, NT, E0]), ALU.mult))
                dve.tensor_scalar(s[:], s[:], ROUTE_SCALE, None, ALU.mult).then_inc(chosen_ready, 1)
                for c in range(NCH):
                    dve.wait_ge(weT_full, c + 1)
                    dve.tensor_copy(weT[:, c * CH:(c + 1) * CH], bank[c % 2][0:E0, :]).then_inc(weT_ready, 1)
                for c in range(NCH):
                    dve.wait_ge(bias_full, c + 1)
                    rows = x[:, 4 * c:4 * c + 4, :].rearrange("p t d -> p (t d)")
                    dve.tensor_tensor(rows, rows, bank[c % 2][:], ALU.add).then_inc(bias_added, 1)
                dve.wait_ge(bias_added, NCH)

                def add_down(n, c, e):
                    dve.wait_ge(down_full, n + 1)
                    if not (isinstance(n, int) and n < NCH):
                        dve.wait_ge(down_added, n - NCH + 1)
                    for j in range(4):
                        t = 4 * c + j
                        ins = dve.scalar_tensor_tensor(x[:, t, :], down[c % 2][:, j, :], s[:, t, bass.ds(e, 1)],
                                                       x[:, t, :], ALU.mult, ALU.add)
                    ins.then_inc(down_added, 1)

                def expert(e, m, first):
                    dve.wait_ge(w_in[m], (e - m) * 32 + 64)
                    for c in range(NCH):
                        n = e * NCH + c
                        dve.wait_ge(silu_ready, n + 1)
                        if not (isinstance(n, int) and n < 2):
                            dve.wait_ge(down_full, n - 1)
                        dve.scalar_tensor_tensor(hid[c % 2][:], gate[c % 2][:], b13[m][:, 1:2], silu[c % 2][:],
                                                 ALU.add, ALU.mult).then_inc(hid_ready, 1)
                        if c:
                            add_down(n - 1, c - 1, e)
                        elif not first:
                            add_down(n - 1, NCH - 1, e - 1)

                expert(0, 0, True)
                expert(1, 1, False)
                with dve.Fori(1, E0 // 2) as pair:
                    expert(pair * 2, 0, False)
                    expert(pair * 2 + 1, 1, False)
                add_down(E0 * NCH - 1, NCH - 1, E0 - 1)

            @block.tensor
            def _(pe):
                add_transposed(None, pe, x, yT, ident, bank, turned, added)()
                pe.wait_ge(normed, 1)
                for c in range(NCH):
                    if c >= 2:
                        pe.wait_ge(xnT_ready, c - 1)
                    for j in range(4):
                        ins = pe.transpose(bank[c % 2][:, j * P:(j + 1) * P], xn[:, 4 * c + j, :], ident[:])
                    ins.then_inc(xnT_full, 1)
                pe.wait_ge(xnT_ready, NCH)
                pe.wait_ge(small_in, SMALL * 16)
                for t in range(NT):
                    ins = pe.matmul(bank[0][:, t * E0:(t + 1) * E0], xnT[:, t * P:(t + 1) * P], wg[:], start=True,
                                    stop=True)
                ins.then_inc(logits, 1)
                pe.wait_ge(chosen_ready, 1)
                for c in range(NCH):
                    if c >= 2:
                        pe.wait_ge(weT_ready, c - 1)
                    for j in range(4):
                        ins = pe.transpose(bank[c % 2][0:E0, j * P:(j + 1) * P], s[:, 4 * c + j, :], ident[:])
                    ins.then_inc(weT_full, 1)
                pe.wait_ge(weT_ready, NCH)
                for c in range(NCH):
                    if c >= 2:
                        pe.wait_ge(bias_added, c - 1)
                    for j in range(4):
                        ins = pe.matmul(bank[c % 2][:, j * P:(j + 1) * P], weT[:, (4 * c + j) * P:(4 * c + j + 1) * P],
                                        b2[:], start=True, stop=True)
                    ins.then_inc(bias_full, 1)

                def put_down(n, c, m):
                    pe.wait_ge(hid_ready, n + 1)
                    if not (isinstance(n, int) and n < 2):
                        pe.wait_ge(down_added, n - 1)
                    for j in range(4):
                        ins = pe.matmul(down[c % 2][:, j, :], hid[c % 2][:, j * P:(j + 1) * P], w[m][:, 2, :],
                                        start=True, stop=True)
                    ins.then_inc(down_full, 1)

                def expert(e, m, first):
                    pe.wait_ge(w_in[m], (e - m) * 32 + 64)
                    for c in range(NCH):
                        n = e * NCH + c
                        cols = slice(c * CH, (c + 1) * CH)
                        if not (isinstance(n, int) and n < 2):
                            pe.wait_ge(hid_ready, n - 1)
                        pe.matmul(up[c % 2][:], w[m][:, 0, :], xnT[:, cols], start=True, stop=True)
                        pe.matmul(gate[c % 2][:], w[m][:, 1, :], xnT[:, cols], start=True, stop=True
                                  ).then_inc(up_full, 1)
                        if c:
                            put_down(n - 1, c - 1, m)
                        elif not first:
                            put_down(n - 1, NCH - 1, 1 - m)

                expert(0, 0, True)
                expert(1, 1, False)
                with pe.Fori(1, E0 // 2) as pair:
                    expert(pair * 2, 0, False)
                    expert(pair * 2 + 1, 1, False)
                put_down(E0 * NCH - 1, NCH - 1, 1)


KW = CKV + ROPE1
QW = 2 * ROPE1 + CKV
NQ = H1 * ROPE1
GROUP = 16
NG = P // GROUP
WIN = 2 * P
SC = WIN + P
FILL = 1e25


def index_width(t):
    return KTS if t == 0 else t * P + P - LW


def rotate(dve, own, dst, mu, cos, sin, turned, swapped):
    own.mark(dve.tensor_tensor(turned, mu, cos, ALU.mult))
    lo, hi = slice(0, HALF1), slice(HALF1, ROPE1)
    last = lambda ap, cols: ap[(slice(None),) * (ap.ndim - 1) + (cols,)]
    own.mark(dve.tensor_tensor(last(swapped, lo), last(mu, hi), last(sin, lo), ALU.mult))
    own.mark(dve.tensor_tensor(last(swapped, hi), last(mu, lo), last(sin, hi), ALU.mult))
    own.wait()
    return dve.tensor_tensor(dst, turned, swapped, ALU.add)


def projections1(nc, dram, x, ident, yT, keep):
    with ExitStack() as ctx:
        sb, ps, sem = allocators(nc, ctx)
        xnT = sb("a1_xnT", [P, T], F32)
        wkvr = sb("wkvr", [P, KW], F32)
        wdq = sb("a1_wdq", [P, CQ], F32)
        wuq = sb("wuq", [DH1, H1, CQ], F32)
        wuk = sb("wuk", [DH1, H1, CKV], F32)
        wuv = sb("wuv", [DH1, H1, CKV], F32)
        wo = sb("a1_wo", [DH1, H1, D], F32)
        wqq = sb("wqq", [CQ, H1 * CKV + NQ], F32)
        widxq = sb("widxq", [P, NIDX * DH1], F32)
        widxk = sb("widxk", [P, P], F32)
        pre = sb("pre_softplus", [P, NT, NQ + ROPE1], F32)
        e = sb("softplus_e", [P, NT, NQ + ROPE1], F32)
        u = sb("softplus_u", [P, NT, NQ + ROPE1], F32)
        angle = {n: sb(n, [P, NT, ROPE1], F32) for n in ("cos_k", "sin_k", "cos_near", "sin_near", "cos_q", "sin_q")}
        xn = u[:, :, 0:D]
        cqT = e[:].rearrange("p t c -> p (t c)")[0:CQ, 0:T]
        near_key = xnT[:, 0:NT * KW].rearrange("p (t k) -> p t k", k=KW)
        work = norm_work(sb, "2")
        bank = [ps(f"a1_bank{i}", [P, CH], F32) for i in range(4)]
        (w_in, turned, added, var, std, own_sem, normed, full, free, act_own, abs_ready, e_ready, u_ready, ln_ready,
         near_ready) = (sem("a1_" + n) for n in (
             "w_in", "turned", "added", "var", "std", "own", "normed", "full", "free", "act_own", "abs_ready", "e_ready",
             "u_ready", "ln_ready", "near_ready"))
        rows, QN, near, nout, qiT, kiT = (keep[n] for n in ("rows", "queries", "near_keys", "nout", "qiT", "kiT"))
        loads = [(wkvr, "wkvr"), (wdq, "a1_wdq"), (wuq, "wuq"), (wuk, "wuk"), (wqq[:, H1 * CKV:], "wqr"),
                 (wuv, "wuv"), (wo, "a1_wo"), (widxq, "widxq"), (widxk, "widxk"), (keep["idx_w"], "idx_w"),
                 (keep["cap0"], "cap0"), (keep["cap"], "cap"), (keep["mask"], "mask"), (keep["cos_far"], "cos_far"),
                 (keep["sin_far"], "sin_far"), *((angle[n], n) for n in angle)]

        jobs = [("xnT", c) for c in range(NCH)] + [("kv", i) for i in range(2)] + [("cq", c) for c in range(NCH)]
        jobs += [("wqq", 0)] + [("q", t) for t in range(NT)]
        SOFT = len(jobs)
        jobs += [("ki", c) for c in range(NCH)] + [("qi", i) for i in range(2 * NCH)] + [("nout", i) for i in range(2)]
        SOFT2 = len(jobs)
        jobs += [("near", c) for c in range(NCH)]

        with nc.Block() as block:
            @block.sync
            def _(sp):
                for dst, src in loads:
                    sp.dma_start(dst if isinstance(dst, bass.AP) else dst[:], dram[src]).then_inc(w_in, 16)
                sp.wait_ge(keep["rows_ready"], 1)
                sp.dma_start(keep["table"].rearrange("(t p) d -> p t d", p=P), rows[:]).then_inc(keep["table_out"], 16)
                sp.wait_ge(keep["table_out"], 16)

            @block.scalar
            def _(act):
                act.wait_ge(var, 1)
                act.activation(work[3][:], work[2][:], ACT.Sqrt).then_inc(std, 1)

                def drain(n):
                    kind, i = jobs[n]
                    src = bank[n % 4]
                    copies = {
                        "xnT": lambda: [(xnT[:, i * CH:(i + 1) * CH], src[:])],
                        "kv": lambda: [(rows[:, 8 * i:8 * i + 8, 0:CKV], kv[:, :, 0:CKV]),
                                       (pre[:, 8 * i:8 * i + 8, NQ:], kv[:, :, CKV:])],
                        "cq": lambda: [(cqT[:, i * CH:(i + 1) * CH], src[0:CQ, :])],
                        "wqq": lambda: [(wqq[:, 0:H1 * CKV], src[0:CQ, 0:H1 * CKV])],
                        "q": lambda: [(QN[:, i, :, ROPE1:ROPE1 + CKV],
                                       src[:, 0:H1 * CKV].rearrange("p (h c) -> p h c", h=H1)),
                                      (pre[:, i, 0:NQ], src[:, H1 * CKV:])],
                        "ki": lambda: [(kiT[:, i * CH:(i + 1) * CH], src[:])],
                        "qi": lambda: [(qiT[:, i // NCH, (i % NCH) * CH:(i % NCH + 1) * CH], src[:])],
                        "nout": lambda: [(nout[:, 4 * i:4 * i + 4, :],
                                          src[0:CKV, :].rearrange("c (h n) -> c h n", h=4))],
                        "near": lambda: [(near[:, P + i * CH:P + (i + 1) * CH], src[0:KW, :])],
                    }
                    kv = src[:].rearrange("p (t k) -> p t k", k=KW)
                    act.wait_ge(full, n + 1)
                    for out, in_ in copies[kind]():
                        ins = act.activation(out, in_, ACT.Copy)
                    ins.then_inc(free, 1)

                for n in range(SOFT):
                    drain(n)
                act.wait_ge(free, SOFT)
                act.activation(e[:], pre[:], ACT.Abs).then_inc(abs_ready, 1)
                act.wait_ge(abs_ready, 1)
                act.activation(e[:], e[:], ACT.Exp, scale=-1.0).then_inc(e_ready, 1)
                for n in range(SOFT, SOFT2):
                    drain(n)
                act.wait_ge(u_ready, 1)
                act.activation(u[:], u[:], ACT.Ln).then_inc(ln_ready, 1)
                for n in range(SOFT2, len(jobs)):
                    drain(n)

            @block.vector
            def _(dve):
                own = Order(dve, own_sem)
                dve.memset(near[:, 0:P], 0.0)
                layer_norm(dve, own, x, xn, work, var, std, 0)
                dve.memset(yT[:], 0.0).then_inc(normed, 1)
                dve.wait_ge(e_ready, 1)
                own.link(dve.tensor_scalar(u[:], e[:], 1.0, None, ALU.add))
                dve.scalar_tensor_tensor(e[:], u[:], -1.0, e[:], ALU.add, ALU.subtract).then_inc(u_ready, 1)
                dve.wait_ge(ln_ready, 1)
                own.link(dve.tensor_tensor(u[:], u[:], e[:], ALU.subtract))
                own.link(dve.scalar_tensor_tensor(pre[:], pre[:], 0.0, u[:], ALU.max, ALU.add))
                mu_k = pre[:, :, NQ:]
                dve.tensor_copy(rows[:, :, CKV:], mu_k).then_inc(keep["rows_ready"], 1)
                dve.wait_ge(w_in, len(loads) * 16)
                own.mark(dve.tensor_copy(near_key[:, :, ROPE1:], rows[:, :, 0:CKV]))
                rotate(dve, own, near_key[:, :, 0:ROPE1], mu_k, angle["cos_k"][:], angle["sin_k"][:],
                       e[:, :, NQ:], u[:, :, NQ:]).then_inc(near_ready, 1)
                dve.wait_ge(near_ready, 1)
                mu_q = pre[:, :, 0:NQ].rearrange("p t (h r) -> p t h r", h=H1)
                e_q = e[:, :, 0:NQ].rearrange("p t (h r) -> p t h r", h=H1)
                u_q = u[:, :, 0:NQ].rearrange("p t (h r) -> p t h r", h=H1)
                every = lambda ap: ap[:].unsqueeze(2).broadcast_to([P, NT, H1, ROPE1])
                own.link(rotate(dve, own, QN[:, :, :, 0:ROPE1], mu_q, every(angle["cos_near"]),
                                every(angle["sin_near"]), e_q, u_q))
                own.link(rotate(dve, own, QN[:, :, :, ROPE1 + CKV:], mu_q, every(angle["cos_q"]),
                                every(angle["sin_q"]), e_q, u_q))

            @block.tensor
            def _(pe):
                def fill(n):
                    kind, i = jobs[n]
                    b = bank[n % 4]
                    if n >= 4:
                        pe.wait_ge(free, n - 3)
                    mm = lambda out, lhsT, rhs: pe.matmul(out, lhsT, rhs, start=True, stop=True)
                    cols = slice(i * CH, (i + 1) * CH)
                    if kind == "xnT":
                        for j in range(4):
                            ins = pe.transpose(b[:, j * P:(j + 1) * P], xn[:, 4 * i + j, :], ident[:])
                    elif kind == "kv":
                        for j in range(8):
                            t = 8 * i + j
                            ins = mm(b[:, j * KW:(j + 1) * KW], xnT[:, t * P:(t + 1) * P], wkvr[:])
                    elif kind == "cq":
                        ins = mm(b[0:CQ, :], wdq[:], xnT[:, cols])
                    elif kind == "wqq":
                        for h in range(H1):
                            ins = mm(b[0:CQ, h * CKV:(h + 1) * CKV], wuq[:, h, :], wuk[:, h, :])
                    elif kind == "q":
                        ins = mm(b[:], cqT[:, i * P:(i + 1) * P], wqq[:])
                    elif kind == "ki":
                        ins = mm(b[:], widxk[:], xnT[:, cols])
                    elif kind == "qi":
                        c = i % NCH
                        ins = mm(b[:], widxq[:, (i // NCH) * P:(i // NCH + 1) * P], xnT[:, c * CH:(c + 1) * CH])
                    elif kind == "nout":
                        for h in range(4):
                            ins = mm(b[0:CKV, h * D:(h + 1) * D], wuv[:, 4 * i + h, :], wo[:, 4 * i + h, :])
                    else:
                        for j in range(4):
                            ins = pe.transpose(b[0:KW, j * P:(j + 1) * P], near_key[:, 4 * i + j, :], ident[:])
                    ins.then_inc(full, 1)

                pe.wait_ge(normed, 1)
                for n, (kind, i) in enumerate(jobs):
                    if n == NCH:
                        pe.wait_ge(w_in, len(loads) * 16)
                        pe.wait_ge(free, NCH)
                    if (kind, i) in (("wqq", 0), ("q", 0)):
                        pe.wait_ge(free, n)
                    if (kind, i) == ("near", 0):
                        pe.wait_ge(near_ready, 1)
                    fill(n)


def selected_attention(nc, dram, ident, yT, keep):
    with ExitStack() as ctx:
        sb, ps, sem = allocators(nc, ctx)
        rows, QN, near, nout, qiT, kiT, mask = (
            keep[n] for n in ("rows", "queries", "near_keys", "nout", "qiT", "kiT", "mask"))
        RING = 3
        index = sb("index", [P, T], F32)
        relu = [sb(f"relu{i}", [P, CH], F32) for i in range(2)]
        top = sb("a1_top", [P, 8], F32)
        place = sb("place", [P, FAR], U32)
        placeT = [sb(f"placeT{i}", [P, FAR], U32) for i in range(RING)]
        far = [sb(f"far{i}", [P, 32, KW], F32) for i in range(RING)]
        turned = sb("far_turned", [P, 32, ROPE1], F32)
        swapped = sb("far_swapped", [P, 32, ROPE1], F32)
        qT = sb("qT", [KW, 2, 32, 4, H1], F32)
        farT = sb("farT", [KW, 4, 4, P], F32)
        probs = sb("a1_probs", [P, NG, SC], F32)
        probsT = sb("a1_probsT", [P, 3, NG, P], F32)
        biggest = sb("biggest", [P, NG], F32)
        den = sb("a1_den", [P, NG], F32)
        ctxT = sb("ctxT", [CKV, NG * P], F32)
        score = [ps(f"a1_score{i}", [P, CH], F32) for i in range(2)]
        turn = [ps(f"a1_turn{i}", [P, CH], F32) for i in range(2)]
        idx = [ps(f"a1_idx{i}", [P, CH], F32) for i in range(2)]
        ctxp = ps("a1_ctx", [CKV, NG * P], F32)
        (idx_full, relu_ready, summed, own_sem, place_ready, keys_ready, turn_full, turn_free, score_full, score_free,
         shift_ready, exp_ready, normed, ctx_full, ctx_copied) = (sem("a1_" + n) for n in (
             "idx_full", "relu_ready", "summed", "own2", "place_ready", "keys_ready", "turn_full", "turn_free",
             "score_full", "score_free", "shift_ready", "exp_ready", "normed_p", "ctx_full", "ctx_copied"))
        far_in = [sem(f"far_in{i}") for i in range(RING)]
        LAG = 2

        chunks = [[(c, min(c + CH, index_width(t))) for c in range(0, index_width(t), CH)] for t in range(NT)]
        idx_base = [0]
        for t in range(NT):
            idx_base.append(idx_base[-1] + len(chunks[t]) * NIDX)
        turns = [("q", i) for i in range(4)] + [("far", g) for g in range(NG)]
        turns2 = [("p", i) for i in range(6)] + [("y", 0)]
        TURNS = len(turns) + len(turns2)

        with nc.Block() as block:
            @block.gpsimd
            def _(pool):
                pool.wait_ge(keep["table_out"], 16)
                for t in range(NT):
                    m = t % RING
                    pool.wait_ge(place_ready, t + 1)
                    if t >= RING:
                        pool.wait_ge(ctx_full, t - RING + 1)
                    for i in range(32):
                        pool.indirect_dma_start(far[m][:, i, :], None, keep["table"],
                                                bass.IndirectOffsetOnAxis(ap=placeT[m][:, i:i + 1], axis=0)
                                                ).then_inc(far_in[m], 16)

            @block.scalar
            def _(act):
                def drain(t, k, n):
                    kind, i = (turns + turns2)[k]
                    src = turn[n % 2]
                    act.wait_ge(turn_full, n + 1)
                    if kind == "q":
                        heads = slice(4 * (i % 2), 4 * (i % 2) + 4)
                        ins = act.activation(qT[:, i // 2, :, :, heads].rearrange("k i a h -> k h a i"),
                                             src[0:KW, :].rearrange("k (h a i) -> k h a i", h=4, a=4), ACT.Copy)
                    elif kind == "far":
                        if NG * t + i >= 4:
                            act.wait_ge(score_full, NG * t + i - 3)
                        ins = act.activation(farT[:, i % 4, :, :], src[0:KW, :].rearrange("k (i l) -> k i l", i=4),
                                             ACT.Copy)
                    elif kind == "p":
                        ins = act.activation(probsT[:, i // 2, 4 * (i % 2):4 * (i % 2) + 4, :],
                                             src[:].rearrange("p (g l) -> p g l", g=4), ACT.Copy)
                    else:
                        ins = act.activation(yT[:, t * P:(t + 1) * P].rearrange("d (a i) -> d i a", a=4),
                                             src[:, 0:P].rearrange("d (i a) -> d i a", a=4), ACT.Copy)
                    ins.then_inc(turn_free, 1)

                for n in range(NT + LAG):
                    t = n - LAG
                    if t >= 0:
                        for k in range(len(turns)):
                            drain(t, k, t * TURNS + k)
                        act.wait_ge(shift_ready, t + 1)
                        for g in range(NG):
                            ins = act.activation(probs[:, g, :], probs[:, g, :], ACT.Exp, bias=biggest[:, g:g + 1],
                                                 scale=SCALE1, accum_out=den[:, g:g + 1])
                        ins.then_inc(exp_ready, 1)
                    if n < NT:
                        for j in range(idx_base[n], idx_base[n + 1]):
                            lo, hi = chunks[n][(j - idx_base[n]) // NIDX]
                            act.wait_ge(idx_full, j + 1)
                            if j >= 2:
                                act.wait_ge(summed, j - 1)
                            act.activation(relu[j % 2][:, 0:hi - lo], idx[j % 2][:, 0:hi - lo], ACT.Relu
                                           ).then_inc(relu_ready, 1)
                    if t >= 0:
                        for k in range(len(turns), TURNS - 1):
                            drain(t, k, t * TURNS + k)
                        act.wait_ge(ctx_full, t + 1)
                        act.activation(ctxT[:], ctxp[:], ACT.Copy).then_inc(ctx_copied, 1)
                        drain(t, TURNS - 1, t * TURNS + TURNS - 1)

            @block.vector
            def _(dve):
                own = Order(dve, own_sem)

                def rank(t):
                    w = index_width(t)
                    values = index[:, 0:w]
                    dve.wait_ge(summed, idx_base[t + 1])
                    if t == 0:
                        own.link(dve.tensor_tensor(values, values, keep["cap0"][:], ALU.min))
                    else:
                        own.link(dve.tensor_tensor(index[:, w - P:w], index[:, w - P:w], keep["cap"][:], ALU.min))
                    for r in range(0, FAR, 8):
                        own.link(dve.max(top[:], values))
                        own.link(dve.max_index(place[:, r:r + 8], top[:], values))
                        if r + 8 < FAR:
                            own.link(dve.match_replace(values, top[:], values, -3.4e38))
                    if t >= RING:
                        dve.wait_ge(far_in[t % RING], (t // RING) * 512)
                    dve.transpose(placeT[t % RING][:], place[:]).then_inc(place_ready, 1)

                for n in range(NT + LAG):
                    t = n - LAG
                    if t >= 0:
                        m = t % RING
                        dve.wait_ge(far_in[m], (t // RING + 1) * 512)
                        every = lambda ap: ap[:].unsqueeze(1).broadcast_to([P, 32, ROPE1])
                        rotate(dve, own, far[m][:, :, CKV:], far[m][:, :, CKV:], every(keep["cos_far"]),
                               every(keep["sin_far"]), turned[:], swapped[:]).then_inc(keys_ready, 1)
                        for g in range(NG):
                            dve.wait_ge(score_full, t * NG + g + 1)
                            if t >= 1 and g == 0:
                                dve.wait_ge(turn_full, t * TURNS - 1)
                            dve.scalar_tensor_tensor(probs[:, g, :], mask[:, min(t, 1), g, :], FILL,
                                                     score[g % 2][:, 0:SC], ALU.mult, ALU.add).then_inc(score_free, 1)
                        dve.wait_ge(score_free, (t + 1) * NG)
                        own.link(dve.tensor_reduce(biggest[:], probs[:], AX.X, ALU.max))
                        dve.tensor_scalar(biggest[:], biggest[:], -SCALE1, None, ALU.mult).then_inc(shift_ready, 1)
                    if n < NT:
                        for j in range(idx_base[n], idx_base[n + 1]):
                            h = (j - idx_base[n]) % NIDX
                            lo, hi = chunks[n][(j - idx_base[n]) // NIDX]
                            dve.wait_ge(relu_ready, j + 1)
                            if h:
                                dve.wait_ge(summed, j)
                                ins = dve.scalar_tensor_tensor(index[:, lo:hi], relu[j % 2][:, 0:hi - lo],
                                                               keep["idx_w"][:, h:h + 1], index[:, lo:hi], ALU.mult,
                                                               ALU.add)
                            else:
                                ins = dve.tensor_scalar(index[:, lo:hi], relu[j % 2][:, 0:hi - lo],
                                                        keep["idx_w"][:, 0:1], None, ALU.mult)
                            ins.then_inc(summed, 1)
                    if t >= 0:
                        dve.wait_ge(exp_ready, t + 1)
                        own.link(dve.reciprocal(den[:], den[:]))
                        for g in range(NG):
                            ins = dve.tensor_scalar(probs[:, g, :], probs[:, g, :], den[:, g:g + 1], None, ALU.mult)
                        ins.then_inc(normed, 1)
                    if n < NT:
                        rank(n)

            @block.tensor
            def _(pe):
                def fill(t, k):
                    kind, i = (turns + turns2)[k]
                    n = t * TURNS + k
                    b = turn[n % 2]
                    if n >= 2:
                        pe.wait_ge(turn_free, n - 1)
                    for j in range(4):
                        out = b[:, j * P:(j + 1) * P]
                        if kind == "q":
                            first = (i // 2) * ROPE1
                            ins = pe.transpose(out[0:KW, :], QN[:, t, 4 * (i % 2) + j, first:first + KW], ident[:])
                        elif kind == "far":
                            ins = pe.transpose(out[0:KW, :], far[t % RING][:, 4 * i + j, :], ident[:])
                        elif kind == "p":
                            g = 4 * (i % 2) + j
                            ins = pe.transpose(out, probs[:, g, (i // 2) * P:(i // 2 + 1) * P], ident[:])
                    if kind == "y":
                        for h in range(H1):
                            ins = pe.matmul(b[:, 0:P], nout[:, h, :], ctxT[:, h:NG * P:H1], start=(h == 0),
                                            stop=(h == H1 - 1))
                    ins.then_inc(turn_full, 1)

                def scores(t, g):
                    n = t * NG + g
                    b = score[n % 2]
                    if g == 0:
                        pe.wait_ge(turn_free, t * TURNS + 4)
                    pe.wait_ge(turn_free, t * TURNS + 4 + g + 1)
                    if n >= 2:
                        pe.wait_ge(score_free, n - 1)
                    pe.matmul(b[:, 0:WIN], qT[:, 0, 4 * g:4 * g + 4].rearrange("k i a h -> k (i a h)"), near[:, t * P:t * P + WIN],
                              start=True, stop=True)
                    for j in range(4):
                        ins = pe.matmul(b[32 * j:32 * j + 32, WIN:SC], qT[:, 1, 4 * g + j].rearrange("k a h -> k (a h)"),
                                        farT[:, g % 4, j, :], start=True, stop=True)
                    ins.then_inc(score_full, 1)

                for n in range(NT + LAG):
                    t = n - LAG
                    if t >= 0:
                        for k in range(4):
                            fill(t, k)
                        pe.wait_ge(keys_ready, t + 1)
                        for g in range(NG):
                            fill(t, 4 + g)
                            if g >= 1:
                                scores(t, g - 1)
                        scores(t, NG - 1)
                    if n < NT:
                        for j in range(idx_base[n], idx_base[n + 1]):
                            h = (j - idx_base[n]) % NIDX
                            lo, hi = chunks[n][(j - idx_base[n]) // NIDX]
                            half = slice((h % 2) * DH1, (h % 2 + 1) * DH1)
                            if j >= 2:
                                pe.wait_ge(relu_ready, j - 1)
                            pe.matmul(idx[j % 2][:, 0:hi - lo], qiT[half, h // 2, n * P:(n + 1) * P],
                                      kiT[half, lo:hi], start=True, stop=True).then_inc(idx_full, 1)
                    if t >= 0:
                        pe.wait_ge(normed, t + 1)
                        for k in range(len(turns), TURNS - 1):
                            fill(t, k)
                        pe.wait_ge(turn_free, (t + 1) * TURNS - 1)
                        if t >= 1:
                            pe.wait_ge(ctx_copied, t)
                        for c in range(2):
                            out = ctxp[:, c * CH:(c + 1) * CH]
                            parts = [1] if t == 0 else [0, 1]
                            for part in parts:
                                pe.matmul(out, rows[:, t - 1 + part, 0:CKV],
                                          probsT[:, part, 4 * c:4 * c + 4, :].rearrange("p g l -> p (g l)"),
                                          start=(part == parts[0]), stop=False, skip_group_check=True)
                            for i in range(16 * c, 16 * c + 16):
                                cols = slice((i % 4) * 32, (i % 4 + 1) * 32)
                                ins = pe.matmul(ctxp[:, i * 32:(i + 1) * 32], far[t % RING][:, i, 0:CKV],
                                                probsT[:, 2, i // 4, cols], start=False, stop=(i % 16 == 15),
                                                skip_group_check=True)
                        ins.then_inc(ctx_full, 1)
                        pe.wait_ge(ctx_copied, t + 1)
                        fill(t, TURNS - 1)


def layer1_attention(nc, dram, x, ident, yT):
    with ExitStack() as ctx:
        sb, _, sem = allocators(nc, ctx)
        keep = {
            "rows": sb("rows", [P, NT, KW], F32),
            "queries": sb("queries", [P, NT, H1, QW], F32),
            "near_keys": sb("near_keys", [KW, P + T], F32),
            "nout": sb("nout", [CKV, H1, D], F32),
            "qiT": sb("qiT", [P, 2, T], F32),
            "kiT": sb("kiT", [P, T], F32),
            "idx_w": sb("idx_w", [P, NIDX], F32),
            "cap0": sb("cap0", [P, KTS], F32),
            "cap": sb("cap", [P, P], F32),
            "mask": sb("mask", [P, 2, NG, SC], F16),
            "cos_far": sb("cos_far", [P, ROPE1], F32),
            "sin_far": sb("sin_far", [P, ROPE1], F32),
            "rows_ready": sem("rows_ready"),
            "table_out": sem("table_out"),
            "table": dram["key_table"],
        }
        projections1(nc, dram, x, ident, yT, keep)
        selected_attention(nc, dram, ident, yT, keep)


TOPK1 = 2
PRIME = 11
HASH_OFF = 7919
CLASS = T // E1
KS = HS // P
CLASS_EXPERTS = [[(r * PRIME + k * HASH_OFF) % E1 for k in range(TOPK1)] for r in range(E1)]


def layer1_experts(nc, dram, x, ident, yT):
    with ExitStack() as ctx:
        sb, ps, sem = allocators(nc, ctx)
        xn = sb("e1_xn", [P, NT, D], F32)
        xnT = sb("e1_xnT", [P, T], F32)
        sw1 = sb("sw1", [P, HS], F32)
        sw3 = sb("sw3", [P, HS], F32)
        sw2 = sb("sw2", [P, KS, D], F32)
        w1 = sb("e1_w1", [P, E1, HR], F32)
        w2 = sb("e1_w2", [HR, E1, D], F32)
        sb13 = sb("sb13", [P, 2, KS], F32)
        sb2 = sb("sb2", [P, 1], F32)
        b1 = sb("e1_b1", [HR, E1], F32)
        b2 = sb("e1_b2", [P, TOPK1, E1], F32)
        b2_sum = sb("e1_b2_sum", [P, E1], F32)
        silu = [sb(f"e1_silu{i}", [P, CH], F32) for i in range(2)]
        hid = [sb(f"e1_hid{i}", [P, CH], F32) for i in range(2)]
        part = [sb(f"e1_part{i}", [P, CLASS], F32) for i in range(2)]
        work = norm_work(sb, "3")
        bank = [ps(f"e1_bank{i}", [P, CH], F32) for i in range(2)]
        up = [ps(f"e1_up{i}", [P, CH], F32) for i in range(2)]
        gate = [ps(f"e1_gate{i}", [P, CH], F32) for i in range(2)]
        down = [ps(f"e1_down{i}", [P, CH], F32) for i in range(2)]
        (w_in, turned, added, var, std, own_sem, normed, xnT_full, xnT_ready, up_full, act_ready, hid_ready, hid_used,
         down_read, y_ready, y_turned, out_ready, out_done) = (
             sem("e1_" + n) for n in (
                 "w_in", "turned", "added", "var", "std", "own", "normed", "xnT_full", "xnT_ready", "up_full",
                 "act_ready", "hid_ready", "hid_used", "down_read", "y_ready", "y_turned", "out_ready",
                 "out_done"))
        loads = [(sw1, "sw1"), (sw3, "sw3"), (sw2, "sw2"), (sb13, "sb13"), (sb2, "sb2"), (w1, "e1_w1"), (w2, "e1_w2"),
                 (b1, "e1_b1"), (b2, "e1_b2")]
        SHARED = NCH * KS
        ROUTED = E1 * TOPK1

        with nc.Block() as block:
            @block.sync
            def _(sp):
                for dst, src in loads:
                    sp.dma_start(dst[:], dram[src]).then_inc(w_in, 16)
                rows = dram["out"].rearrange("(t p) d -> p t d", p=P)
                for c in range(NCH):
                    sp.wait_ge(out_ready, c + 1)
                    sp.dma_start(rows[:, 4 * c:4 * c + 4, :], x[:, 4 * c:4 * c + 4, :]).then_inc(out_done, 16)
                sp.wait_ge(out_done, NCH * 16)

            @block.scalar
            def _(act):
                act.wait_ge(var, 1)
                act.activation(work[3][:], work[2][:], ACT.Sqrt).then_inc(std, 1)
                act.wait_ge(w_in, len(loads) * 16)
                for n in range(SHARED):
                    act.wait_ge(up_full, n + 1)
                    if n >= 2:
                        act.wait_ge(hid_ready, n - 1)
                    act.activation(silu[n % 2][:], up[n % 2][:], ACT.Silu, bias=sb13[:, 0, n % KS:n % KS + 1]
                                   ).then_inc(act_ready, 1)
                for i in range(ROUTED):
                    n = SHARED + i
                    e = CLASS_EXPERTS[i // TOPK1][i % TOPK1]
                    act.wait_ge(up_full, n + 1)
                    act.wait_ge(hid_used, n - 1)
                    act.activation(hid[n % 2][:, 0:CLASS], up[n % 2][:, 0:CLASS], ACT.Gelu, bias=b1[:, e:e + 1]
                                   ).then_inc(act_ready, 1)

            @block.vector
            def _(dve):
                own = Order(dve, own_sem)
                add_transposed(dve, None, x, yT, ident, bank, turned, added)()
                dve.wait_ge(added, NCH)
                layer_norm(dve, own, x, xn, work, var, std, 0)
                dve.wait_ge(w_in, len(loads) * 16)
                dve.tensor_tensor(b2_sum[:], b2[:, 0, :], b2[:, 1, :], ALU.add).then_inc(normed, 1)
                for c in range(NCH):
                    dve.wait_ge(xnT_full, c + 1)
                    dve.tensor_copy(xnT[:, c * CH:(c + 1) * CH], bank[c % 2][:]).then_inc(xnT_ready, 1)

                def shared_out(c):
                    dve.wait_ge(hid_used, (c + 1) * KS)
                    dve.tensor_scalar(yT[:, c * CH:(c + 1) * CH], down[c % 2][:], sb2[:], 0.5, ALU.add, ALU.mult
                                      ).then_inc(down_read, 1)

                for n in range(SHARED):
                    dve.wait_ge(act_ready, n + 1)
                    if n >= 2:
                        dve.wait_ge(hid_used, n - 1)
                    dve.scalar_tensor_tensor(hid[n % 2][:], gate[n % 2][:], sb13[:, 1, n % KS:n % KS + 1],
                                             silu[n % 2][:], ALU.add, ALU.mult).then_inc(hid_ready, 1)
                    if n >= KS and n % KS == 0:
                        shared_out(n // KS - 1)
                shared_out(NCH - 1)
                dve.wait_ge(down_read, NCH)
                for r in range(E1):
                    n = NCH + r
                    dve.wait_ge(hid_used, SHARED + (r + 1) * TOPK1)
                    own.link(dve.tensor_scalar(part[r % 2][:], down[n % 2][:, 0:CLASS], b2_sum[:, r:r + 1],
                                               0.5 / TOPK1, ALU.add, ALU.mult))
                    dve.tensor_tensor(yT[:, r:T:E1], yT[:, r:T:E1], part[r % 2][:], ALU.add).then_inc(down_read, 1)
                add_transposed(dve, None, x, yT, ident, bank, y_turned, out_ready)()

            @block.tensor
            def _(pe):
                add_transposed(None, pe, x, yT, ident, bank, turned, added)()
                pe.wait_ge(normed, 1)
                for c in range(NCH):
                    if c >= 2:
                        pe.wait_ge(xnT_ready, c - 1)
                    for j in range(4):
                        ins = pe.transpose(bank[c % 2][:, j * P:(j + 1) * P], xn[:, 4 * c + j, :], ident[:])
                    ins.then_inc(xnT_full, 1)
                pe.wait_ge(w_in, len(loads) * 16)
                pe.wait_ge(xnT_ready, NCH)

                def rise(n):
                    if n >= 2:
                        pe.wait_ge(act_ready, n - 1)
                    if n < SHARED:
                        if n >= 2:
                            pe.wait_ge(hid_ready, n - 1)
                        c, k = n // KS, n % KS
                        cols, half = slice(c * CH, (c + 1) * CH), slice(k * P, (k + 1) * P)
                        pe.matmul(up[n % 2][:], sw1[:, half], xnT[:, cols], start=True, stop=True)
                        ins = pe.matmul(gate[n % 2][:], sw3[:, half], xnT[:, cols], start=True, stop=True)
                    else:
                        r, k = (n - SHARED) // TOPK1, (n - SHARED) % TOPK1
                        ins = pe.matmul(up[n % 2][:, 0:CLASS], w1[:, CLASS_EXPERTS[r][k], :], xnT[:, r:T:E1],
                                        start=True, stop=True)
                    ins.then_inc(up_full, 1)

                def fall(n):
                    if n < SHARED:
                        out, k, last = n // KS, n % KS, KS - 1
                        pe.wait_ge(hid_ready, n + 1)
                        w, width = sw2[:, k, :], CH
                    else:
                        r, k = (n - SHARED) // TOPK1, (n - SHARED) % TOPK1
                        out, last = NCH + r, TOPK1 - 1
                        pe.wait_ge(act_ready, n + 1)
                        w, width = w2[:, CLASS_EXPERTS[r][k], :], CLASS
                    if k == 0 and out >= 2:
                        pe.wait_ge(down_read, out - 1)
                    ins = pe.matmul(down[out % 2][:, 0:width], w, hid[n % 2][:, 0:width], start=(k == 0),
                                    stop=(k == last))
                    ins.then_inc(hid_used, 1)

                for n in range(SHARED + ROUTED):
                    rise(n)
                    if n:
                        fall(n - 1)
                fall(SHARED + ROUTED - 1)
                pe.wait_ge(down_read, NCH + E1)
                add_transposed(None, pe, x, yT, ident, bank, y_turned, out_ready)()


def build(nc, dram):
    with ExitStack() as ctx:
        sb, _, _ = allocators(nc, ctx)
        x = sb("x", [P, NT, D], F32)
        ident = sb("ident", [P, P], F32)
        yT = sb("yT", [P, T], F32)
        layer0_attention(nc, dram, x, ident, yT)
        layer0_experts(nc, dram, x, ident, yT)
        layer1_attention(nc, dram, x, ident, yT)
        layer1_experts(nc, dram, x, ident, yT)


def tables():
    f32 = np.float32
    t = {"ident": np.eye(P, dtype=f32)}
    inv = 1.0 / 10000.0 ** (np.arange(0, DH0, 2, dtype=f32) / DH0)
    angle = np.outer(np.arange(T, dtype=f32), inv)
    cos = np.concatenate([np.cos(angle), np.cos(angle)], -1)[:, ::2].T.astype(f32)
    sin = np.concatenate([np.sin(angle), np.sin(angle)], -1)[:, ::2].T.astype(f32)
    t["cos0"] = np.ascontiguousarray(np.tile(cos, (4, 1)))
    t["sin0"] = np.ascontiguousarray(np.tile(np.concatenate([-sin, sin], 0), (2, 1)))
    theta = (1.0 / 10000.0 ** (2.0 * np.arange(HALF1, dtype=f32) / f32(ROPE1))).astype(np.float64)
    place = np.arange(T)

    def turn(steps):
        c, s = np.cos(np.outer(steps, theta)), np.sin(np.outer(steps, theta))
        return np.concatenate([c, c], 1).astype(f32), np.concatenate([-s, s], 1).astype(f32)

    for name, steps in (("k", place), ("near", np.where(place < LW, place, 2 * place - LW + 1)), ("q", place)):
        for part, table in zip(("cos_", "sin_"), turn(steps)):
            t[part + name] = table.reshape(NT, P, ROPE1).transpose(1, 0, 2)
    t["cos_far"], t["sin_far"] = (np.tile(v, (4, 1)) for v in turn(LW + np.arange(FAR)))
    l, k = np.arange(P)[:, None], np.arange(P)[None, :]
    t["cap"] = np.where(k <= l, 3.4e38, -3.3e38).astype(f32)
    k = np.arange(KTS)[None, :]
    t["cap0"] = np.where(k <= l - LW, 3.4e38, np.where(k <= l, -3.3e38, -1e36 * (k + 1))).astype(f32)
    row = np.arange(P)
    i4, quarter = row // 32, row % 32 // H1
    l = (32 * quarter + i4)[:, None, None] + 4 * np.arange(NG)[None, :, None]
    s = np.arange(WIN)[None, None, :] - P
    gathered = np.broadcast_to(np.arange(P)[None, None, :] // FAR == quarter[:, None, None], (P, NG, P))
    first = np.where(l < LW, (s >= 0) & (s < KTS), (s > l - LW) & (s <= l))
    rest = (s > l - LW) & (s <= l)
    keep = np.stack([np.concatenate([first, gathered & (l >= LW)], 2), np.concatenate([rest, gathered], 2)], 1)
    t["mask"] = np.where(keep, 0.0, -60000.0).astype(np.float16)
    t["iota"] = np.tile(np.arange(E0, dtype=f32), (P, 1))
    return t


def layouts(a):
    even_odd = np.concatenate([np.arange(0, DH0, 2), np.arange(1, DH0, 2)])
    odd_even = np.concatenate([np.arange(1, DH0, 2), np.arange(0, DH0, 2)])
    twice = lambda w, axis: np.concatenate([w, w], axis)

    def up(w, order):
        w = w.reshape(H0, DH0, LAT0)[:, order, :].transpose(2, 0, 1)
        return twice(twice(w, 2).reshape(LAT0, H0 * P), 0)

    m = {
        "x": a["L0_attn_x"].reshape(T, D),
        "ln_scale": a["L0_attn_ln_scale"].reshape(D, 1),
        "ln_bias": a["L0_attn_ln_bias"].reshape(D, 1),
        "wdq": twice(a["L0_attn_w_down_q"].T, 1),
        "wdkv": twice(a["L0_attn_w_down_kv"].T, 1),
        "wq": up(a["L0_attn_w_up_q"], even_odd),
        "wq_sw": up(a["L0_attn_w_up_q"], odd_even),
        "wk": up(a["L0_attn_w_up_k"], even_odd),
        "wk_sw": up(a["L0_attn_w_up_k"], odd_even),
        "wv": a["L0_attn_w_up_v"].reshape(H0, DH0, LAT0).transpose(0, 2, 1),
        "wg": a["L0_ffn_Wg"].T,
        "e0_w1": a["L0_ffn_W1"].transpose(0, 2, 1),
        "e0_w3": a["L0_ffn_W3"].transpose(0, 2, 1),
        "e0_w2": a["L0_ffn_W2"].transpose(0, 2, 1),
        "e0_b13": np.stack([a["L0_ffn_b1"], a["L0_ffn_b3"]], 2),
        "e0_b2": a["L0_ffn_b2"],
        "wkvr": np.concatenate([a["L1_attn_W_dkv"], a["L1_attn_W_kr"]], 1),
        "a1_wdq": a["L1_attn_W_dq"],
        "wuq": a["L1_attn_W_uq"].reshape(CQ, H1, DH1).transpose(2, 1, 0),
        "wuk": a["L1_attn_W_uk"].reshape(CKV, H1, DH1).transpose(2, 1, 0),
        "wuv": a["L1_attn_W_uv"].reshape(CKV, H1, DH1).transpose(2, 1, 0),
        "wqr": a["L1_attn_W_qr"],
        "a1_wo": a["L1_attn_W_out"].reshape(H1, DH1, D).transpose(1, 0, 2),
        "widxq": a["L1_attn_idx_wq"],
        "widxk": twice(a["L1_attn_idx_wk"], 1),
        "idx_w": np.tile(a["L1_attn_idx_w"], (P, 1)),
        "sw1": a["L1_ffn_sw1"],
        "sw3": a["L1_ffn_sw3"],
        "sw2": a["L1_ffn_sw2"].reshape(KS, P, D).transpose(1, 0, 2),
        "sb13": np.stack([a["L1_ffn_sb1"].reshape(KS, P).T, a["L1_ffn_sb3"].reshape(KS, P).T], 1),
        "sb2": a["L1_ffn_sb2"].reshape(D, 1),
        "e1_w1": a["L1_ffn_w1"].transpose(1, 0, 2),
        "e1_b1": a["L1_ffn_b1"].T,
        "e1_w2": a["L1_ffn_w2"].transpose(1, 0, 2),
        "e1_b2": a["L1_ffn_b2"][CLASS_EXPERTS].transpose(2, 1, 0),
        "w_out": a["L0_attn_w_out"].reshape(D, H0, DH0).transpose(1, 2, 0),
    }
    return m


def kernel(**inputs):
    import concourse.bacc as bacc
    from concourse.bass_utils import run_bass_kernel_spmd as run

    nc = bacc.Bacc("TRN2", target_bir_lowering=False, num_devices=1)
    arrays, dram = {}, {}
    host = layouts({k: np.asarray(v) for k, v in inputs.items()})
    host.update(tables())
    for name, a in host.items():
        a = np.ascontiguousarray(a)
        arrays["in_" + name] = a
        dram[name] = nc.dram_tensor("in_" + name, a.shape, mybir.dt.from_np(a.dtype), kind="ExternalInput").ap()
    dram["out"] = nc.dram_tensor("out_0", (T, D), F32, kind="ExternalOutput").ap()
    dram["key_table"] = nc.dram_tensor("key_table", (T, KW), F32, kind="Internal").ap()
    build(nc, dram)
    r = run(nc, [arrays], core_ids=[0])
    return r.results[0]["out_0"].reshape(1, T, D)
```

```python
from contextlib import ExitStack

import numpy as np

import concourse.bass as bass
from concourse import mybir

F32 = mybir.dt.float32
F16 = mybir.dt.float16
U32 = mybir.dt.uint32
ALU = mybir.AluOpType
ACT = mybir.ActivationFunctionType
AX = mybir.AxisListType

P = 128
T = 2048
NT = T // P
D = 128
CH = 512
NCH = T // CH
LN_EPS = 1e-5

H0 = 16
DH0 = 64
LAT0 = 64
E0 = 16
TOPK0 = 4
GROUPS0 = 4
TOPG0 = 2
ROUTE_SCALE = 2.5
H1 = 8
DH1 = 64
CKV = 32
CQ = 64
ROPE1 = 32
HALF1 = ROPE1 // 2
NIDX = 4
KTS = 96
LW = 64
FAR = KTS - LW
SCALE1 = float((DH1 + ROPE1) ** -0.5)
E1 = 8
HS = 256
HR = 128


class Order:

    def __init__(self, eng, sem):
        self.eng, self.sem, self.n = eng, sem, 0

    def mark(self, ins):
        ins.then_inc(self.sem, 1)
        self.n += 1

    def wait(self):
        self.eng.wait_ge(self.sem, self.n)

    def link(self, ins):
        self.mark(ins)
        self.wait()


def layer_norm(dve, own, src, dst, work, var_ready, std_ready, k):
    stats, mv, var, std, rec, t, rstd = work
    for i in range(NT):
        own.mark(dve.bn_stats(stats[:, i, :], src[:, i, :]))
    own.wait()
    for i in range(NT):
        own.mark(dve.bn_aggr(mv[:, i, :], stats[:, i, :]))
    own.wait()
    dve.tensor_scalar(var[:], mv[:, :, 1], LN_EPS, None, ALU.add).then_inc(var_ready, 1)
    dve.wait_ge(std_ready, k + 1)
    own.link(dve.reciprocal(rec[:], std[:]))
    own.link(dve.tensor_tensor(t[:], rec[:], rec[:], ALU.mult))
    own.link(dve.tensor_tensor(t[:], t[:], var[:], ALU.mult))
    own.link(dve.tensor_scalar(t[:], t[:], -0.5, 1.5, ALU.mult, ALU.add))
    own.link(dve.tensor_tensor(rstd[:], rec[:], t[:], ALU.mult))
    for i in range(NT):
        own.mark(dve.tensor_scalar(dst[:, i, :], src[:, i, :], mv[:, i, 0:1], rstd[:, i:i + 1],
                                   ALU.subtract, ALU.mult))
    own.wait()


def norm_work(sb, tag):
    return (sb(f"stats{tag}", [P, NT, 6], F32), sb(f"mv{tag}", [P, NT, 2], F32),
            *(sb(f"{n}{tag}", [P, NT], F32) for n in ("var", "std", "rec", "newton", "rstd")))


def allocators(nc, ctx):
    return (lambda n, s, d: ctx.enter_context(nc.sbuf_tensor(n, s, d)),
            lambda n, s, d: ctx.enter_context(nc.psum_tensor(n, s, d)),
            lambda n: ctx.enter_context(nc.semaphore(n)))


def latents(nc, dram, x, ident, keep):
    with ExitStack() as ctx:
        sb, ps, sem = allocators(nc, ctx)
        xa = sb("xa", [P, NT, D], F32)
        xh = sb("xh", [P, NT, D], F32)
        hT = sb("hT", [P, T], F32)
        scale = sb("ln_scale", [P, 1], F32)
        bias = sb("ln_bias", [P, 1], F32)
        wdq = sb("wdq", [P, P], F32)
        wdkv = sb("wdkv", [P, P], F32)
        stage = [sb(f"w_stage{i}", [P, H0 * P], F32) for i in range(2)]
        work = norm_work(sb, "0")
        bank = [ps(f"lat_bank{i}", [P, CH], F32) for i in range(2)]
        x_in, small_in = sem("x_in"), sem("small_in")
        w_in = [sem(f"w_in{i}") for i in range(2)]
        w_split, rope_in = sem("w_split"), keep["rope_in"]
        var0, std0, own_sem = sem("var0"), sem("std0"), sem("dve_own0")
        xh_ready, hT_bank, hT_ready, lat_bank, lat_ready = (
            sem(n) for n in ("xh_ready", "hT_bank", "hT_ready", "lat_bank_full", "lat_ready"))
        weights = ["wq", "wq_sw", "wk", "wk_sw", "wv"]

        with nc.Block() as block:
            @block.sync
            def _(sp):
                sp.dma_start(x[:], dram["x"].rearrange("(t p) d -> p t d", p=P)).then_inc(x_in, 16)
                for dst, src in ((ident, "ident"), (scale, "ln_scale"), (bias, "ln_bias"), (wdq, "wdq"),
                                 (wdkv, "wdkv")):
                    sp.dma_start(dst[:], dram[src]).then_inc(small_in, 16)
                for i, w in enumerate(weights):
                    if i >= 2:
                        sp.wait_ge(w_split, i - 1)
                    sp.dma_start(stage[i % 2][:, 0:keep[w].shape[1]], dram[w]).then_inc(w_in[i % 2], 16)
                sp.dma_start(keep["cos"][:], dram["cos0"]).then_inc(rope_in, 16)
                sp.dma_start(keep["sin"][:], dram["sin0"]).then_inc(rope_in, 16)
                sp.dma_start(keep["w_out"][:], dram["w_out"]).then_inc(keep["head_w_in"], 16)

            @block.scalar
            def _(act):
                for k in range(2):
                    act.wait_ge(var0, k + 1)
                    act.activation(work[3][:], work[2][:], ACT.Sqrt).then_inc(std0, 1)

            @block.vector
            def _(dve):
                own = Order(dve, own_sem)
                dve.wait_ge(x_in, 16)
                layer_norm(dve, own, x, xa, work, var0, std0, 0)
                layer_norm(dve, own, xa, xh, work, var0, std0, 1)
                dve.tensor_tensor(x[:], x[:], xa[:], ALU.add).then_inc(xh_ready, 1)
                dve.wait_ge(small_in, 5 * 16)
                for c in range(NCH):
                    dve.wait_ge(hT_bank, c + 1)
                    dve.tensor_scalar(hT[:, c * CH:(c + 1) * CH], bank[c % 2][:], scale[:], bias[:], ALU.mult,
                                      ALU.add).then_inc(hT_ready, 1)
                for i in range(2 * NCH):
                    c, kv = i % NCH, i // NCH
                    hi, lo = (keep["ck1"], keep["ck2"]) if kv else (keep["cq1"], keep["cq2"])
                    cols = slice(c * CH, (c + 1) * CH)
                    dve.wait_ge(lat_bank, i + 1)
                    own.link(dve.tensor_copy(hi[:, cols], bank[i % 2][:]))
                    dve.tensor_tensor(lo[:, cols], bank[i % 2][:], hi[:, cols], ALU.subtract).then_inc(lat_ready, 1)
                for m in range(2):
                    dve.memset(keep["k_b"][m][LAT0:LAT0 + 2, :], 1.0)
                    dve.memset(keep["v"][m][:, :, DH0:DH0 + 1], 1.0)

            @block.gpsimd
            def _(pool):
                own = 0
                for i, w in enumerate(weights):
                    pool.wait_ge(w_in[i % 2], 16 * (i // 2 + 1))
                    if i:
                        pool.wait_ge(w_split, i)
                    cols = slice(0, keep[w].shape[1])
                    pool.tensor_copy(keep[w][:], stage[i % 2][:, cols]).then_inc(keep["pool_own"], 1)
                    own += 1
                    pool.wait_ge(keep["pool_own"], own)
                    pool.tensor_tensor(keep[w][LAT0:P, :], stage[i % 2][LAT0:P, cols], keep[w][LAT0:P, :],
                                       ALU.subtract).then_inc(w_split, 1)

            @block.tensor
            def _(pe):
                pe.wait_ge(small_in, 5 * 16)
                pe.wait_ge(xh_ready, 1)
                for c in range(NCH):
                    if c >= 2:
                        pe.wait_ge(hT_ready, c - 1)
                    for j in range(4):
                        ins = pe.transpose(bank[c % 2][:, j * P:(j + 1) * P], xh[:, 4 * c + j, :], ident[:])
                    ins.then_inc(hT_bank, 1)
                pe.wait_ge(hT_ready, NCH)
                for i in range(2 * NCH):
                    c, kv = i % NCH, i // NCH
                    if i >= 2:
                        pe.wait_ge(lat_ready, i - 1)
                    pe.matmul(bank[i % 2][:], (wdkv if kv else wdq)[:], hT[:, c * CH:(c + 1) * CH], start=True,
                              stop=True).then_inc(lat_bank, 1)


KT0 = T // P
KPAIR = KT0 // 2
STEPS = NCH * KPAIR
QT = CH // P
VW = 2 * DH0 + 1
LAG = 2
SLOTS = 4
VECTOR_LOW = list(range(2 * NCH + 2))
POOL_LOW = [st for st in range(STEPS) if st not in VECTOR_LOW]


def aux_prepare():
    plan = []
    for j in range(2 * NCH):
        plan += [(j, "rope", (j, 0)), (j, "rope", (j, 1))]
    plan += [(2 * NCH, "v", 0), (2 * NCH, "v", 1)]
    plan += [(2 * NCH + 1 + n * 18 // (NT * NCH), "max", (n // NCH, n % NCH)) for n in range(NT * NCH)]
    plan += [(2 * NCH + 20, "shift", 0), (2 * NCH + 20, "shift", 1)]
    return plan


def aux_finish(m, quarter, step):
    plan = [(step + 2, "norm", quarter)]
    return plan + ([(step + 4, "turn", quarter), (step + 5, "out", quarter)] if m else [])


def aux_plan(m, first, last):
    plan = [] if first else aux_finish(1 - m, NCH - 1, LAG - 1)
    for quarter in range(NCH - 1):
        plan += aux_finish(m, quarter, (quarter + 1) * KPAIR + LAG - 1)
    plan += [(st + 1, "low", st) for st in VECTOR_LOW]
    plan += [] if last else aux_prepare()
    return sorted(plan, key=lambda u: u[0])


def banked(plan):
    return [(kind, arg) for _, kind, arg in plan if kind not in ("low", "norm")]


PRO = len(aux_prepare())
BODY = [len(banked(aux_plan(m, False, False))) for m in range(2)]
FIRST = len(banked(aux_plan(0, True, False)))


def aux_base(h, m):
    if isinstance(h, int) and h == 0:
        return PRO
    return PRO + FIRST + (0 if m else BODY[1]) + (h - (1 if m else 2)) * (sum(BODY) // 2)


def heads(nc, dram, x, keep):
    with ExitStack() as ctx:
        sb, ps, sem = allocators(nc, ctx)
        qa = [sb(f"q_a{i}", [P, T], F16) for i in range(2)]
        qb = [sb(f"q_b{i}", [LAT0 + 2, T], F16) for i in range(2)]
        ka = [sb(f"k_a{i}", [P, T], F16) for i in range(2)]
        kb = keep["k_b"]
        v = keep["v"]
        probs = sb("probs", [P, SLOTS, 2, CH], F32)
        probs_hi = sb("probs_hi", [P, SLOTS, 2, CH], F16)
        probs_lo = sb("probs_lo", [P, SLOTS, 2, CH], F16)
        term = [[sb(f"rope_term{i}{j}", [P, CH], F32) for j in range(2)] for i in range(2)]
        roped = [sb(f"roped{i}", [P, CH], F32) for i in range(2)]
        part_max = sb("part_max", [P, NT, NCH], F32)
        row_max = sb("row_max", [P, NT], F32)
        shift16 = sb("shift16", [P, NT], F16)
        shift = sb("shift", [P, 2, NT], F32)
        shift_row = sb("shift_row", [NT, 2, P], F16)
        unnorm = [sb(f"unnorm{i}", [P, 2, QT // 2 * VW], F32) for i in range(2)]
        inv = sb("inv", [P, QT], F32)
        summed = sb("summed", [P, QT, DH0], F32)
        heads_out = sb("heads_out", [P, NT, 2, DH0], F32)
        headsT = sb("headsT", [P, CH], F32)
        scores = [ps(f"scores{i}", [P, 2, CH], F32) for i in range(2)]
        acc = ps("acc", [P, 2, CH], F32)
        aux = ps("aux", [P, 2, CH], F32)
        (aux_full, aux_free, rope_sum, hi_ready, lo_ready, shift_ready, shift_in, scores_ready, probs_ready,
         pool_low, vector_low, probs_used, acc_copied, norm_own, norm_ready, dve_own, v_own) = (
            sem(n) for n in ("aux_full", "aux_free", "rope_sum", "hi_ready", "lo_ready", "shift_ready", "shift_in",
                             "scores_ready", "probs_ready", "pool_low", "vector_low", "probs_used", "acc_copied",
                             "norm_own", "norm_ready", "dve_own1", "v_own"))
        ident = keep["ident"]
        prepare = aux_prepare()
        known = lambda n, below: isinstance(n, int) and n < below

        def prepared_in(hp, mp, kind, arg):
            if known(hp, 1):
                return banked(prepare).index((kind, arg)) + 1
            plan = aux_plan(1 - mp, known(hp, 2), False)
            return aux_base(hp - 1, 1 - mp) + banked(plan).index((kind, arg)) + 1

        def every_head(eng, body):
            body(0, 0, True, False)
            body(1, 1, False, False)
            with eng.Fori(1, H0 // 2 - 1) as pair:
                body(pair * 2, 0, False, False)
                body(pair * 2 + 1, 1, False, False)
            body(H0 - 2, 0, False, False)
            body(H0 - 1, 1, False, True)

        def low_half(eng, h, st):
            n, slot = h * STEPS + st, st % SLOTS
            eng.wait_ge(probs_ready, n + 1)
            if not known(n, SLOTS):
                eng.wait_ge(probs_used, n - SLOTS + 1)
            return eng.tensor_tensor(probs_lo[:, slot], probs[:, slot], probs_hi[:, slot], ALU.subtract)

        with nc.Block() as block:
            @block.sync
            def _(sp):
                def send_shift(hp, mp):
                    sp.wait_ge(aux_free, prepared_in(hp, mp, "shift", 1))
                    for i in range(2):
                        sp.dma_start(qb[mp][LAT0 + i:LAT0 + i + 1, :].rearrange("a (t p) -> a t p", p=P),
                                     shift_row[:, i, :]).then_inc(shift_in, 16)

                def body(h, m, first, last):
                    if not last:
                        send_shift(h + 1, 1 - m)

                send_shift(0, 0)
                every_head(sp, body)

            @block.gpsimd
            def _(pool):
                def rope_add(hp, mp, j):
                    n = hp * (2 * NCH) + j
                    pool.wait_ge(aux_free, prepared_in(hp, mp, "rope", (j, 1)))
                    if not known(n, 2):
                        pool.wait_ge(lo_ready, n - 1)
                    pool.tensor_tensor(roped[j % 2][:], term[j % 2][0][:], term[j % 2][1][:], ALU.add
                                       ).then_inc(rope_sum, 1)

                def rope_low(hp, mp, j):
                    n = hp * (2 * NCH) + j
                    cols = slice((j % NCH) * CH, (j % NCH + 1) * CH)
                    pool.wait_ge(hi_ready, n + 1)
                    rows, dst = (slice(0, LAT0), qb[mp]) if j < NCH else (slice(LAT0, P), ka[mp])
                    hi = qa[mp] if j < NCH else ka[mp]
                    pool.tensor_tensor(dst[rows, cols], roped[j % 2][rows, :], hi[rows, cols], ALU.subtract
                                       ).then_inc(lo_ready, 1)

                for j in range(2 * NCH):
                    if j:
                        pool.wait_ge(lo_ready, j)
                    rope_add(0, 0, j)
                    rope_low(0, 0, j)
                pool.wait_ge(lo_ready, 2 * NCH)

                def body(h, m, first, last):
                    for st in range(STEPS):
                        if st in POOL_LOW:
                            low_half(pool, h, st).then_inc(pool_low, 1)
                        if not last and 2 <= st < 2 * NCH + 2:
                            pool.wait_ge(rope_sum, (h + 1) * (2 * NCH) + min(st, 2 * NCH))
                            rope_low(h + 1, 1 - m, st - 2)
                            pool.wait_ge(lo_ready, (h + 1) * (2 * NCH) + st - 1)
                        if not last and st < 2 * NCH:
                            rope_add(h + 1, 1 - m, st)

                every_head(pool, body)

            @block.scalar
            def _(act):
                def high_halves(hp, mp, j):
                    n = hp * (2 * NCH) + j
                    cols = slice((j % NCH) * CH, (j % NCH + 1) * CH)
                    act.wait_ge(rope_sum, n + 1)
                    if j < NCH:
                        act.activation(qa[mp][:, cols], roped[j % 2][:], ACT.Copy).then_inc(hi_ready, 1)
                    else:
                        act.activation(kb[mp][0:LAT0, cols], roped[j % 2][0:LAT0, :], ACT.Copy)
                        act.activation(ka[mp][:, cols], roped[j % 2][:], ACT.Copy).then_inc(hi_ready, 1)

                def copy_acc(q, slot):
                    act.wait_ge(probs_used, (q + 1) * KPAIR)
                    if not known(q, 2):
                        act.wait_ge(norm_ready, q - 1)
                    act.activation(unnorm[slot][:], acc[:, :, 0:QT // 2 * VW], ACT.Copy).then_inc(acc_copied, 1)

                for j in range(2 * NCH):
                    high_halves(0, 0, j)

                def body(h, m, first, last):
                    for st in range(STEPS):
                        n = h * STEPS + st
                        act.wait_ge(scores_ready, n + 1)
                        if not known(n, SLOTS):
                            act.wait_ge(probs_used, n - SLOTS + 1)
                        for dst in (probs, probs_hi):
                            ins = act.activation(dst[:, st % SLOTS], scores[st % 2][:], ACT.Exp,
                                                 scale=float(DH0) ** -0.5)
                        ins.then_inc(probs_ready, 1)
                        if not last and 1 <= st < 2 * NCH + 1:
                            high_halves(h + 1, 1 - m, st - 1)
                        if st % KPAIR == LAG - 1 and not (first and st < KPAIR):
                            copy_acc(h * NCH - 1 + st // KPAIR, (st // KPAIR - 1) % 2)

                every_head(act, body)
                copy_acc(H0 * NCH - 1, 1)

            @block.vector
            def _(dve):
                def empty(u, slot, kind, arg, hp, mp, h):
                    bank = aux[:, slot, :]
                    dve.wait_ge(aux_full, u + 1)
                    if kind == "rope":
                        j, part = arg
                        cols = slice((j % NCH) * CH, (j % NCH + 1) * CH)
                        if not (known(hp, 1) and j < 2):
                            dve.wait_ge(rope_sum, hp * (2 * NCH) + j - 1)
                        table = keep["sin"] if part else keep["cos"]
                        dve.tensor_tensor(term[j % 2][part][:], bank, table[:, cols], ALU.mult).then_inc(aux_free, 1)
                    elif kind == "v":
                        if not known(hp, 2):
                            dve.wait_ge(probs_used, (hp - 1) * STEPS)
                        tiles = slice(8 * arg, 8 * arg + 8)
                        rows = bank.rearrange("p (t d) -> p t d", d=DH0)
                        dve.tensor_copy(v[mp][:, tiles, 0:DH0], rows).then_inc(v_own, 1)
                        dve.wait_ge(v_own, hp * 2 + arg + 1)
                        dve.tensor_tensor(v[mp][:, tiles, DH0 + 1:], rows, v[mp][:, tiles, 0:DH0], ALU.subtract
                                          ).then_inc(aux_free, 1)
                    elif kind == "max":
                        t, c = arg
                        dve.tensor_reduce(part_max[:, t, c:c + 1], bank, AX.X, ALU.max).then_inc(aux_free, 1)
                    elif kind == "shift":
                        if not known(hp, 1):
                            dve.wait_ge(shift_in, hp * 32)
                        dve.tensor_copy(shift_row[:, arg, :], bank[0:NT, 0:P]).then_inc(aux_free, 1)
                    elif kind == "turn":
                        dve.tensor_copy(headsT[:], bank).then_inc(aux_free, 1)
                    elif kind == "out":
                        rows = x[:, QT * arg:QT * arg + QT, :].rearrange("p t d -> p (t d)")
                        dve.tensor_tensor(rows, rows, bank, ALU.add).then_inc(aux_free, 1)

                def normalise(q, slot, quarter, m):
                    own = Order(dve, norm_own)
                    own.n = q * 2
                    sums = unnorm[slot][:].rearrange("p b (t c) -> p (b t) c", c=VW)
                    dve.wait_ge(acc_copied, q + 1)
                    own.mark(dve.reciprocal(inv[:].unsqueeze(2), sums[:, :, DH0:DH0 + 1]))
                    own.link(dve.tensor_tensor(summed[:], sums[:, :, 0:DH0], sums[:, :, DH0 + 1:], ALU.add))
                    dve.tensor_tensor(heads_out[:, QT * quarter:QT * quarter + QT, m, :], summed[:],
                                      inv[:].unsqueeze(2).broadcast_to([P, QT, DH0]), ALU.mult
                                      ).then_inc(norm_ready, 1)

                def row_maxima(hp, mp):
                    dve.wait_ge(aux_free, prepared_in(hp, mp, "max", (NT - 1, NCH - 1)))
                    step = hp * 3
                    dve.tensor_reduce(row_max[:], part_max[:], AX.X, ALU.max).then_inc(dve_own, 1)
                    dve.wait_ge(dve_own, step + 1)
                    dve.tensor_scalar(shift16[:], row_max[:], -1.0, None, ALU.mult).then_inc(dve_own, 1)
                    dve.wait_ge(dve_own, step + 2)
                    dve.tensor_copy(shift[:, 0, :], shift16[:]).then_inc(dve_own, 1)
                    dve.wait_ge(dve_own, step + 3)
                    dve.scalar_tensor_tensor(shift[:, 1, :], row_max[:], -1.0, shift[:, 0, :], ALU.mult,
                                             ALU.subtract).then_inc(shift_ready, 1)

                dve.wait_ge(keep["rope_in"], 2 * 16)
                for u, (kind, arg) in enumerate(banked(prepare)):
                    if kind == "shift" and arg == 0:
                        row_maxima(0, 0)
                    empty(u, u % 2, kind, arg, 0, 0, None)

                def body(h, m, first, last):
                    base, u = aux_base(h, m), 0
                    for _, kind, arg in aux_plan(m, first, last):
                        if kind == "low":
                            low_half(dve, h, arg).then_inc(vector_low, 1)
                        elif kind == "norm":
                            old = arg == NCH - 1
                            normalise(h * NCH - 1 if old else h * NCH + arg, arg % 2, arg, 1 - m if old else m)
                        else:
                            if kind == "shift" and arg == 0:
                                row_maxima(h + 1, 1 - m)
                            empty(base + u, u % 2, kind, arg, h + 1, 1 - m, h)
                            u += 1

                every_head(dve, body)
                normalise(H0 * NCH - 1, 1, NCH - 1, 1)
                base = aux_base(H0 - 1, 1) + len(banked(aux_plan(1, False, True)))
                for u, kind in enumerate(("turn", "out")):
                    empty(base + u, u, kind, NCH - 1, None, None, H0 - 1)

            @block.tensor
            def _(pe):
                def fill(u, slot, kind, arg, hp, mp, h):
                    bank = aux[:, slot, :]
                    if not known(u, 2):
                        pe.wait_ge(aux_free, u - 1)
                    if kind == "rope":
                        j, part = arg
                        q = j < NCH
                        w = keep[("wq", "wq_sw", "wk", "wk_sw")[2 * (not q) + part]]
                        hi, lo = (keep["cq1"], keep["cq2"]) if q else (keep["ck1"], keep["ck2"])
                        cols = slice((j % NCH) * CH, (j % NCH + 1) * CH)
                        w = w[:, bass.ds(hp * P, P)]
                        pe.matmul(bank, w, hi[:, cols], start=True, stop=False)
                        ins = pe.matmul(bank, w, lo[:, cols], start=False, stop=True)
                    elif kind == "v":
                        for t in range(8):
                            tok = (8 * arg + t) * P
                            w, out = keep["wv"][:, bass.ds(hp * DH0, DH0)], bank[:, t * DH0:(t + 1) * DH0]
                            pe.matmul(out, keep["ck1"][:, tok:tok + P], w, start=True, stop=False)
                            ins = pe.matmul(out, keep["ck2"][:, tok:tok + P], w, start=False, stop=True)
                    elif kind == "max":
                        t, c = arg
                        if t == 0 and c == 0:
                            pe.wait_ge(hi_ready, (hp + 1) * (2 * NCH))
                        ins = pe.matmul(bank, qa[mp][0:LAT0, t * P:(t + 1) * P], ka[mp][0:LAT0, c * CH:(c + 1) * CH],
                                        start=True, stop=True)
                    elif kind == "shift":
                        pe.wait_ge(shift_ready, hp + 1)
                        ins = pe.transpose(bank[0:NT, 0:P], shift[:, arg, :], ident[:])
                    elif kind == "turn":
                        pe.wait_ge(norm_ready, h * NCH + arg + 1)
                        for i in range(QT):
                            ins = pe.transpose(bank[:, i * P:(i + 1) * P],
                                               heads_out[:, QT * arg + i, :, :].rearrange("p a d -> p (a d)"), ident[:])
                    elif kind == "out":
                        pe.wait_ge(aux_free, u)
                        for i in range(QT):
                            ins = pe.matmul(bank[:, i * P:(i + 1) * P], headsT[:, i * P:(i + 1) * P],
                                            keep["w_out"][:, bass.ds((h - 1) * (D // 2), D)], start=True, stop=True)
                    ins.then_inc(aux_full, 1)

                def score(h, m, st, i):
                    quarter, pair = st // KPAIR, st % KPAIR
                    n = h * STEPS + st
                    if st == 0 and i == 0:
                        pe.wait_ge(lo_ready, (h + 1) * (2 * NCH))
                        pe.wait_ge(shift_in, (h + 1) * 32)
                    if not known(n, 2) and i == 0:
                        pe.wait_ge(probs_ready, n - 1)
                    cols = slice(quarter * CH, (quarter + 1) * CH)
                    keys = slice((2 * pair + i) * P, (2 * pair + i + 1) * P)
                    out = scores[st % 2][:, i, :]
                    pe.matmul(out, ka[m][:, keys], qa[m][:, cols], start=True, stop=False)
                    ins = pe.matmul(out, kb[m][:, keys], qb[m][:, cols], start=False, stop=True)
                    if i:
                        ins.then_inc(scores_ready, 1)

                def weigh(h, m, st, i):
                    quarter, pair = st // KPAIR, st % KPAIR
                    if st == 0 and i == 0:
                        pe.wait_ge(aux_free, prepared_in(h, m, "v", 1))
                    if pair == 0 and i == 0 and not known(h * NCH + quarter, 1):
                        pe.wait_ge(acc_copied, h * NCH + quarter)
                    if i == 0 and st in POOL_LOW:
                        pe.wait_ge(pool_low, h * len(POOL_LOW) + POOL_LOW.index(st) + 1)
                    elif i == 0:
                        pe.wait_ge(vector_low, h * len(VECTOR_LOW) + VECTOR_LOW.index(st) + 1)
                    kt = 2 * pair + i
                    for t in range(QT):
                        queries = slice(t * P, (t + 1) * P)
                        out = acc[:, t // 2, (t % 2) * VW:(t % 2 + 1) * VW]
                        pe.matmul(out, probs_hi[:, st % SLOTS, i, queries], v[m][:, kt, :],
                                  start=(kt == 0 and t % 2 == 0), stop=False, skip_group_check=True)
                        ins = pe.matmul(out[:, 0:DH0 + 1], probs_lo[:, st % SLOTS, i, queries],
                                        v[m][:, kt, 0:DH0 + 1], start=False, stop=(kt == KT0 - 1),
                                        skip_group_check=True)
                    if i:
                        ins.then_inc(probs_used, 1)

                pe.wait_ge(keep["head_w_in"], 16)
                for u, (kind, arg) in enumerate(banked(prepare)):
                    fill(u, u % 2, kind, arg, 0, 0, None)

                def body(h, m, first, last):
                    base, u = aux_base(h, m), 0
                    plan = aux_plan(m, first, last)
                    for st in range(STEPS):
                        now = [(kind, arg) for kind, arg in banked([w for w in plan if w[0] == st])]
                        for part in range(4):
                            if part < 2:
                                score(h, m, st, part)
                            elif st >= LAG:
                                weigh(h, m, st - LAG, part - 2)
                            elif not first:
                                weigh(h - 1, 1 - m, STEPS + st - LAG, part - 2)
                            for kind, arg in now[part * len(now) // 4:(part + 1) * len(now) // 4]:
                                old = kind in ("turn", "out") and arg == NCH - 1
                                fill(base + u, u % 2, kind, arg, h + 1, 1 - m, h - 1 if old else h)
                                u += 1

                every_head(pe, body)
                for st in range(STEPS - LAG, STEPS):
                    for i in range(2):
                        weigh(H0 - 1, 1, st, i)
                base = aux_base(H0 - 1, 1) + len(banked(aux_plan(1, False, True)))
                for u, kind in enumerate(("turn", "out")):
                    fill(base + u, u, kind, NCH - 1, None, None, H0 - 1)


def layer0_attention(nc, dram, x, ident):
    with ExitStack() as ctx:
        sb, _, sem = allocators(nc, ctx)
        keep = {"ident": ident}
        for n in ("cos", "sin"):
            keep[n] = sb(n, [P, T], F32)
        for n in ("wq", "wq_sw", "wk", "wk_sw"):
            keep[n] = sb(n, [P, H0 * P], F16)
        for n in ("cq1", "cq2", "ck1", "ck2"):
            keep[n] = sb(n, [P, T], F16)
        keep["wv"] = sb("wv", [P, H0 * DH0], F16)
        keep["w_out"] = sb("w_out", [P, H0 // 2 * D], F32)
        keep["k_b"] = [sb(f"k_b{i}", [LAT0 + 2, T], F16) for i in range(2)]
        keep["v"] = [sb(f"v{i}", [P, KT0, VW], F16) for i in range(2)]
        for n in ("rope_in", "head_w_in", "pool_own"):
            keep[n] = sem(n)
        latents(nc, dram, x, ident, keep)
        heads(nc, dram, x, keep)


def add_transposed(dve, pe, x, yT, ident, bank, turned, added):
    def turn():
        for c in range(NCH):
            if c >= 2:
                pe.wait_ge(added, c - 1)
            for j in range(4):
                t = 4 * c + j
                ins = pe.transpose(bank[c % 2][:, j * P:(j + 1) * P], yT[:, t * P:(t + 1) * P], ident[:])
            ins.then_inc(turned, 1)

    def add():
        for c in range(NCH):
            dve.wait_ge(turned, c + 1)
            rows = x[:, 4 * c:4 * c + 4, :].rearrange("p t d -> p (t d)")
            dve.tensor_tensor(rows, rows, bank[c % 2][:], ALU.add).then_inc(added, 1)

    return turn if dve is None else add


def layer0_experts(nc, dram, x, ident):
    with ExitStack() as ctx:
        sb, ps, sem = allocators(nc, ctx)
        xn = sb("e0_xn", [P, NT, D], F32)
        xnT = sb("e0_xnT", [P, T], F32)
        wg = sb("wg", [P, E0], F32)
        b2 = sb("e0_b2", [E0, D], F32)
        iota = sb("iota", [P, E0], F32)
        s = sb("gate_s", [P, NT, E0], F32)
        best_of = sb("best_of_group", [P, NT, 8], F32)
        top = sb("gate_top", [P, NT, 8], F32)
        at = sb("gate_at", [P, NT, 8], U32)
        atf = sb("gate_atf", [P, NT, 8], F32)
        gmask = sb("group_mask", [P, NT, GROUPS0], F32)
        hit = sb("gate_hit", [P, NT, E0], F32)
        chosen = sb("gate_chosen", [P, NT, E0], F32)
        total = sb("gate_total", [P, NT], F32)
        weT = sb("gate_wT", [E0, T], F32)
        w = [sb(f"e0_w{i}", [P, 3, P], F32) for i in range(2)]
        b13 = [sb(f"e0_b13{i}", [P, 2], F32) for i in range(2)]
        silu = [sb(f"e0_silu{i}", [P, CH], F32) for i in range(2)]
        hid = [sb(f"e0_hid{i}", [P, CH], F32) for i in range(2)]
        work = norm_work(sb, "1")
        bank = [ps(f"e0_bank{i}", [P, CH], F32) for i in range(2)]
        up = [ps(f"e0_up{i}", [P, CH], F32) for i in range(2)]
        gate = [ps(f"e0_gate{i}", [P, CH], F32) for i in range(2)]
        down = [ps(f"e0_down{i}", [P, 4, D], F32) for i in range(2)]
        (small_in, var, std, own_sem, normed, xnT_full, xnT_ready, logits, gated, weT_full, weT_ready,
         bias_full, bias_added, chosen_ready, up_full, silu_ready, hid_ready, down_full, down_added) = (
            sem("e0_" + n) for n in (
                "small_in", "var", "std", "own", "normed", "xnT_full", "xnT_ready", "logits",
                "gated", "weT_full", "weT_ready", "bias_full", "bias_added", "chosen_ready", "up_full", "silu_ready",
                "hid_ready", "down_full", "down_added"))
        w_in = [sem(f"e0_w_in{i}") for i in range(2)]
        SMALL = 3

        with nc.Block() as block:
            @block.sync
            def _(sp):
                for dst, src in ((wg, "wg"), (b2, "e0_b2"), (iota, "iota")):
                    sp.dma_start(dst[:], dram[src]).then_inc(small_in, 16)

                def load(e, m):
                    for j, n in enumerate(("e0_w1", "e0_w3", "e0_w2")):
                        sp.dma_start(w[m][:, j, :], dram[n][bass.ds(e, 1), :, :].rearrange("a d i -> (a d) i")
                                     ).then_inc(w_in[m], 16)
                    sp.dma_start(b13[m][:], dram["e0_b13"][bass.ds(e, 1), :, :].rearrange("a i j -> (a i) j")
                                 ).then_inc(w_in[m], 16)

                load(0, 0)
                load(1, 1)
                with sp.Fori(1, E0 // 2) as pair:
                    for m in range(2):
                        e = pair * 2 + m
                        sp.wait_ge(down_full, (e - 1) * NCH)
                        load(e, m)

            @block.scalar
            def _(act):
                act.wait_ge(var, 1)
                act.activation(work[3][:], work[2][:], ACT.Sqrt).then_inc(std, 1)
                act.wait_ge(logits, 1)
                act.activation(s[:].rearrange("p t e -> p (t e)"), bank[0][:, 0:NT * E0], ACT.Sigmoid
                               ).then_inc(gated, 1)

                def expert(e, m):
                    act.wait_ge(w_in[m], (e - m) * 32 + 64)
                    for c in range(NCH):
                        n = e * NCH + c
                        act.wait_ge(up_full, n + 1)
                        if not (isinstance(n, int) and n < 2):
                            act.wait_ge(hid_ready, n - 1)
                        act.activation(silu[c % 2][:], up[c % 2][:], ACT.Silu, bias=b13[m][:, 0:1]
                                       ).then_inc(silu_ready, 1)

                expert(0, 0)
                expert(1, 1)
                with act.Fori(1, E0 // 2) as pair:
                    expert(pair * 2, 0)
                    expert(pair * 2 + 1, 1)

            @block.vector
            def _(dve):
                own = Order(dve, own_sem)
                layer_norm(dve, own, x, xn, work, var, std, 0)
                dve.memset(best_of[:], -1.0).then_inc(normed, 1)
                for c in range(NCH):
                    dve.wait_ge(xnT_full, c + 1)
                    dve.tensor_copy(xnT[:, c * CH:(c + 1) * CH], bank[c % 2][:]).then_inc(xnT_ready, 1)

                def top8(values):
                    for t in range(NT):
                        own.mark(dve.max(top[:, t, :], values[:, t, :]))
                    own.wait()
                    for t in range(NT):
                        own.mark(dve.max_index(at[:, t, :], top[:, t, :], values[:, t, :]))
                    own.wait()
                    own.link(dve.tensor_copy(atf[:], at[:]))

                def mark(mask, n, count):
                    places = iota[:, 0:n].unsqueeze(1).broadcast_to([P, NT, n])
                    for k in range(count):
                        own.link(dve.tensor_tensor(hit[:, :, 0:n] if k else mask, places,
                                                   atf[:, :, k:k + 1].broadcast_to([P, NT, n]), ALU.is_equal))
                        if k:
                            own.link(dve.tensor_tensor(mask, mask, hit[:, :, 0:n], ALU.add))

                dve.wait_ge(small_in, SMALL * 16)
                dve.wait_ge(gated, 1)
                dve.wait_ge(normed, 1)
                own.link(dve.tensor_reduce(best_of[:, :, 0:GROUPS0],
                                           s[:].rearrange("p t (g k) -> p t g k", g=GROUPS0), AX.X, ALU.max))
                top8(best_of)
                mark(gmask[:], GROUPS0, TOPG0)
                per_expert = gmask[:].unsqueeze(3).broadcast_to([P, NT, GROUPS0, E0 // GROUPS0])
                own.link(dve.tensor_tensor(hit[:].rearrange("p t (g k) -> p t g k", g=GROUPS0),
                                           s[:].rearrange("p t (g k) -> p t g k", g=GROUPS0), per_expert, ALU.mult))
                own.link(dve.tensor_scalar(gmask[:], gmask[:], -1.0, None, ALU.add))
                own.link(dve.tensor_tensor(chosen[:].rearrange("p t (g k) -> p t g k", g=GROUPS0),
                                           hit[:].rearrange("p t (g k) -> p t g k", g=GROUPS0), per_expert, ALU.add))
                top8(chosen)
                mark(chosen[:], E0, TOPK0)
                own.link(dve.tensor_tensor(s[:], s[:], chosen[:], ALU.mult))
                own.link(dve.tensor_reduce(total[:], s[:], AX.X, ALU.add))
                own.link(dve.reciprocal(total[:], total[:]))
                own.link(dve.tensor_tensor(s[:], s[:], total[:].unsqueeze(2).broadcast_to([P, NT, E0]), ALU.mult))
                dve.tensor_scalar(s[:], s[:], ROUTE_SCALE, None, ALU.mult).then_inc(chosen_ready, 1)
                for c in range(NCH):
                    dve.wait_ge(weT_full, c + 1)
                    dve.tensor_copy(weT[:, c * CH:(c + 1) * CH], bank[c % 2][0:E0, :]).then_inc(weT_ready, 1)
                for c in range(NCH):
                    dve.wait_ge(bias_full, c + 1)
                    rows = x[:, 4 * c:4 * c + 4, :].rearrange("p t d -> p (t d)")
                    dve.tensor_tensor(rows, rows, bank[c % 2][:], ALU.add).then_inc(bias_added, 1)
                dve.wait_ge(bias_added, NCH)

                def add_down(n, c, e):
                    dve.wait_ge(down_full, n + 1)
                    if not (isinstance(n, int) and n < NCH):
                        dve.wait_ge(down_added, n - NCH + 1)
                    for j in range(4):
                        t = 4 * c + j
                        ins = dve.scalar_tensor_tensor(x[:, t, :], down[c % 2][:, j, :], s[:, t, bass.ds(e, 1)],
                                                       x[:, t, :], ALU.mult, ALU.add)
                    ins.then_inc(down_added, 1)

                def expert(e, m, first):
                    dve.wait_ge(w_in[m], (e - m) * 32 + 64)
                    for c in range(NCH):
                        n = e * NCH + c
                        dve.wait_ge(silu_ready, n + 1)
                        if not (isinstance(n, int) and n < 2):
                            dve.wait_ge(down_full, n - 1)
                        dve.scalar_tensor_tensor(hid[c % 2][:], gate[c % 2][:], b13[m][:, 1:2], silu[c % 2][:],
                                                 ALU.add, ALU.mult).then_inc(hid_ready, 1)
                        if c:
                            add_down(n - 1, c - 1, e)
                        elif not first:
                            add_down(n - 1, NCH - 1, e - 1)

                expert(0, 0, True)
                expert(1, 1, False)
                with dve.Fori(1, E0 // 2) as pair:
                    expert(pair * 2, 0, False)
                    expert(pair * 2 + 1, 1, False)
                add_down(E0 * NCH - 1, NCH - 1, E0 - 1)

            @block.tensor
            def _(pe):
                pe.wait_ge(normed, 1)
                for c in range(NCH):
                    if c >= 2:
                        pe.wait_ge(xnT_ready, c - 1)
                    for j in range(4):
                        ins = pe.transpose(bank[c % 2][:, j * P:(j + 1) * P], xn[:, 4 * c + j, :], ident[:])
                    ins.then_inc(xnT_full, 1)
                pe.wait_ge(xnT_ready, NCH)
                pe.wait_ge(small_in, SMALL * 16)
                for t in range(NT):
                    ins = pe.matmul(bank[0][:, t * E0:(t + 1) * E0], xnT[:, t * P:(t + 1) * P], wg[:], start=True,
                                    stop=True)
                ins.then_inc(logits, 1)
                pe.wait_ge(chosen_ready, 1)
                for c in range(NCH):
                    if c >= 2:
                        pe.wait_ge(weT_ready, c - 1)
                    for j in range(4):
                        ins = pe.transpose(bank[c % 2][0:E0, j * P:(j + 1) * P], s[:, 4 * c + j, :], ident[:])
                    ins.then_inc(weT_full, 1)
                pe.wait_ge(weT_ready, NCH)
                for c in range(NCH):
                    if c >= 2:
                        pe.wait_ge(bias_added, c - 1)
                    for j in range(4):
                        ins = pe.matmul(bank[c % 2][:, j * P:(j + 1) * P], weT[:, (4 * c + j) * P:(4 * c + j + 1) * P],
                                        b2[:], start=True, stop=True)
                    ins.then_inc(bias_full, 1)

                def put_down(n, c, m):
                    pe.wait_ge(hid_ready, n + 1)
                    if not (isinstance(n, int) and n < 2):
                        pe.wait_ge(down_added, n - 1)
                    for j in range(4):
                        ins = pe.matmul(down[c % 2][:, j, :], hid[c % 2][:, j * P:(j + 1) * P], w[m][:, 2, :],
                                        start=True, stop=True)
                    ins.then_inc(down_full, 1)

                def expert(e, m, first):
                    pe.wait_ge(w_in[m], (e - m) * 32 + 64)
                    for c in range(NCH):
                        n = e * NCH + c
                        cols = slice(c * CH, (c + 1) * CH)
                        if not (isinstance(n, int) and n < 2):
                            pe.wait_ge(hid_ready, n - 1)
                        pe.matmul(up[c % 2][:], w[m][:, 0, :], xnT[:, cols], start=True, stop=True)
                        pe.matmul(gate[c % 2][:], w[m][:, 1, :], xnT[:, cols], start=True, stop=True
                                  ).then_inc(up_full, 1)
                        if c:
                            put_down(n - 1, c - 1, m)
                        elif not first:
                            put_down(n - 1, NCH - 1, 1 - m)

                expert(0, 0, True)
                expert(1, 1, False)
                with pe.Fori(1, E0 // 2) as pair:
                    expert(pair * 2, 0, False)
                    expert(pair * 2 + 1, 1, False)
                put_down(E0 * NCH - 1, NCH - 1, 1)


KW = CKV + ROPE1
QW = 2 * ROPE1 + CKV
NQ = H1 * ROPE1
GROUP = 16
NG = P // GROUP
WIN = 2 * P
SC = WIN + P
FILL = 1e25


def index_width(t):
    return KTS if t == 0 else t * P + P - LW


def rotate(dve, own, dst, mu, cos, sin, turned, swapped):
    own.mark(dve.tensor_tensor(turned, mu, cos, ALU.mult))
    lo, hi = slice(0, HALF1), slice(HALF1, ROPE1)
    last = lambda ap, cols: ap[(slice(None),) * (ap.ndim - 1) + (cols,)]
    own.mark(dve.tensor_tensor(last(swapped, lo), last(mu, hi), last(sin, lo), ALU.mult))
    own.mark(dve.tensor_tensor(last(swapped, hi), last(mu, lo), last(sin, hi), ALU.mult))
    own.wait()
    return dve.tensor_tensor(dst, turned, swapped, ALU.add)


def projections1(nc, dram, x, ident, yT, keep):
    with ExitStack() as ctx:
        sb, ps, sem = allocators(nc, ctx)
        xnT = sb("a1_xnT", [P, T], F32)
        wkvr = sb("wkvr", [P, KW], F32)
        wdq = sb("a1_wdq", [P, CQ], F32)
        wuq = sb("wuq", [DH1, H1, CQ], F32)
        wuk = sb("wuk", [DH1, H1, CKV], F32)
        wuv = sb("wuv", [DH1, H1, CKV], F32)
        wo = sb("a1_wo", [DH1, H1, D], F32)
        wqq = sb("wqq", [CQ, H1 * CKV + NQ], F32)
        widxq = sb("widxq", [P, NIDX * DH1], F32)
        widxk = sb("widxk", [P, P], F32)
        pre = sb("pre_softplus", [P, NT, NQ + ROPE1], F32)
        e = sb("softplus_e", [P, NT, NQ + ROPE1], F32)
        u = sb("softplus_u", [P, NT, NQ + ROPE1], F32)
        angle = {n: sb(n, [P, NT, ROPE1], F32) for n in ("cos_k", "sin_k", "cos_near", "sin_near", "cos_q", "sin_q")}
        xn = u[:, :, 0:D]
        cqT = e[:].rearrange("p t c -> p (t c)")[0:CQ, 0:T]
        near_key = xnT[:, 0:NT * KW].rearrange("p (t k) -> p t k", k=KW)
        work = norm_work(sb, "2")
        bank = [ps(f"a1_bank{i}", [P, CH], F32) for i in range(4)]
        (w_in, turned, added, var, std, own_sem, normed, full, free, act_own, abs_ready, e_ready, u_ready, ln_ready,
         near_ready) = (sem("a1_" + n) for n in (
             "w_in", "turned", "added", "var", "std", "own", "normed", "full", "free", "act_own", "abs_ready", "e_ready",
             "u_ready", "ln_ready", "near_ready"))
        rows, QN, near, nout, qiT, kiT = (keep[n] for n in ("rows", "queries", "near_keys", "nout", "qiT", "kiT"))
        loads = [(wkvr, "wkvr"), (wdq, "a1_wdq"), (wuq, "wuq"), (wuk, "wuk"), (wqq[:, H1 * CKV:], "wqr"),
                 (wuv, "wuv"), (wo, "a1_wo"), (widxq, "widxq"), (widxk, "widxk"), (keep["idx_w"], "idx_w"),
                 (keep["cap0"], "cap0"), (keep["cap"], "cap"), (keep["mask"], "mask"), (keep["cos_far"], "cos_far"),
                 (keep["sin_far"], "sin_far"), *((angle[n], n) for n in angle)]

        jobs = [("xnT", c) for c in range(NCH)] + [("kv", i) for i in range(2)] + [("cq", c) for c in range(NCH)]
        jobs += [("wqq", 0)] + [("q", t) for t in range(NT)]
        SOFT = len(jobs)
        jobs += [("ki", c) for c in range(NCH)] + [("qi", i) for i in range(2 * NCH)] + [("nout", i) for i in range(2)]
        SOFT2 = len(jobs)
        jobs += [("near", c) for c in range(NCH)]

        with nc.Block() as block:
            @block.sync
            def _(sp):
                for dst, src in loads:
                    sp.dma_start(dst if isinstance(dst, bass.AP) else dst[:], dram[src]).then_inc(w_in, 16)
                sp.wait_ge(keep["rows_ready"], 1)
                sp.dma_start(keep["table"].rearrange("(t p) d -> p t d", p=P), rows[:]).then_inc(keep["table_out"], 16)
                sp.wait_ge(keep["table_out"], 16)

            @block.scalar
            def _(act):
                act.wait_ge(var, 1)
                act.activation(work[3][:], work[2][:], ACT.Sqrt).then_inc(std, 1)

                def drain(n):
                    kind, i = jobs[n]
                    src = bank[n % 4]
                    copies = {
                        "xnT": lambda: [(xnT[:, i * CH:(i + 1) * CH], src[:])],
                        "kv": lambda: [(rows[:, 8 * i:8 * i + 8, 0:CKV], kv[:, :, 0:CKV]),
                                       (pre[:, 8 * i:8 * i + 8, NQ:], kv[:, :, CKV:])],
                        "cq": lambda: [(cqT[:, i * CH:(i + 1) * CH], src[0:CQ, :])],
                        "wqq": lambda: [(wqq[:, 0:H1 * CKV], src[0:CQ, 0:H1 * CKV])],
                        "q": lambda: [(QN[:, i, :, ROPE1:ROPE1 + CKV],
                                       src[:, 0:H1 * CKV].rearrange("p (h c) -> p h c", h=H1)),
                                      (pre[:, i, 0:NQ], src[:, H1 * CKV:])],
                        "ki": lambda: [(kiT[:, i * CH:(i + 1) * CH], src[:])],
                        "qi": lambda: [(qiT[:, i // NCH, (i % NCH) * CH:(i % NCH + 1) * CH], src[:])],
                        "nout": lambda: [(nout[:, 4 * i:4 * i + 4, :],
                                          src[0:CKV, :].rearrange("c (h n) -> c h n", h=4))],
                        "near": lambda: [(near[:, P + i * CH:P + (i + 1) * CH], src[0:KW, :])],
                    }
                    kv = src[:].rearrange("p (t k) -> p t k", k=KW)
                    act.wait_ge(full, n + 1)
                    for out, in_ in copies[kind]():
                        ins = act.activation(out, in_, ACT.Copy)
                    ins.then_inc(free, 1)

                for n in range(SOFT):
                    drain(n)
                act.wait_ge(free, SOFT)
                act.activation(e[:], pre[:], ACT.Abs).then_inc(abs_ready, 1)
                act.wait_ge(abs_ready, 1)
                act.activation(e[:], e[:], ACT.Exp, scale=-1.0).then_inc(e_ready, 1)
                for n in range(SOFT, SOFT2):
                    drain(n)
                act.wait_ge(u_ready, 1)
                act.activation(u[:], u[:], ACT.Ln).then_inc(ln_ready, 1)
                for n in range(SOFT2, len(jobs)):
                    drain(n)

            @block.vector
            def _(dve):
                own = Order(dve, own_sem)
                dve.memset(near[:, 0:P], 0.0)
                layer_norm(dve, own, x, xn, work, var, std, 0)
                dve.memset(yT[:], 0.0).then_inc(normed, 1)
                dve.wait_ge(e_ready, 1)
                own.link(dve.tensor_scalar(u[:], e[:], 1.0, None, ALU.add))
                dve.scalar_tensor_tensor(e[:], u[:], -1.0, e[:], ALU.add, ALU.subtract).then_inc(u_ready, 1)
                dve.wait_ge(ln_ready, 1)
                own.link(dve.tensor_tensor(u[:], u[:], e[:], ALU.subtract))
                own.link(dve.scalar_tensor_tensor(pre[:], pre[:], 0.0, u[:], ALU.max, ALU.add))
                mu_k = pre[:, :, NQ:]
                dve.tensor_copy(rows[:, :, CKV:], mu_k).then_inc(keep["rows_ready"], 1)
                dve.wait_ge(w_in, len(loads) * 16)
                own.mark(dve.tensor_copy(near_key[:, :, ROPE1:], rows[:, :, 0:CKV]))
                rotate(dve, own, near_key[:, :, 0:ROPE1], mu_k, angle["cos_k"][:], angle["sin_k"][:],
                       e[:, :, NQ:], u[:, :, NQ:]).then_inc(near_ready, 1)
                dve.wait_ge(near_ready, 1)
                mu_q = pre[:, :, 0:NQ].rearrange("p t (h r) -> p t h r", h=H1)
                e_q = e[:, :, 0:NQ].rearrange("p t (h r) -> p t h r", h=H1)
                u_q = u[:, :, 0:NQ].rearrange("p t (h r) -> p t h r", h=H1)
                every = lambda ap: ap[:].unsqueeze(2).broadcast_to([P, NT, H1, ROPE1])
                own.link(rotate(dve, own, QN[:, :, :, 0:ROPE1], mu_q, every(angle["cos_near"]),
                                every(angle["sin_near"]), e_q, u_q))
                own.link(rotate(dve, own, QN[:, :, :, ROPE1 + CKV:], mu_q, every(angle["cos_q"]),
                                every(angle["sin_q"]), e_q, u_q))

            @block.tensor
            def _(pe):
                def fill(n):
                    kind, i = jobs[n]
                    b = bank[n % 4]
                    if n >= 4:
                        pe.wait_ge(free, n - 3)
                    mm = lambda out, lhsT, rhs: pe.matmul(out, lhsT, rhs, start=True, stop=True)
                    cols = slice(i * CH, (i + 1) * CH)
                    if kind == "xnT":
                        for j in range(4):
                            ins = pe.transpose(b[:, j * P:(j + 1) * P], xn[:, 4 * i + j, :], ident[:])
                    elif kind == "kv":
                        for j in range(8):
                            t = 8 * i + j
                            ins = mm(b[:, j * KW:(j + 1) * KW], xnT[:, t * P:(t + 1) * P], wkvr[:])
                    elif kind == "cq":
                        ins = mm(b[0:CQ, :], wdq[:], xnT[:, cols])
                    elif kind == "wqq":
                        for h in range(H1):
                            ins = mm(b[0:CQ, h * CKV:(h + 1) * CKV], wuq[:, h, :], wuk[:, h, :])
                    elif kind == "q":
                        ins = mm(b[:], cqT[:, i * P:(i + 1) * P], wqq[:])
                    elif kind == "ki":
                        ins = mm(b[:], widxk[:], xnT[:, cols])
                    elif kind == "qi":
                        c = i % NCH
                        ins = mm(b[:], widxq[:, (i // NCH) * P:(i // NCH + 1) * P], xnT[:, c * CH:(c + 1) * CH])
                    elif kind == "nout":
                        for h in range(4):
                            ins = mm(b[0:CKV, h * D:(h + 1) * D], wuv[:, 4 * i + h, :], wo[:, 4 * i + h, :])
                    else:
                        for j in range(4):
                            ins = pe.transpose(b[0:KW, j * P:(j + 1) * P], near_key[:, 4 * i + j, :], ident[:])
                    ins.then_inc(full, 1)

                pe.wait_ge(normed, 1)
                for n, (kind, i) in enumerate(jobs):
                    if n == NCH:
                        pe.wait_ge(w_in, len(loads) * 16)
                        pe.wait_ge(free, NCH)
                    if (kind, i) in (("wqq", 0), ("q", 0)):
                        pe.wait_ge(free, n)
                    if (kind, i) == ("near", 0):
                        pe.wait_ge(near_ready, 1)
                    fill(n)


def selected_attention(nc, dram, ident, yT, keep):
    with ExitStack() as ctx:
        sb, ps, sem = allocators(nc, ctx)
        rows, QN, near, nout, qiT, kiT, mask = (
            keep[n] for n in ("rows", "queries", "near_keys", "nout", "qiT", "kiT", "mask"))
        RING = 3
        index = sb("index", [P, T], F32)
        relu = [sb(f"relu{i}", [P, CH], F32) for i in range(2)]
        top = sb("a1_top", [P, 8], F32)
        place = sb("place", [P, FAR], U32)
        placeT = [sb(f"placeT{i}", [P, FAR], U32) for i in range(RING)]
        far = [sb(f"far{i}", [P, 32, KW], F32) for i in range(RING)]
        turned = sb("far_turned", [P, 32, ROPE1], F32)
        swapped = sb("far_swapped", [P, 32, ROPE1], F32)
        qT = sb("qT", [KW, 2, 32, 4, H1], F32)
        farT = sb("farT", [KW, 4, 4, P], F32)
        probs = sb("a1_probs", [P, NG, SC], F32)
        probsT = sb("a1_probsT", [P, 3, NG, P], F32)
        biggest = sb("biggest", [P, NG], F32)
        den = sb("a1_den", [P, NG], F32)
        ctxT = sb("ctxT", [CKV, NG * P], F32)
        score = [ps(f"a1_score{i}", [P, CH], F32) for i in range(2)]
        turn = [ps(f"a1_turn{i}", [P, CH], F32) for i in range(2)]
        idx = [ps(f"a1_idx{i}", [P, CH], F32) for i in range(2)]
        ctxp = ps("a1_ctx", [CKV, NG * P], F32)
        (idx_full, relu_ready, summed, own_sem, place_ready, keys_ready, turn_full, turn_free, score_full, score_free,
         shift_ready, exp_ready, normed, ctx_full, ctx_copied) = (sem("a1_" + n) for n in (
             "idx_full", "relu_ready", "summed", "own2", "place_ready", "keys_ready", "turn_full", "turn_free",
             "score_full", "score_free", "shift_ready", "exp_ready", "normed_p", "ctx_full", "ctx_copied"))
        far_in = [sem(f"far_in{i}") for i in range(RING)]
        LAG = 2

        chunks = [[(c, min(c + CH, index_width(t))) for c in range(0, index_width(t), CH)] for t in range(NT)]
        idx_base = [0]
        for t in range(NT):
            idx_base.append(idx_base[-1] + len(chunks[t]) * NIDX)
        turns = [("q", i) for i in range(4)] + [("far", g) for g in range(NG)]
        turns2 = [("p", i) for i in range(6)] + [("y", 0)]
        TURNS = len(turns) + len(turns2)

        with nc.Block() as block:
            @block.gpsimd
            def _(pool):
                pool.wait_ge(keep["table_out"], 16)
                for t in range(NT):
                    m = t % RING
                    pool.wait_ge(place_ready, t + 1)
                    if t >= RING:
                        pool.wait_ge(ctx_full, t - RING + 1)
                    for i in range(32):
                        pool.indirect_dma_start(far[m][:, i, :], None, keep["table"],
                                                bass.IndirectOffsetOnAxis(ap=placeT[m][:, i:i + 1], axis=0)
                                                ).then_inc(far_in[m], 16)

            @block.scalar
            def _(act):
                def drain(t, k, n):
                    kind, i = (turns + turns2)[k]
                    src = turn[n % 2]
                    act.wait_ge(turn_full, n + 1)
                    if kind == "q":
                        heads = slice(4 * (i % 2), 4 * (i % 2) + 4)
                        ins = act.activation(qT[:, i // 2, :, :, heads].rearrange("k i a h -> k h a i"),
                                             src[0:KW, :].rearrange("k (h a i) -> k h a i", h=4, a=4), ACT.Copy)
                    elif kind == "far":
                        if NG * t + i >= 4:
                            act.wait_ge(score_full, NG * t + i - 3)
                        ins = act.activation(farT[:, i % 4, :, :], src[0:KW, :].rearrange("k (i l) -> k i l", i=4),
                                             ACT.Copy)
                    elif kind == "p":
                        ins = act.activation(probsT[:, i // 2, 4 * (i % 2):4 * (i % 2) + 4, :],
                                             src[:].rearrange("p (g l) -> p g l", g=4), ACT.Copy)
                    else:
                        ins = act.activation(yT[:, t * P:(t + 1) * P].rearrange("d (a i) -> d i a", a=4),
                                             src[:, 0:P].rearrange("d (i a) -> d i a", a=4), ACT.Copy)
                    ins.then_inc(turn_free, 1)

                for n in range(NT + LAG):
                    t = n - LAG
                    if t >= 0:
                        for k in range(len(turns)):
                            drain(t, k, t * TURNS + k)
                        act.wait_ge(shift_ready, t + 1)
                        for g in range(NG):
                            ins = act.activation(probs[:, g, :], probs[:, g, :], ACT.Exp, bias=biggest[:, g:g + 1],
                                                 scale=SCALE1, accum_out=den[:, g:g + 1])
                        ins.then_inc(exp_ready, 1)
                    if n < NT:
                        for j in range(idx_base[n], idx_base[n + 1]):
                            lo, hi = chunks[n][(j - idx_base[n]) // NIDX]
                            act.wait_ge(idx_full, j + 1)
                            if j >= 2:
                                act.wait_ge(summed, j - 1)
                            act.activation(relu[j % 2][:, 0:hi - lo], idx[j % 2][:, 0:hi - lo], ACT.Relu
                                           ).then_inc(relu_ready, 1)
                    if t >= 0:
                        for k in range(len(turns), TURNS - 1):
                            drain(t, k, t * TURNS + k)
                        act.wait_ge(ctx_full, t + 1)
                        act.activation(ctxT[:], ctxp[:], ACT.Copy).then_inc(ctx_copied, 1)
                        drain(t, TURNS - 1, t * TURNS + TURNS - 1)

            @block.vector
            def _(dve):
                own = Order(dve, own_sem)

                def rank(t):
                    w = index_width(t)
                    values = index[:, 0:w]
                    dve.wait_ge(summed, idx_base[t + 1])
                    if t == 0:
                        own.link(dve.tensor_tensor(values, values, keep["cap0"][:], ALU.min))
                    else:
                        own.link(dve.tensor_tensor(index[:, w - P:w], index[:, w - P:w], keep["cap"][:], ALU.min))
                    for r in range(0, FAR, 8):
                        own.link(dve.max(top[:], values))
                        own.link(dve.max_index(place[:, r:r + 8], top[:], values))
                        if r + 8 < FAR:
                            own.link(dve.match_replace(values, top[:], values, -3.4e38))
                    if t >= RING:
                        dve.wait_ge(far_in[t % RING], (t // RING) * 512)
                    dve.transpose(placeT[t % RING][:], place[:]).then_inc(place_ready, 1)

                for n in range(NT + LAG):
                    t = n - LAG
                    if t >= 0:
                        m = t % RING
                        dve.wait_ge(far_in[m], (t // RING + 1) * 512)
                        every = lambda ap: ap[:].unsqueeze(1).broadcast_to([P, 32, ROPE1])
                        rotate(dve, own, far[m][:, :, CKV:], far[m][:, :, CKV:], every(keep["cos_far"]),
                               every(keep["sin_far"]), turned[:], swapped[:]).then_inc(keys_ready, 1)
                        for g in range(NG):
                            dve.wait_ge(score_full, t * NG + g + 1)
                            if t >= 1 and g == 0:
                                dve.wait_ge(turn_full, t * TURNS - 1)
                            dve.scalar_tensor_tensor(probs[:, g, :], mask[:, min(t, 1), g, :], FILL,
                                                     score[g % 2][:, 0:SC], ALU.mult, ALU.add).then_inc(score_free, 1)
                        dve.wait_ge(score_free, (t + 1) * NG)
                        own.link(dve.tensor_reduce(biggest[:], probs[:], AX.X, ALU.max))
                        dve.tensor_scalar(biggest[:], biggest[:], -SCALE1, None, ALU.mult).then_inc(shift_ready, 1)
                    if n < NT:
                        for j in range(idx_base[n], idx_base[n + 1]):
                            h = (j - idx_base[n]) % NIDX
                            lo, hi = chunks[n][(j - idx_base[n]) // NIDX]
                            dve.wait_ge(relu_ready, j + 1)
                            if h:
                                dve.wait_ge(summed, j)
                                ins = dve.scalar_tensor_tensor(index[:, lo:hi], relu[j % 2][:, 0:hi - lo],
                                                               keep["idx_w"][:, h:h + 1], index[:, lo:hi], ALU.mult,
                                                               ALU.add)
                            else:
                                ins = dve.tensor_scalar(index[:, lo:hi], relu[j % 2][:, 0:hi - lo],
                                                        keep["idx_w"][:, 0:1], None, ALU.mult)
                            ins.then_inc(summed, 1)
                    if t >= 0:
                        dve.wait_ge(exp_ready, t + 1)
                        own.link(dve.reciprocal(den[:], den[:]))
                        for g in range(NG):
                            ins = dve.tensor_scalar(probs[:, g, :], probs[:, g, :], den[:, g:g + 1], None, ALU.mult)
                        ins.then_inc(normed, 1)
                    if n < NT:
                        rank(n)

            @block.tensor
            def _(pe):
                def fill(t, k):
                    kind, i = (turns + turns2)[k]
                    n = t * TURNS + k
                    b = turn[n % 2]
                    if n >= 2:
                        pe.wait_ge(turn_free, n - 1)
                    for j in range(4):
                        out = b[:, j * P:(j + 1) * P]
                        if kind == "q":
                            first = (i // 2) * ROPE1
                            ins = pe.transpose(out[0:KW, :], QN[:, t, 4 * (i % 2) + j, first:first + KW], ident[:])
                        elif kind == "far":
                            ins = pe.transpose(out[0:KW, :], far[t % RING][:, 4 * i + j, :], ident[:])
                        elif kind == "p":
                            g = 4 * (i % 2) + j
                            ins = pe.transpose(out, probs[:, g, (i // 2) * P:(i // 2 + 1) * P], ident[:])
                    if kind == "y":
                        for h in range(H1):
                            ins = pe.matmul(b[:, 0:P], nout[:, h, :], ctxT[:, h:NG * P:H1], start=(h == 0),
                                            stop=(h == H1 - 1))
                    ins.then_inc(turn_full, 1)

                def scores(t, g):
                    n = t * NG + g
                    b = score[n % 2]
                    if g == 0:
                        pe.wait_ge(turn_free, t * TURNS + 4)
                    pe.wait_ge(turn_free, t * TURNS + 4 + g + 1)
                    if n >= 2:
                        pe.wait_ge(score_free, n - 1)
                    pe.matmul(b[:, 0:WIN], qT[:, 0, 4 * g:4 * g + 4].rearrange("k i a h -> k (i a h)"), near[:, t * P:t * P + WIN],
                              start=True, stop=True)
                    for j in range(4):
                        ins = pe.matmul(b[32 * j:32 * j + 32, WIN:SC], qT[:, 1, 4 * g + j].rearrange("k a h -> k (a h)"),
                                        farT[:, g % 4, j, :], start=True, stop=True)
                    ins.then_inc(score_full, 1)

                for n in range(NT + LAG):
                    t = n - LAG
                    if t >= 0:
                        for k in range(4):
                            fill(t, k)
                        pe.wait_ge(keys_ready, t + 1)
                        for g in range(NG):
                            fill(t, 4 + g)
                            if g >= 1:
                                scores(t, g - 1)
                        scores(t, NG - 1)
                    if n < NT:
                        for j in range(idx_base[n], idx_base[n + 1]):
                            h = (j - idx_base[n]) % NIDX
                            lo, hi = chunks[n][(j - idx_base[n]) // NIDX]
                            half = slice((h % 2) * DH1, (h % 2 + 1) * DH1)
                            if j >= 2:
                                pe.wait_ge(relu_ready, j - 1)
                            pe.matmul(idx[j % 2][:, 0:hi - lo], qiT[half, h // 2, n * P:(n + 1) * P],
                                      kiT[half, lo:hi], start=True, stop=True).then_inc(idx_full, 1)
                    if t >= 0:
                        pe.wait_ge(normed, t + 1)
                        for k in range(len(turns), TURNS - 1):
                            fill(t, k)
                        pe.wait_ge(turn_free, (t + 1) * TURNS - 1)
                        if t >= 1:
                            pe.wait_ge(ctx_copied, t)
                        for c in range(2):
                            out = ctxp[:, c * CH:(c + 1) * CH]
                            parts = [1] if t == 0 else [0, 1]
                            for part in parts:
                                pe.matmul(out, rows[:, t - 1 + part, 0:CKV],
                                          probsT[:, part, 4 * c:4 * c + 4, :].rearrange("p g l -> p (g l)"),
                                          start=(part == parts[0]), stop=False, skip_group_check=True)
                            for i in range(16 * c, 16 * c + 16):
                                cols = slice((i % 4) * 32, (i % 4 + 1) * 32)
                                ins = pe.matmul(ctxp[:, i * 32:(i + 1) * 32], far[t % RING][:, i, 0:CKV],
                                                probsT[:, 2, i // 4, cols], start=False, stop=(i % 16 == 15),
                                                skip_group_check=True)
                        ins.then_inc(ctx_full, 1)
                        pe.wait_ge(ctx_copied, t + 1)
                        fill(t, TURNS - 1)


def layer1_attention(nc, dram, x, ident, yT):
    with ExitStack() as ctx:
        sb, _, sem = allocators(nc, ctx)
        keep = {
            "rows": sb("rows", [P, NT, KW], F32),
            "queries": sb("queries", [P, NT, H1, QW], F32),
            "near_keys": sb("near_keys", [KW, P + T], F32),
            "nout": sb("nout", [CKV, H1, D], F32),
            "qiT": sb("qiT", [P, 2, T], F32),
            "kiT": sb("kiT", [P, T], F32),
            "idx_w": sb("idx_w", [P, NIDX], F32),
            "cap0": sb("cap0", [P, KTS], F32),
            "cap": sb("cap", [P, P], F32),
            "mask": sb("mask", [P, 2, NG, SC], F16),
            "cos_far": sb("cos_far", [P, ROPE1], F32),
            "sin_far": sb("sin_far", [P, ROPE1], F32),
            "rows_ready": sem("rows_ready"),
            "table_out": sem("table_out"),
            "table": dram["key_table"],
        }
        projections1(nc, dram, x, ident, yT, keep)
        selected_attention(nc, dram, ident, yT, keep)


TOPK1 = 2
PRIME = 11
HASH_OFF = 7919
CLASS = T // E1
KS = HS // P
CLASS_EXPERTS = [[(r * PRIME + k * HASH_OFF) % E1 for k in range(TOPK1)] for r in range(E1)]


def layer1_experts(nc, dram, x, ident, yT):
    with ExitStack() as ctx:
        sb, ps, sem = allocators(nc, ctx)
        xn = sb("e1_xn", [P, NT, D], F32)
        xnT = sb("e1_xnT", [P, T], F32)
        sw1 = sb("sw1", [P, HS], F32)
        sw3 = sb("sw3", [P, HS], F32)
        sw2 = sb("sw2", [P, KS, D], F32)
        w1 = sb("e1_w1", [P, E1, HR], F32)
        w2 = sb("e1_w2", [HR, E1, D], F32)
        sb13 = sb("sb13", [P, 2, KS], F32)
        sb2 = sb("sb2", [P, 1], F32)
        b1 = sb("e1_b1", [HR, E1], F32)
        b2 = sb("e1_b2", [P, TOPK1, E1], F32)
        b2_sum = sb("e1_b2_sum", [P, E1], F32)
        silu = [sb(f"e1_silu{i}", [P, CH], F32) for i in range(2)]
        hid = [sb(f"e1_hid{i}", [P, CH], F32) for i in range(2)]
        part = [sb(f"e1_part{i}", [P, CLASS], F32) for i in range(2)]
        work = norm_work(sb, "3")
        bank = [ps(f"e1_bank{i}", [P, CH], F32) for i in range(2)]
        up = [ps(f"e1_up{i}", [P, CH], F32) for i in range(2)]
        gate = [ps(f"e1_gate{i}", [P, CH], F32) for i in range(2)]
        down = [ps(f"e1_down{i}", [P, CH], F32) for i in range(2)]
        (w_in, turned, added, var, std, own_sem, normed, xnT_full, xnT_ready, up_full, act_ready, hid_ready, hid_used,
         down_read, y_ready, y_turned, out_ready, out_done) = (
             sem("e1_" + n) for n in (
                 "w_in", "turned", "added", "var", "std", "own", "normed", "xnT_full", "xnT_ready", "up_full",
                 "act_ready", "hid_ready", "hid_used", "down_read", "y_ready", "y_turned", "out_ready",
                 "out_done"))
        loads = [(sw1, "sw1"), (sw3, "sw3"), (sw2, "sw2"), (sb13, "sb13"), (sb2, "sb2"), (w1, "e1_w1"), (w2, "e1_w2"),
                 (b1, "e1_b1"), (b2, "e1_b2")]
        SHARED = NCH * KS
        ROUTED = E1 * TOPK1

        with nc.Block() as block:
            @block.sync
            def _(sp):
                for dst, src in loads:
                    sp.dma_start(dst[:], dram[src]).then_inc(w_in, 16)
                rows = dram["out"].rearrange("(t p) d -> p t d", p=P)
                for c in range(NCH):
                    sp.wait_ge(out_ready, c + 1)
                    sp.dma_start(rows[:, 4 * c:4 * c + 4, :], x[:, 4 * c:4 * c + 4, :]).then_inc(out_done, 16)
                sp.wait_ge(out_done, NCH * 16)

            @block.scalar
            def _(act):
                act.wait_ge(var, 1)
                act.activation(work[3][:], work[2][:], ACT.Sqrt).then_inc(std, 1)
                act.wait_ge(w_in, len(loads) * 16)
                for n in range(SHARED):
                    act.wait_ge(up_full, n + 1)
                    if n >= 2:
                        act.wait_ge(hid_ready, n - 1)
                    act.activation(silu[n % 2][:], up[n % 2][:], ACT.Silu, bias=sb13[:, 0, n % KS:n % KS + 1]
                                   ).then_inc(act_ready, 1)
                for i in range(ROUTED):
                    n = SHARED + i
                    e = CLASS_EXPERTS[i // TOPK1][i % TOPK1]
                    act.wait_ge(up_full, n + 1)
                    act.wait_ge(hid_used, n - 1)
                    act.activation(hid[n % 2][:, 0:CLASS], up[n % 2][:, 0:CLASS], ACT.Gelu, bias=b1[:, e:e + 1]
                                   ).then_inc(act_ready, 1)

            @block.vector
            def _(dve):
                own = Order(dve, own_sem)
                add_transposed(dve, None, x, yT, ident, bank, turned, added)()
                dve.wait_ge(added, NCH)
                layer_norm(dve, own, x, xn, work, var, std, 0)
                dve.wait_ge(w_in, len(loads) * 16)
                dve.tensor_tensor(b2_sum[:], b2[:, 0, :], b2[:, 1, :], ALU.add).then_inc(normed, 1)
                for c in range(NCH):
                    dve.wait_ge(xnT_full, c + 1)
                    dve.tensor_copy(xnT[:, c * CH:(c + 1) * CH], bank[c % 2][:]).then_inc(xnT_ready, 1)

                def shared_out(c):
                    dve.wait_ge(hid_used, (c + 1) * KS)
                    dve.tensor_scalar(yT[:, c * CH:(c + 1) * CH], down[c % 2][:], sb2[:], 0.5, ALU.add, ALU.mult
                                      ).then_inc(down_read, 1)

                for n in range(SHARED):
                    dve.wait_ge(act_ready, n + 1)
                    if n >= 2:
                        dve.wait_ge(hid_used, n - 1)
                    dve.scalar_tensor_tensor(hid[n % 2][:], gate[n % 2][:], sb13[:, 1, n % KS:n % KS + 1],
                                             silu[n % 2][:], ALU.add, ALU.mult).then_inc(hid_ready, 1)
                    if n >= KS and n % KS == 0:
                        shared_out(n // KS - 1)
                shared_out(NCH - 1)
                dve.wait_ge(down_read, NCH)
                for r in range(E1):
                    n = NCH + r
                    dve.wait_ge(hid_used, SHARED + (r + 1) * TOPK1)
                    own.link(dve.tensor_scalar(part[r % 2][:], down[n % 2][:, 0:CLASS], b2_sum[:, r:r + 1],
                                               0.5 / TOPK1, ALU.add, ALU.mult))
                    dve.tensor_tensor(yT[:, r:T:E1], yT[:, r:T:E1], part[r % 2][:], ALU.add).then_inc(down_read, 1)
                add_transposed(dve, None, x, yT, ident, bank, y_turned, out_ready)()

            @block.tensor
            def _(pe):
                add_transposed(None, pe, x, yT, ident, bank, turned, added)()
                pe.wait_ge(normed, 1)
                for c in range(NCH):
                    if c >= 2:
                        pe.wait_ge(xnT_ready, c - 1)
                    for j in range(4):
                        ins = pe.transpose(bank[c % 2][:, j * P:(j + 1) * P], xn[:, 4 * c + j, :], ident[:])
                    ins.then_inc(xnT_full, 1)
                pe.wait_ge(w_in, len(loads) * 16)
                pe.wait_ge(xnT_ready, NCH)

                def rise(n):
                    if n >= 2:
                        pe.wait_ge(act_ready, n - 1)
                    if n < SHARED:
                        if n >= 2:
                            pe.wait_ge(hid_ready, n - 1)
                        c, k = n // KS, n % KS
                        cols, half = slice(c * CH, (c + 1) * CH), slice(k * P, (k + 1) * P)
                        pe.matmul(up[n % 2][:], sw1[:, half], xnT[:, cols], start=True, stop=True)
                        ins = pe.matmul(gate[n % 2][:], sw3[:, half], xnT[:, cols], start=True, stop=True)
                    else:
                        r, k = (n - SHARED) // TOPK1, (n - SHARED) % TOPK1
                        ins = pe.matmul(up[n % 2][:, 0:CLASS], w1[:, CLASS_EXPERTS[r][k], :], xnT[:, r:T:E1],
                                        start=True, stop=True)
                    ins.then_inc(up_full, 1)

                def fall(n):
                    if n < SHARED:
                        out, k, last = n // KS, n % KS, KS - 1
                        pe.wait_ge(hid_ready, n + 1)
                        w, width = sw2[:, k, :], CH
                    else:
                        r, k = (n - SHARED) // TOPK1, (n - SHARED) % TOPK1
                        out, last = NCH + r, TOPK1 - 1
                        pe.wait_ge(act_ready, n + 1)
                        w, width = w2[:, CLASS_EXPERTS[r][k], :], CLASS
                    if k == 0 and out >= 2:
                        pe.wait_ge(down_read, out - 1)
                    ins = pe.matmul(down[out % 2][:, 0:width], w, hid[n % 2][:, 0:width], start=(k == 0),
                                    stop=(k == last))
                    ins.then_inc(hid_used, 1)

                for n in range(SHARED + ROUTED):
                    rise(n)
                    if n:
                        fall(n - 1)
                fall(SHARED + ROUTED - 1)
                pe.wait_ge(down_read, NCH + E1)
                add_transposed(None, pe, x, yT, ident, bank, y_turned, out_ready)()


def build(nc, dram):
    with ExitStack() as ctx:
        sb, _, _ = allocators(nc, ctx)
        x = sb("x", [P, NT, D], F32)
        ident = sb("ident", [P, P], F32)
        yT = sb("yT", [P, T], F32)
        layer0_attention(nc, dram, x, ident)
        layer0_experts(nc, dram, x, ident)
        layer1_attention(nc, dram, x, ident, yT)
        layer1_experts(nc, dram, x, ident, yT)


def tables():
    f32 = np.float32
    t = {"ident": np.eye(P, dtype=f32)}
    inv = 1.0 / 10000.0 ** (np.arange(0, DH0, 2, dtype=f32) / DH0)
    angle = np.outer(np.arange(T, dtype=f32), inv)
    cos = np.concatenate([np.cos(angle), np.cos(angle)], -1)[:, ::2].T.astype(f32)
    sin = np.concatenate([np.sin(angle), np.sin(angle)], -1)[:, ::2].T.astype(f32)
    t["cos0"] = np.ascontiguousarray(np.tile(cos, (4, 1)))
    t["sin0"] = np.ascontiguousarray(np.tile(np.concatenate([-sin, sin], 0), (2, 1)))
    theta = (1.0 / 10000.0 ** (2.0 * np.arange(HALF1, dtype=f32) / f32(ROPE1))).astype(np.float64)
    place = np.arange(T)

    def turn(steps):
        c, s = np.cos(np.outer(steps, theta)), np.sin(np.outer(steps, theta))
        return np.concatenate([c, c], 1).astype(f32), np.concatenate([-s, s], 1).astype(f32)

    for name, steps in (("k", place), ("near", np.where(place < LW, place, 2 * place - LW + 1)), ("q", place)):
        for part, table in zip(("cos_", "sin_"), turn(steps)):
            t[part + name] = table.reshape(NT, P, ROPE1).transpose(1, 0, 2)
    t["cos_far"], t["sin_far"] = (np.tile(v, (4, 1)) for v in turn(LW + np.arange(FAR)))
    l, k = np.arange(P)[:, None], np.arange(P)[None, :]
    t["cap"] = np.where(k <= l, 3.4e38, -3.3e38).astype(f32)
    k = np.arange(KTS)[None, :]
    t["cap0"] = np.where(k <= l - LW, 3.4e38, np.where(k <= l, -3.3e38, -1e36 * (k + 1))).astype(f32)
    row = np.arange(P)
    i4, quarter = row // 32, row % 32 // H1
    l = (32 * quarter + i4)[:, None, None] + 4 * np.arange(NG)[None, :, None]
    s = np.arange(WIN)[None, None, :] - P
    gathered = np.broadcast_to(np.arange(P)[None, None, :] // FAR == quarter[:, None, None], (P, NG, P))
    first = np.where(l < LW, (s >= 0) & (s < KTS), (s > l - LW) & (s <= l))
    rest = (s > l - LW) & (s <= l)
    keep = np.stack([np.concatenate([first, gathered & (l >= LW)], 2), np.concatenate([rest, gathered], 2)], 1)
    t["mask"] = np.where(keep, 0.0, -60000.0).astype(np.float16)
    t["iota"] = np.tile(np.arange(E0, dtype=f32), (P, 1))
    return t


def layouts(a):
    even_odd = np.concatenate([np.arange(0, DH0, 2), np.arange(1, DH0, 2)])
    odd_even = np.concatenate([np.arange(1, DH0, 2), np.arange(0, DH0, 2)])
    twice = lambda w, axis: np.concatenate([w, w], axis)

    def up(w, order):
        w = w.reshape(H0, DH0, LAT0)[:, order, :].transpose(2, 0, 1)
        return twice(twice(w, 2).reshape(LAT0, H0 * P), 0)

    m = {
        "x": a["L0_attn_x"].reshape(T, D),
        "ln_scale": a["L0_attn_ln_scale"].reshape(D, 1),
        "ln_bias": a["L0_attn_ln_bias"].reshape(D, 1),
        "wdq": twice(a["L0_attn_w_down_q"].T, 1),
        "wdkv": twice(a["L0_attn_w_down_kv"].T, 1),
        "wq": up(a["L0_attn_w_up_q"], even_odd),
        "wq_sw": up(a["L0_attn_w_up_q"], odd_even),
        "wk": up(a["L0_attn_w_up_k"], even_odd),
        "wk_sw": up(a["L0_attn_w_up_k"], odd_even),
        "wv": twice(a["L0_attn_w_up_v"].T, 0),
        "wg": a["L0_ffn_Wg"].T,
        "e0_w1": a["L0_ffn_W1"].transpose(0, 2, 1),
        "e0_w3": a["L0_ffn_W3"].transpose(0, 2, 1),
        "e0_w2": a["L0_ffn_W2"].transpose(0, 2, 1),
        "e0_b13": np.stack([a["L0_ffn_b1"], a["L0_ffn_b3"]], 2),
        "e0_b2": a["L0_ffn_b2"],
        "wkvr": np.concatenate([a["L1_attn_W_dkv"], a["L1_attn_W_kr"]], 1),
        "a1_wdq": a["L1_attn_W_dq"],
        "wuq": a["L1_attn_W_uq"].reshape(CQ, H1, DH1).transpose(2, 1, 0),
        "wuk": a["L1_attn_W_uk"].reshape(CKV, H1, DH1).transpose(2, 1, 0),
        "wuv": a["L1_attn_W_uv"].reshape(CKV, H1, DH1).transpose(2, 1, 0),
        "wqr": a["L1_attn_W_qr"],
        "a1_wo": a["L1_attn_W_out"].reshape(H1, DH1, D).transpose(1, 0, 2),
        "widxq": a["L1_attn_idx_wq"],
        "widxk": twice(a["L1_attn_idx_wk"], 1),
        "idx_w": np.tile(a["L1_attn_idx_w"], (P, 1)),
        "sw1": a["L1_ffn_sw1"],
        "sw3": a["L1_ffn_sw3"],
        "sw2": a["L1_ffn_sw2"].reshape(KS, P, D).transpose(1, 0, 2),
        "sb13": np.stack([a["L1_ffn_sb1"].reshape(KS, P).T, a["L1_ffn_sb3"].reshape(KS, P).T], 1),
        "sb2": a["L1_ffn_sb2"].reshape(D, 1),
        "e1_w1": a["L1_ffn_w1"].transpose(1, 0, 2),
        "e1_b1": a["L1_ffn_b1"].T,
        "e1_w2": a["L1_ffn_w2"].transpose(1, 0, 2),
        "e1_b2": a["L1_ffn_b2"][CLASS_EXPERTS].transpose(2, 1, 0),
        "w_out": a["L0_attn_w_out"].reshape(D, H0 // 2, P).transpose(2, 1, 0).reshape(P, H0 // 2 * D),
    }
    return m


def kernel(**inputs):
    import concourse.bacc as bacc
    from concourse.bass_utils import run_bass_kernel_spmd as run

    nc = bacc.Bacc("TRN2", target_bir_lowering=False, num_devices=1)
    arrays, dram = {}, {}
    host = layouts({k: np.asarray(v) for k, v in inputs.items()})
    host.update(tables())
    for name, a in host.items():
        a = np.ascontiguousarray(a)
        arrays["in_" + name] = a
        dram[name] = nc.dram_tensor("in_" + name, a.shape, mybir.dt.from_np(a.dtype), kind="ExternalInput").ap()
    dram["out"] = nc.dram_tensor("out_0", (T, D), F32, kind="ExternalOutput").ap()
    dram["key_table"] = nc.dram_tensor("key_table", (T, KW), F32, kind="Internal").ap()
    build(nc, dram)
    r = run(nc, [arrays], core_ids=[0])
    return r.results[0]["out_0"].reshape(1, T, D)
```

```python
from contextlib import ExitStack

import numpy as np

import concourse.bass as bass
from concourse import mybir

F32 = mybir.dt.float32
F16 = mybir.dt.float16
BF16 = mybir.dt.bfloat16
U16 = mybir.dt.uint16
U32 = mybir.dt.uint32
ALU = mybir.AluOpType
ACT = mybir.ActivationFunctionType
AX = mybir.AxisListType

P = 128
T = 2048
NT = T // P
D = 128
CH = 512
NCH = T // CH
LN_EPS = 1e-5

H0 = 16
DH0 = 64
LAT0 = 64
E0 = 16
TOPK0 = 4
GROUPS0 = 4
TOPG0 = 2
ROUTE_SCALE = 2.5
H1 = 8
DH1 = 64
CKV = 32
CQ = 64
ROPE1 = 32
HALF1 = ROPE1 // 2
NIDX = 4
KTS = 96
LW = 64
FAR = KTS - LW
SCALE1 = float((DH1 + ROPE1) ** -0.5)
E1 = 8
HS = 256
HR = 128


class Order:

    def __init__(self, eng, sem):
        self.eng, self.sem, self.n = eng, sem, 0

    def mark(self, ins):
        ins.then_inc(self.sem, 1)
        self.n += 1

    def wait(self):
        self.eng.wait_ge(self.sem, self.n)

    def link(self, ins):
        self.mark(ins)
        self.wait()


def inverse_root(dve, own, work, var_ready, std_ready, k):
    stats, mv, var, std, rec, t, rstd = work
    dve.wait_ge(std_ready, k + 1)
    own.link(dve.reciprocal(rec[:], std[:]))
    own.link(dve.tensor_tensor(t[:], rec[:], rec[:], ALU.mult))
    own.link(dve.tensor_tensor(t[:], t[:], var[:], ALU.mult))
    own.link(dve.tensor_scalar(t[:], t[:], -0.5, 1.5, ALU.mult, ALU.add))
    own.link(dve.tensor_tensor(rstd[:], rec[:], t[:], ALU.mult))


def layer_norm(dve, own, src, dst, work, var_ready, std_ready, k, normed=None):
    stats, mv, var, std, rec, t, rstd = work
    for i in range(NT):
        own.mark(dve.bn_stats(stats[:, i, :], src[:, i, :]))
    own.wait()
    for i in range(NT):
        own.mark(dve.bn_aggr(mv[:, i, :], stats[:, i, :]))
    own.wait()
    dve.tensor_scalar(var[:], mv[:, :, 1], LN_EPS, None, ALU.add).then_inc(var_ready, 1)
    inverse_root(dve, own, work, var_ready, std_ready, k)
    for i in range(NT):
        ins = dve.tensor_scalar(dst[:, i, :], src[:, i, :], mv[:, i, 0:1], rstd[:, i:i + 1], ALU.subtract, ALU.mult)
        if normed is None:
            own.mark(ins)
        elif i % 4 == 3:
            ins.then_inc(normed, 1)
    if normed is None:
        own.wait()


def norm_work(sb, tag):
    return (sb(f"stats{tag}", [P, NT, 6], F32), sb(f"mv{tag}", [P, NT, 2], F32),
            *(sb(f"{n}{tag}", [P, NT], F32) for n in ("var", "std", "rec", "newton", "rstd")))


def allocators(nc, ctx):
    return (lambda n, s, d: ctx.enter_context(nc.sbuf_tensor(n, s, d)),
            lambda n, s, d: ctx.enter_context(nc.psum_tensor(n, s, d)),
            lambda n: ctx.enter_context(nc.semaphore(n)))


def latents(nc, dram, x, ident, keep):
    with ExitStack() as ctx:
        sb, ps, sem = allocators(nc, ctx)
        xa = sb("xa", [P, NT, D], F32)
        xh = sb("xh", [P, NT, D], F32)
        hT = sb("hT", [P, T], F32)
        scale = sb("ln_scale", [P, 1], F32)
        bias = sb("ln_bias", [P, 1], F32)
        wdq = sb("wdq", [P, P], F32)
        wdkv = sb("wdkv", [P, P], F32)
        stage = [sb(f"w_stage{i}", [P, H0 * P], F32) for i in range(2)]
        work = norm_work(sb, "0")
        bank = [ps(f"lat_bank{i}", [P, CH], F32) for i in range(2)]
        x_in, small_in = sem("x_in"), sem("small_in")
        w_in = [sem(f"w_in{i}") for i in range(2)]
        w_high, w_split, rope_in = sem("w_high"), sem("w_split"), keep["rope_in"]
        var0, std0, own_sem = sem("var0"), sem("std0"), sem("dve_own0")
        xh_ready, hT_bank, hT_ready, lat_bank, lat_ready = (
            sem(n) for n in ("xh_ready", "hT_bank", "hT_ready", "lat_bank_full", "lat_ready"))
        weights = ["wq", "wq_sw", "wk", "wk_sw", "wv"]

        with nc.Block() as block:
            @block.sync
            def _(sp):
                sp.dma_start(x[:], dram["x"].rearrange("(t p) d -> p t d", p=P)).then_inc(x_in, 16)
                for dst, src in ((ident, "ident"), (scale, "ln_scale"), (bias, "ln_bias"), (wdq, "wdq"),
                                 (wdkv, "wdkv")):
                    sp.dma_start(dst[:], dram[src]).then_inc(small_in, 16)
                for i, w in enumerate(weights):
                    if i >= 2:
                        sp.wait_ge(w_split, i - 1)
                    sp.dma_start(stage[i % 2][:, 0:keep[w].shape[1]], dram[w]).then_inc(w_in[i % 2], 16)
                sp.dma_start(keep["cos"][:], dram["cos0"]).then_inc(rope_in, 16)
                sp.dma_start(keep["sin"][:], dram["sin0"]).then_inc(rope_in, 16)
                sp.dma_start(keep["w_out"][:], dram["w_out"]).then_inc(keep["head_w_in"], 16)

            @block.scalar
            def _(act):
                def high_half(i):
                    w = keep[weights[i]]
                    act.wait_ge(w_in[i % 2], 16 * (i // 2 + 1))
                    act.activation(w[:], stage[i % 2][:, 0:w.shape[1]], ACT.Copy).then_inc(w_high, 1)

                high_half(0)
                high_half(1)
                for k in range(2):
                    act.wait_ge(var0, k + 1)
                    act.activation(work[3][:], work[2][:], ACT.Sqrt).then_inc(std0, 1)
                for i in range(2, len(weights)):
                    high_half(i)

            @block.vector
            def _(dve):
                own = Order(dve, own_sem)
                for m in range(2):
                    dve.memset(keep["k_b"][m][LAT0:LAT0 + 2, :], 1.0)
                    dve.memset(keep["v"][m][:, :, DH0:DH0 + 1], 1.0)
                dve.wait_ge(x_in, 16)
                layer_norm(dve, own, x, xa, work, var0, std0, 0)
                _, mv, var, _, _, t, rstd = work
                own.link(dve.tensor_tensor(t[:], mv[:, :, 1], rstd[:], ALU.mult))
                own.link(dve.tensor_tensor(t[:], t[:], rstd[:], ALU.mult))
                dve.tensor_scalar(var[:], t[:], LN_EPS, None, ALU.add).then_inc(var0, 1)
                inverse_root(dve, own, work, var0, std0, 1)
                for c in range(NCH):
                    for i in range(4 * c, 4 * c + 4):
                        ins = dve.tensor_scalar(xh[:, i, :], xa[:, i, :], rstd[:, i:i + 1], None, ALU.mult)
                    ins.then_inc(xh_ready, 1)
                dve.wait_ge(small_in, 5 * 16)
                for c in range(NCH):
                    dve.wait_ge(hT_bank, c + 1)
                    dve.tensor_scalar(hT[:, c * CH:(c + 1) * CH], bank[c % 2][:], scale[:], bias[:], ALU.mult,
                                      ALU.add).then_inc(hT_ready, 1)
                for i in range(2 * NCH):
                    c, kv = i % NCH, i // NCH
                    hi, lo = (keep["ck1"], keep["ck2"]) if kv else (keep["cq1"], keep["cq2"])
                    cols = slice(c * CH, (c + 1) * CH)
                    dve.wait_ge(lat_bank, i + 1)
                    own.link(dve.tensor_copy(hi[:, cols], bank[i % 2][:]))
                    dve.tensor_tensor(lo[:, cols], bank[i % 2][:], hi[:, cols], ALU.subtract).then_inc(lat_ready, 1)

            @block.gpsimd
            def _(pool):
                for i, w in enumerate(weights):
                    cols = slice(0, keep[w].shape[1])
                    pool.wait_ge(w_high, i + 1)
                    pool.tensor_tensor(keep[w][LAT0:P, :], stage[i % 2][LAT0:P, cols], keep[w][LAT0:P, :],
                                       ALU.subtract).then_inc(w_split, 1)
                pool.wait_ge(xh_ready, 1)
                pool.wait_ge(w_split, len(weights))
                pool.tensor_tensor(x[:], x[:], xa[:], ALU.add)

            @block.tensor
            def _(pe):
                pe.wait_ge(small_in, 5 * 16)
                for c in range(NCH):
                    if c >= 2:
                        pe.wait_ge(hT_ready, c - 1)
                    pe.wait_ge(xh_ready, c + 1)
                    for j in range(4):
                        ins = pe.transpose(bank[c % 2][:, j * P:(j + 1) * P], xh[:, 4 * c + j, :], ident[:])
                    ins.then_inc(hT_bank, 1)
                pe.wait_ge(hT_ready, NCH)
                for i in range(2 * NCH):
                    c, kv = i % NCH, i // NCH
                    if i >= 2:
                        pe.wait_ge(lat_ready, i - 1)
                    pe.matmul(bank[i % 2][:], (wdkv if kv else wdq)[:], hT[:, c * CH:(c + 1) * CH], start=True,
                              stop=True).then_inc(lat_bank, 1)


KT0 = T // P
KPAIR = KT0 // 2
STEPS = NCH * KPAIR
QT = CH // P
VW = 2 * DH0 + 1
LAG = 3
SLOTS = 4
AUX = 4
VECTOR_LOW = list(range(2 * NCH + 2))
POOL_LOW = [st for st in range(STEPS) if st not in VECTOR_LOW]


def aux_prepare():
    plan = []
    for j in range(2 * NCH):
        plan += [(j, "rope", (j, 0)), (j, "rope", (j, 1))]
    plan += [(2 * NCH, "v", 0), (2 * NCH, "v", 1)]
    plan += [(2 * NCH + 1 + n * 18 // (NT * NCH), "max", (n // NCH, n % NCH)) for n in range(NT * NCH)]
    plan += [(2 * NCH + 20, "shift", 0), (2 * NCH + 20, "shift", 1)]
    return plan


def aux_first():
    order = [("rope", (j, i)) for j in range(NCH + 1) for i in range(2)]
    for c in range(NCH):
        if c + 1 < NCH:
            order += [("rope", (NCH + 1 + c, 0)), ("rope", (NCH + 1 + c, 1))]
        order += [("max", (t, c)) for t in range(NT)]
    return order + [("v", 0), ("v", 1), ("shift", 0), ("shift", 1)]


def aux_finish(m, quarter, step):
    plan = [(step + 2, "norm", quarter)]
    return plan + ([(step + 4, "turn", quarter), (step + 5, "out", quarter)] if m else [])


def aux_plan(m, first, last):
    plan = [] if first else aux_finish(1 - m, NCH - 1, LAG - 1)
    for quarter in range(NCH - 1):
        plan += aux_finish(m, quarter, (quarter + 1) * KPAIR + LAG - 1)
    plan += [(st + 1, "low", st) for st in VECTOR_LOW]
    plan += [] if last else aux_prepare()
    return sorted(plan, key=lambda u: u[0])


def banked(plan):
    return [(kind, arg) for _, kind, arg in plan if kind not in ("low", "norm")]


PRO = len(aux_prepare())
BODY = [len(banked(aux_plan(m, False, False))) for m in range(2)]
FIRST = len(banked(aux_plan(0, True, False)))


def aux_base(h, m):
    if isinstance(h, int) and h == 0:
        return PRO
    return PRO + FIRST + (0 if m else BODY[1]) + (h - (1 if m else 2)) * (sum(BODY) // 2)


def aux_slot(h, m, u):
    first = aux_base(0, 0) if isinstance(h, int) and h == 0 else aux_base(2 - m, m)
    return (first + u) % AUX


def heads(nc, dram, x, keep):
    with ExitStack() as ctx:
        sb, ps, sem = allocators(nc, ctx)
        qa = [sb(f"q_a{i}", [P, T], F16) for i in range(2)]
        qb = [sb(f"q_b{i}", [LAT0 + 2, T], F16) for i in range(2)]
        ka = [sb(f"k_a{i}", [P, T], F16) for i in range(2)]
        kb = keep["k_b"]
        v = keep["v"]
        probs = sb("probs", [P, SLOTS, 2, CH], F32)
        probs_hi = sb("probs_hi", [P, SLOTS, 2, CH], F16)
        probs_lo = sb("probs_lo", [P, SLOTS, 2, CH], F16)
        term = [[sb(f"rope_term{i}{j}", [P, CH], F32) for j in range(2)] for i in range(2)]
        roped = [sb(f"roped{i}", [P, CH], F32) for i in range(2)]
        part_max = sb("part_max", [P, NT, NCH], F32)
        row_max = sb("row_max", [P, NT], F32)
        shift16 = sb("shift16", [P, NT], F16)
        shift = sb("shift", [P, 2, NT], F32)
        shift_row = sb("shift_row", [NT, 2, P], F16)
        unnorm = [sb(f"unnorm{i}", [P, 2, QT // 2 * VW], F32) for i in range(2)]
        inv = sb("inv", [P, QT], F32)
        summed = sb("summed", [P, QT, DH0], F32)
        heads_out = sb("heads_out", [P, NT, 2, DH0], F32)
        headsT = sb("headsT", [P, CH], F32)
        scores = [ps(f"scores{i}", [P, CH], F32) for i in range(2)]
        acc = ps("acc", [P, 2, CH], F32)
        aux = ps("aux", [P, AUX, CH], F32)
        (aux_full, aux_free, rope_sum, hi_ready, lo_ready, shift_ready, shift_in, scores_ready, probs_ready,
         pool_low, vector_low, probs_used, acc_copied, norm_own, norm_ready, dve_own, v_own) = (
            sem(n) for n in ("aux_full", "aux_free", "rope_sum", "hi_ready", "lo_ready", "shift_ready", "shift_in",
                             "scores_ready", "probs_ready", "pool_low", "vector_low", "probs_used", "acc_copied",
                             "norm_own", "norm_ready", "dve_own1", "v_own"))
        ident = keep["ident"]
        prepare = aux_first()
        known = lambda n, below: isinstance(n, int) and n < below

        def prepared_in(hp, mp, kind, arg):
            if known(hp, 1):
                return prepare.index((kind, arg)) + 1
            plan = aux_plan(1 - mp, known(hp, 2), False)
            return aux_base(hp - 1, 1 - mp) + banked(plan).index((kind, arg)) + 1

        def every_head(eng, body):
            body(0, 0, True, False)
            body(1, 1, False, False)
            with eng.Fori(1, H0 // 2 - 1) as pair:
                body(pair * 2, 0, False, False)
                body(pair * 2 + 1, 1, False, False)
            body(H0 - 2, 0, False, False)
            body(H0 - 1, 1, False, True)

        def low_half(eng, h, st):
            n, slot = h * STEPS + st, st % SLOTS
            eng.wait_ge(probs_ready, 2 * n + 2)
            if not known(n, SLOTS):
                eng.wait_ge(probs_used, n - SLOTS + 1)
            return eng.tensor_tensor(probs_lo[:, slot], probs[:, slot], probs_hi[:, slot], ALU.subtract)

        with nc.Block() as block:
            @block.sync
            def _(sp):
                def send_shift(hp, mp):
                    sp.wait_ge(aux_free, prepared_in(hp, mp, "shift", 1))
                    for i in range(2):
                        sp.dma_start(qb[mp][LAT0 + i:LAT0 + i + 1, :].rearrange("a (t p) -> a t p", p=P),
                                     shift_row[:, i, :]).then_inc(shift_in, 16)

                def body(h, m, first, last):
                    if not last:
                        send_shift(h + 1, 1 - m)

                send_shift(0, 0)
                every_head(sp, body)

            @block.gpsimd
            def _(pool):
                def rope_add(hp, mp, j):
                    n = hp * (2 * NCH) + j
                    pool.wait_ge(aux_free, prepared_in(hp, mp, "rope", (j, 1)))
                    if not known(n, 2):
                        pool.wait_ge(lo_ready, n - 1)
                    pool.tensor_tensor(roped[j % 2][:], term[j % 2][0][:], term[j % 2][1][:], ALU.add
                                       ).then_inc(rope_sum, 1)

                def rope_low(hp, mp, j):
                    n = hp * (2 * NCH) + j
                    cols = slice((j % NCH) * CH, (j % NCH + 1) * CH)
                    pool.wait_ge(hi_ready, n + 1)
                    rows, dst = (slice(0, LAT0), qb[mp]) if j < NCH else (slice(LAT0, P), ka[mp])
                    hi = qa[mp] if j < NCH else ka[mp]
                    pool.tensor_tensor(dst[rows, cols], roped[j % 2][rows, :], hi[rows, cols], ALU.subtract
                                       ).then_inc(lo_ready, 1)

                for j in range(2 * NCH):
                    if j:
                        pool.wait_ge(lo_ready, j)
                    rope_add(0, 0, j)
                    rope_low(0, 0, j)
                pool.wait_ge(lo_ready, 2 * NCH)

                def body(h, m, first, last):
                    for st in range(STEPS):
                        if st in POOL_LOW:
                            low_half(pool, h, st).then_inc(pool_low, 1)
                        if not last and 2 <= st < 2 * NCH + 2:
                            pool.wait_ge(rope_sum, (h + 1) * (2 * NCH) + min(st, 2 * NCH))
                            rope_low(h + 1, 1 - m, st - 2)
                            pool.wait_ge(lo_ready, (h + 1) * (2 * NCH) + st - 1)
                        if not last and st < 2 * NCH:
                            rope_add(h + 1, 1 - m, st)

                every_head(pool, body)

            @block.scalar
            def _(act):
                def high_halves(hp, mp, j):
                    n = hp * (2 * NCH) + j
                    cols = slice((j % NCH) * CH, (j % NCH + 1) * CH)
                    act.wait_ge(rope_sum, n + 1)
                    if j < NCH:
                        act.activation(qa[mp][:, cols], roped[j % 2][:], ACT.Copy).then_inc(hi_ready, 1)
                    else:
                        act.activation(kb[mp][0:LAT0, cols], roped[j % 2][0:LAT0, :], ACT.Copy)
                        act.activation(ka[mp][:, cols], roped[j % 2][:], ACT.Copy).then_inc(hi_ready, 1)

                def copy_acc(q, slot):
                    act.wait_ge(probs_used, (q + 1) * KPAIR)
                    if not known(q, 2):
                        act.wait_ge(norm_ready, q - 1)
                    act.activation(unnorm[slot][:], acc[:, :, 0:QT // 2 * VW], ACT.Copy).then_inc(acc_copied, 1)

                for j in range(2 * NCH):
                    high_halves(0, 0, j)

                def body(h, m, first, last):
                    for st in range(STEPS):
                        n = h * STEPS + st
                        if not known(n, SLOTS):
                            act.wait_ge(probs_used, n - SLOTS + 1)
                        for i in range(2):
                            act.wait_ge(scores_ready, 2 * n + i + 1)
                            for dst in (probs, probs_hi):
                                ins = act.activation(dst[:, st % SLOTS, i], scores[i][:], ACT.Exp,
                                                     scale=float(DH0) ** -0.5)
                            ins.then_inc(probs_ready, 1)
                        if not last and 1 <= st < 2 * NCH + 1:
                            high_halves(h + 1, 1 - m, st - 1)
                        if st % KPAIR == LAG - 1 and not (first and st < KPAIR):
                            copy_acc(h * NCH - 1 + st // KPAIR, (st // KPAIR - 1) % 2)

                every_head(act, body)
                copy_acc(H0 * NCH - 1, 1)

            @block.vector
            def _(dve):
                def empty(u, slot, kind, arg, hp, mp, h):
                    bank = aux[:, slot, :]
                    dve.wait_ge(aux_full, u + 1)
                    if kind == "rope":
                        j, part = arg
                        cols = slice((j % NCH) * CH, (j % NCH + 1) * CH)
                        if not (known(hp, 1) and j < 2):
                            dve.wait_ge(rope_sum, hp * (2 * NCH) + j - 1)
                        table = keep["sin"] if part else keep["cos"]
                        dve.tensor_tensor(term[j % 2][part][:], bank, table[:, cols], ALU.mult).then_inc(aux_free, 1)
                    elif kind == "v":
                        if not known(hp, 2):
                            dve.wait_ge(probs_used, (hp - 1) * STEPS)
                        tiles = slice(8 * arg, 8 * arg + 8)
                        rows = bank.rearrange("p (t d) -> p t d", d=DH0)
                        dve.tensor_copy(v[mp][:, tiles, 0:DH0], rows).then_inc(v_own, 1)
                        dve.wait_ge(v_own, hp * 2 + arg + 1)
                        dve.tensor_tensor(v[mp][:, tiles, DH0 + 1:], rows, v[mp][:, tiles, 0:DH0], ALU.subtract
                                          ).then_inc(aux_free, 1)
                    elif kind == "max":
                        t, c = arg
                        dve.tensor_reduce(part_max[:, t, c:c + 1], bank, AX.X, ALU.max).then_inc(aux_free, 1)
                    elif kind == "shift":
                        if not known(hp, 1):
                            dve.wait_ge(shift_in, hp * 32)
                        dve.tensor_copy(shift_row[:, arg, :], bank[0:NT, 0:P]).then_inc(aux_free, 1)
                    elif kind == "turn":
                        dve.tensor_copy(headsT[:], bank).then_inc(aux_free, 1)
                    elif kind == "out":
                        rows = x[:, QT * arg:QT * arg + QT, :].rearrange("p t d -> p (t d)")
                        dve.tensor_tensor(rows, rows, bank, ALU.add).then_inc(aux_free, 1)

                def normalise(q, slot, quarter, m):
                    own = Order(dve, norm_own)
                    own.n = q * 2
                    sums = unnorm[slot][:].rearrange("p b (t c) -> p (b t) c", c=VW)
                    dve.wait_ge(acc_copied, q + 1)
                    own.mark(dve.reciprocal(inv[:].unsqueeze(2), sums[:, :, DH0:DH0 + 1]))
                    own.link(dve.tensor_tensor(summed[:], sums[:, :, 0:DH0], sums[:, :, DH0 + 1:], ALU.add))
                    dve.tensor_tensor(heads_out[:, QT * quarter:QT * quarter + QT, m, :], summed[:],
                                      inv[:].unsqueeze(2).broadcast_to([P, QT, DH0]), ALU.mult
                                      ).then_inc(norm_ready, 1)

                def row_maxima(hp, mp):
                    dve.wait_ge(aux_free, prepared_in(hp, mp, "max", (NT - 1, NCH - 1)))
                    step = hp * 3
                    dve.tensor_reduce(row_max[:], part_max[:], AX.X, ALU.max).then_inc(dve_own, 1)
                    dve.wait_ge(dve_own, step + 1)
                    dve.tensor_scalar(shift16[:], row_max[:], -1.0, None, ALU.mult).then_inc(dve_own, 1)
                    dve.wait_ge(dve_own, step + 2)
                    dve.tensor_copy(shift[:, 0, :], shift16[:]).then_inc(dve_own, 1)
                    dve.wait_ge(dve_own, step + 3)
                    dve.scalar_tensor_tensor(shift[:, 1, :], row_max[:], -1.0, shift[:, 0, :], ALU.mult,
                                             ALU.subtract).then_inc(shift_ready, 1)

                dve.wait_ge(keep["rope_in"], 2 * 16)
                for u, (kind, arg) in enumerate(prepare):
                    if kind == "shift" and arg == 0:
                        row_maxima(0, 0)
                    empty(u, u % AUX, kind, arg, 0, 0, None)

                def body(h, m, first, last):
                    base, u = aux_base(h, m), 0
                    for _, kind, arg in aux_plan(m, first, last):
                        if kind == "low":
                            low_half(dve, h, arg).then_inc(vector_low, 1)
                        elif kind == "norm":
                            old = arg == NCH - 1
                            normalise(h * NCH - 1 if old else h * NCH + arg, arg % 2, arg, 1 - m if old else m)
                        else:
                            if kind == "shift" and arg == 0:
                                row_maxima(h + 1, 1 - m)
                            empty(base + u, aux_slot(h, m, u), kind, arg, h + 1, 1 - m, h)
                            u += 1

                every_head(dve, body)
                normalise(H0 * NCH - 1, 1, NCH - 1, 1)
                base, done = aux_base(H0 - 1, 1), len(banked(aux_plan(1, False, True)))
                for u, kind in enumerate(("turn", "out"), done):
                    empty(base + u, aux_slot(H0 - 1, 1, u), kind, NCH - 1, None, None, H0 - 1)

            @block.tensor
            def _(pe):
                def fill(u, slot, kind, arg, hp, mp, h):
                    bank = aux[:, slot, :]
                    if not known(u, AUX):
                        pe.wait_ge(aux_free, u - AUX + 1)
                    if kind == "rope":
                        j, part = arg
                        q = j < NCH
                        w = keep[("wq", "wq_sw", "wk", "wk_sw")[2 * (not q) + part]]
                        hi, lo = (keep["cq1"], keep["cq2"]) if q else (keep["ck1"], keep["ck2"])
                        cols = slice((j % NCH) * CH, (j % NCH + 1) * CH)
                        w = w[:, bass.ds(hp * P, P)]
                        pe.matmul(bank, w, hi[:, cols], start=True, stop=False)
                        ins = pe.matmul(bank, w, lo[:, cols], start=False, stop=True)
                    elif kind == "v":
                        for t in range(8):
                            tok = (8 * arg + t) * P
                            w, out = keep["wv"][:, bass.ds(hp * DH0, DH0)], bank[:, t * DH0:(t + 1) * DH0]
                            pe.matmul(out, keep["ck1"][:, tok:tok + P], w, start=True, stop=False)
                            ins = pe.matmul(out, keep["ck2"][:, tok:tok + P], w, start=False, stop=True)
                    elif kind == "max":
                        t, c = arg
                        if t == 0 and known(hp, 1):
                            pe.wait_ge(hi_ready, NCH + 1 + c)
                        elif t == 0 and c == 0:
                            pe.wait_ge(hi_ready, (hp + 1) * (2 * NCH))
                        ins = pe.matmul(bank, qa[mp][0:LAT0, t * P:(t + 1) * P], ka[mp][0:LAT0, c * CH:(c + 1) * CH],
                                        start=True, stop=True)
                    elif kind == "shift":
                        pe.wait_ge(shift_ready, hp + 1)
                        ins = pe.transpose(bank[0:NT, 0:P], shift[:, arg, :], ident[:])
                    elif kind == "turn":
                        pe.wait_ge(norm_ready, h * NCH + arg + 1)
                        for i in range(QT):
                            ins = pe.transpose(bank[:, i * P:(i + 1) * P],
                                               heads_out[:, QT * arg + i, :, :].rearrange("p a d -> p (a d)"), ident[:])
                    elif kind == "out":
                        pe.wait_ge(aux_free, u)
                        for i in range(QT):
                            ins = pe.matmul(bank[:, i * P:(i + 1) * P], headsT[:, i * P:(i + 1) * P],
                                            keep["w_out"][:, bass.ds((h - 1) * (D // 2), D)], start=True, stop=True)
                    ins.then_inc(aux_full, 1)

                def score(h, m, st, i):
                    quarter, pair = st // KPAIR, st % KPAIR
                    n = h * STEPS + st
                    if st == 0 and i == 0:
                        pe.wait_ge(lo_ready, (h + 1) * (2 * NCH))
                        pe.wait_ge(shift_in, (h + 1) * 32)
                    if not known(n, 1):
                        pe.wait_ge(probs_ready, 2 * n + i - 1)
                    cols = slice(quarter * CH, (quarter + 1) * CH)
                    keys = slice((2 * pair + i) * P, (2 * pair + i + 1) * P)
                    out = scores[i][:]
                    pe.matmul(out, ka[m][:, keys], qa[m][:, cols], start=True, stop=False)
                    ins = pe.matmul(out, kb[m][:, keys], qb[m][:, cols], start=False, stop=True)
                    ins.then_inc(scores_ready, 1)

                def weigh(h, m, st, i):
                    quarter, pair = st // KPAIR, st % KPAIR
                    if st == 0 and i == 0:
                        pe.wait_ge(aux_free, prepared_in(h, m, "v", 1))
                    if pair == 0 and i == 0 and not known(h * NCH + quarter, 1):
                        pe.wait_ge(acc_copied, h * NCH + quarter)
                    if i == 0 and st in POOL_LOW:
                        pe.wait_ge(pool_low, h * len(POOL_LOW) + POOL_LOW.index(st) + 1)
                    elif i == 0:
                        pe.wait_ge(vector_low, h * len(VECTOR_LOW) + VECTOR_LOW.index(st) + 1)
                    kt = 2 * pair + i
                    for t in range(QT):
                        queries = slice(t * P, (t + 1) * P)
                        out = acc[:, t // 2, (t % 2) * VW:(t % 2 + 1) * VW]
                        pe.matmul(out, probs_hi[:, st % SLOTS, i, queries], v[m][:, kt, :],
                                  start=(kt == 0 and t % 2 == 0), stop=False, skip_group_check=True)
                        ins = pe.matmul(out[:, 0:DH0 + 1], probs_lo[:, st % SLOTS, i, queries],
                                        v[m][:, kt, 0:DH0 + 1], start=False, stop=(kt == KT0 - 1),
                                        skip_group_check=True)
                    if i:
                        ins.then_inc(probs_used, 1)

                pe.wait_ge(keep["head_w_in"], 16)
                for u, (kind, arg) in enumerate(prepare):
                    fill(u, u % AUX, kind, arg, 0, 0, None)

                def body(h, m, first, last):
                    base, u = aux_base(h, m), 0
                    plan = aux_plan(m, first, last)
                    for st in range(STEPS):
                        now = [(kind, arg) for kind, arg in banked([w for w in plan if w[0] == st])]
                        for part in range(4):
                            if part < 2:
                                score(h, m, st, part)
                            elif st >= LAG:
                                weigh(h, m, st - LAG, part - 2)
                            elif not first:
                                weigh(h - 1, 1 - m, STEPS + st - LAG, part - 2)
                            for kind, arg in now[part * len(now) // 4:(part + 1) * len(now) // 4]:
                                old = kind in ("turn", "out") and arg == NCH - 1
                                fill(base + u, aux_slot(h, m, u), kind, arg, h + 1, 1 - m, h - 1 if old else h)
                                u += 1

                every_head(pe, body)
                for st in range(STEPS - LAG, STEPS):
                    for i in range(2):
                        weigh(H0 - 1, 1, st, i)
                base, done = aux_base(H0 - 1, 1), len(banked(aux_plan(1, False, True)))
                for u, kind in enumerate(("turn", "out"), done):
                    fill(base + u, aux_slot(H0 - 1, 1, u), kind, NCH - 1, None, None, H0 - 1)


def layer0_attention(nc, dram, x, ident):
    with ExitStack() as ctx:
        sb, _, sem = allocators(nc, ctx)
        keep = {"ident": ident}
        for n in ("cos", "sin"):
            keep[n] = sb(n, [P, T], F32)
        for n in ("wq", "wq_sw", "wk", "wk_sw"):
            keep[n] = sb(n, [P, H0 * P], F16)
        for n in ("cq1", "cq2", "ck1", "ck2"):
            keep[n] = sb(n, [P, T], F16)
        keep["wv"] = sb("wv", [P, H0 * DH0], F16)
        keep["w_out"] = sb("w_out", [P, H0 // 2 * D], F32)
        keep["k_b"] = [sb(f"k_b{i}", [LAT0 + 2, T], F16) for i in range(2)]
        keep["v"] = [sb(f"v{i}", [P, KT0, VW], F16) for i in range(2)]
        for n in ("rope_in", "head_w_in"):
            keep[n] = sem(n)
        latents(nc, dram, x, ident, keep)
        heads(nc, dram, x, keep)


def add_transposed(dve, pe, x, yT, ident, bank, turned, added):
    def turn():
        for c in range(NCH):
            if c >= 2:
                pe.wait_ge(added, c - 1)
            for j in range(4):
                t = 4 * c + j
                ins = pe.transpose(bank[c % 2][:, j * P:(j + 1) * P], yT[:, t * P:(t + 1) * P], ident[:])
            ins.then_inc(turned, 1)

    def add():
        for c in range(NCH):
            dve.wait_ge(turned, c + 1)
            rows = x[:, 4 * c:4 * c + 4, :].rearrange("p t d -> p (t d)")
            dve.tensor_tensor(rows, rows, bank[c % 2][:], ALU.add).then_inc(added, 1)

    return turn if dve is None else add


RING0 = 4
BIAS_AT = 2
DOWN_LAG = 3


def layer0_experts(nc, dram, x, ident):
    with ExitStack() as ctx:
        sb, ps, sem = allocators(nc, ctx)
        xn = sb("e0_xn", [P, NT, D], F32)
        xnT = sb("e0_xnT", [P, T], F32)
        wg = sb("wg", [P, E0], F32)
        b2 = sb("e0_b2", [E0, D], F32)
        iota = sb("iota", [P, E0], F32)
        s = sb("gate_s", [P, NT, E0], F32)
        best_of = sb("best_of_group", [P, NT, 8], F32)
        top = sb("gate_top", [P, NT, 8], F32)
        at = sb("gate_at", [P, NT, 8], U32)
        atf = sb("gate_atf", [P, NT, 8], F32)
        gmask = sb("group_mask", [P, NT, GROUPS0], F32)
        hit = sb("gate_hit", [P, NT, E0], F32)
        chosen = sb("gate_chosen", [P, NT, E0], F32)
        total = sb("gate_total", [P, NT], F32)
        weT = sb("gate_wT", [E0, T], F32)
        xn_hi = sb("e0_xn_hi", [P, T], F16)
        xn_lo = sb("e0_xn_lo", [P, T], F16)
        w = [sb(f"e0_w{i}", [P, 3, P], F32) for i in range(RING0)]
        w_hi = [sb(f"e0_w_hi{i}", [P, 3, P], F16) for i in range(RING0)]
        w_lo = [sb(f"e0_w_lo{i}", [P, 3, P], F16) for i in range(RING0)]
        b13 = [sb(f"e0_b13{i}", [P, 2], F32) for i in range(RING0)]
        silu = [sb(f"e0_silu{i}", [P, CH], F32) for i in range(2)]
        hid = [sb(f"e0_hid{i}", [P, CH], F32) for i in range(2)]
        hid_hi = [sb(f"e0_hid_hi{i}", [P, CH], F16) for i in range(NCH)]
        hid_lo = [sb(f"e0_hid_lo{i}", [P, CH], F16) for i in range(NCH)]
        work = norm_work(sb, "1")
        bank = [ps(f"e0_bank{i}", [P, CH], F32) for i in range(2)]
        up = [ps(f"e0_up{i}", [P, CH], F32) for i in range(2)]
        gate = [ps(f"e0_gate{i}", [P, CH], F32) for i in range(2)]
        down = [ps(f"e0_down{i}", [P, 4, D], F32) for i in range(2)]
        (small_in, var, std, own_sem, normed, xnT_full, xnT_ready, logits, gated, weT_full, weT_ready,
         bias_full, bias_added, chosen_ready, up_full, silu_ready, hid_ready, down_full, down_added, xn_hi_ready,
         xn_lo_ready, w_hi_ready, w_lo_ready, hi_ready, lo_ready) = (
            sem("e0_" + n) for n in (
                "small_in", "var", "std", "own", "normed", "xnT_full", "xnT_ready", "logits",
                "gated", "weT_full", "weT_ready", "bias_full", "bias_added", "chosen_ready", "up_full", "silu_ready",
                "hid_ready", "down_full", "down_added", "xn_hi_ready", "xn_lo_ready", "w_hi_ready", "w_lo_ready",
                "hi_ready", "lo_ready"))
        w_in = [sem(f"e0_w_in{i}") for i in range(RING0)]
        known = lambda n, below: isinstance(n, int) and n < below

        def every_expert(eng, body):
            for e in range(RING0):
                body(e, e, True)
            with eng.Fori(1, E0 // RING0 - 1) as quad:
                for m in range(RING0):
                    body(quad * RING0 + m, m, True)
            for m in range(RING0):
                body(E0 - RING0 + m, m, m + 2 < RING0)

        SMALL = 3

        with nc.Block() as block:
            @block.sync
            def _(sp):
                for dst, src in ((wg, "wg"), (b2, "e0_b2"), (iota, "iota")):
                    sp.dma_start(dst[:], dram[src]).then_inc(small_in, 16)

                def load(e, m):
                    for j, n in enumerate(("e0_w1", "e0_w3", "e0_w2")):
                        sp.dma_start(w[m][:, j, :], dram[n][bass.ds(e, 1), :, :].rearrange("a d i -> (a d) i")
                                     ).then_inc(w_in[m], 16)
                    sp.dma_start(b13[m][:], dram["e0_b13"][bass.ds(e, 1), :, :].rearrange("a i j -> (a i) j")
                                 ).then_inc(w_in[m], 16)

                def expert(e, m, ahead):
                    if not known(e, RING0):
                        sp.wait_ge(down_full, (e - RING0 + 1) * NCH)
                    load(e, m)

                every_expert(sp, expert)

            @block.scalar
            def _(act):
                act.wait_ge(var, 1)
                act.activation(work[3][:], work[2][:], ACT.Sqrt).then_inc(std, 1)
                for c in range(NCH):
                    act.wait_ge(xnT_full, c + 1)
                    act.activation(xnT[:, c * CH:(c + 1) * CH], bank[c % 2][:], ACT.Copy).then_inc(xnT_ready, 1)
                act.wait_ge(logits, 1)
                act.activation(s[:].rearrange("p t e -> p (t e)"), bank[0][:, 0:NT * E0], ACT.Sigmoid
                               ).then_inc(gated, 1)

                for c in range(NCH):
                    cols = slice(c * CH, (c + 1) * CH)
                    act.wait_ge(xnT_ready, c + 1)
                    act.activation(xn_hi[:, cols], xnT[:, cols], ACT.Copy).then_inc(xn_hi_ready, 1)

                def split(e, m):
                    act.wait_ge(w_in[m], (e - m) * (64 // RING0) + 64)
                    if not known(e, RING0):
                        act.wait_ge(down_full, (e - RING0 + 1) * NCH)
                    act.activation(w_hi[m][:], w[m][:], ACT.Copy).then_inc(w_hi_ready, 1)

                def high(n, c):
                    act.wait_ge(hid_ready, n + 1)
                    if not known(n, NCH):
                        act.wait_ge(down_full, n - NCH + 1)
                    act.activation(hid_hi[c][:], hid[c % 2][:], ACT.Copy).then_inc(hi_ready, 1)

                def expert(e, m, ahead):
                    for c in range(NCH):
                        n = e * NCH + c
                        if known(n, BIAS_AT + 1) and n == BIAS_AT:
                            for i in range(NCH):
                                act.wait_ge(weT_full, i + 1)
                                act.activation(weT[:, i * CH:(i + 1) * CH], bank[i % 2][0:E0, :], ACT.Copy
                                               ).then_inc(weT_ready, 1)
                        act.wait_ge(up_full, n + 1)
                        if not known(n, 2):
                            act.wait_ge(hid_ready, n - 1)
                        act.activation(silu[c % 2][:], up[c % 2][:], ACT.Silu, bias=b13[m][:, 0:1]
                                       ).then_inc(silu_ready, 1)
                        if not known(n, 1):
                            high(n - 1, (c - 1) % NCH)
                        if c == 1 and ahead:
                            split(e + 2, (m + 2) % RING0)

                split(0, 0)
                split(1, 1)
                every_expert(act, expert)
                high(E0 * NCH - 1, NCH - 1)

            @block.gpsimd
            def _(pool):
                for c in range(NCH):
                    cols = slice(c * CH, (c + 1) * CH)
                    pool.wait_ge(xn_hi_ready, c + 1)
                    pool.tensor_tensor(xn_lo[:, cols], xnT[:, cols], xn_hi[:, cols], ALU.subtract
                                       ).then_inc(xn_lo_ready, 1)

                def split(e, m):
                    pool.wait_ge(w_hi_ready, e + 1)
                    pool.tensor_tensor(w_lo[m][:], w[m][:], w_hi[m][:], ALU.subtract).then_inc(w_lo_ready, 1)

                def expert(e, m, ahead):
                    for c in range(NCH):
                        n = e * NCH + c
                        pool.wait_ge(hi_ready, n + 1)
                        if not known(n, NCH):
                            pool.wait_ge(down_full, n - NCH + 1)
                        pool.tensor_tensor(hid_lo[c][:], hid[c % 2][:], hid_hi[c][:], ALU.subtract
                                           ).then_inc(lo_ready, 1)
                        if c == 1 and ahead:
                            split(e + 2, (m + 2) % RING0)

                split(0, 0)
                split(1, 1)
                every_expert(pool, expert)

            @block.vector
            def _(dve):
                own = Order(dve, own_sem)
                layer_norm(dve, own, x, xn, work, var, std, 0, normed)
                own.link(dve.memset(best_of[:], -1.0))

                def top8(values):
                    for t in range(NT):
                        own.mark(dve.max(top[:, t, :], values[:, t, :]))
                    own.wait()
                    for t in range(NT):
                        own.mark(dve.max_index(at[:, t, :], top[:, t, :], values[:, t, :]))
                    own.wait()
                    own.link(dve.tensor_copy(atf[:], at[:]))

                def mark(mask, n, count):
                    places = iota[:, 0:n].unsqueeze(1).broadcast_to([P, NT, n])
                    for k in range(count):
                        own.link(dve.tensor_tensor(hit[:, :, 0:n] if k else mask, places,
                                                   atf[:, :, k:k + 1].broadcast_to([P, NT, n]), ALU.is_equal))
                        if k:
                            own.link(dve.tensor_tensor(mask, mask, hit[:, :, 0:n], ALU.add))

                dve.wait_ge(small_in, SMALL * 16)
                dve.wait_ge(gated, 1)
                own.link(dve.tensor_reduce(best_of[:, :, 0:GROUPS0],
                                           s[:].rearrange("p t (g k) -> p t g k", g=GROUPS0), AX.X, ALU.max))
                top8(best_of)
                mark(gmask[:], GROUPS0, TOPG0)
                per_expert = gmask[:].unsqueeze(3).broadcast_to([P, NT, GROUPS0, E0 // GROUPS0])
                own.link(dve.tensor_tensor(hit[:].rearrange("p t (g k) -> p t g k", g=GROUPS0),
                                           s[:].rearrange("p t (g k) -> p t g k", g=GROUPS0), per_expert, ALU.mult))
                own.link(dve.tensor_scalar(gmask[:], gmask[:], -1.0, None, ALU.add))
                own.link(dve.tensor_tensor(chosen[:].rearrange("p t (g k) -> p t g k", g=GROUPS0),
                                           hit[:].rearrange("p t (g k) -> p t g k", g=GROUPS0), per_expert, ALU.add))
                top8(chosen)
                mark(chosen[:], E0, TOPK0)
                own.link(dve.tensor_tensor(s[:], s[:], chosen[:], ALU.mult))
                own.link(dve.tensor_reduce(total[:], s[:], AX.X, ALU.add))
                own.link(dve.reciprocal(total[:], total[:]))
                own.link(dve.tensor_tensor(s[:], s[:], total[:].unsqueeze(2).broadcast_to([P, NT, E0]), ALU.mult))
                dve.tensor_scalar(s[:], s[:], ROUTE_SCALE, None, ALU.mult).then_inc(chosen_ready, 1)
                def add_biases():
                    for c in range(NCH):
                        dve.wait_ge(bias_full, c + 1)
                        rows = x[:, 4 * c:4 * c + 4, :].rearrange("p t d -> p (t d)")
                        dve.tensor_tensor(rows, rows, bank[c % 2][:], ALU.add).then_inc(bias_added, 1)
                    dve.wait_ge(bias_added, NCH)

                def add_down(n, c, e):
                    dve.wait_ge(down_full, n + 1)
                    if not (isinstance(n, int) and n < NCH):
                        dve.wait_ge(down_added, n - NCH + 1)
                    for j in range(4):
                        t = 4 * c + j
                        ins = dve.scalar_tensor_tensor(x[:, t, :], down[c % 2][:, j, :], s[:, t, bass.ds(e, 1)],
                                                       x[:, t, :], ALU.mult, ALU.add)
                    ins.then_inc(down_added, 1)

                def expert(e, m, ahead):
                    dve.wait_ge(w_in[m], (e - m) * (64 // RING0) + 64)
                    for c in range(NCH):
                        n = e * NCH + c
                        if known(n, BIAS_AT + 1) and n == BIAS_AT:
                            add_biases()
                        dve.wait_ge(silu_ready, n + 1)
                        if not known(n, 2):
                            dve.wait_ge(lo_ready, n - 1)
                        dve.scalar_tensor_tensor(hid[c % 2][:], gate[c % 2][:], b13[m][:, 1:2], silu[c % 2][:],
                                                 ALU.add, ALU.mult).then_inc(hid_ready, 1)
                        if not known(n, DOWN_LAG):
                            add_down(n - DOWN_LAG, (c - DOWN_LAG) % NCH, e if c >= DOWN_LAG else e - 1)

                every_expert(dve, expert)
                for c in range(NCH - DOWN_LAG, NCH):
                    add_down((E0 - 1) * NCH + c, c, E0 - 1)

            @block.tensor
            def _(pe):
                for c in range(NCH):
                    pe.wait_ge(normed, c + 1)
                    if c >= 2:
                        pe.wait_ge(xnT_ready, c - 1)
                    for j in range(4):
                        ins = pe.transpose(bank[c % 2][:, j * P:(j + 1) * P], xn[:, 4 * c + j, :], ident[:])
                    ins.then_inc(xnT_full, 1)
                pe.wait_ge(xnT_ready, NCH)
                pe.wait_ge(small_in, SMALL * 16)
                for t in range(NT):
                    ins = pe.matmul(bank[0][:, t * E0:(t + 1) * E0], xnT[:, t * P:(t + 1) * P], wg[:], start=True,
                                    stop=True)
                ins.then_inc(logits, 1)
                def output_biases():
                    pe.wait_ge(chosen_ready, 1)
                    for c in range(NCH):
                        if c >= 2:
                            pe.wait_ge(weT_ready, c - 1)
                        for j in range(4):
                            ins = pe.transpose(bank[c % 2][0:E0, j * P:(j + 1) * P], s[:, 4 * c + j, :], ident[:])
                        ins.then_inc(weT_full, 1)
                    pe.wait_ge(weT_ready, NCH)
                    for c in range(NCH):
                        if c >= 2:
                            pe.wait_ge(bias_added, c - 1)
                        for j in range(4):
                            ins = pe.matmul(bank[c % 2][:, j * P:(j + 1) * P], weT[:, (4 * c + j) * P:(4 * c + j + 1) * P],
                                            b2[:], start=True, stop=True)
                        ins.then_inc(bias_full, 1)

                def put_down(n, c, m):
                    pe.wait_ge(lo_ready, n + 1)
                    if not known(n, 2):
                        pe.wait_ge(down_added, n - 1)
                    for j in range(4):
                        tokens, out = slice(j * P, (j + 1) * P), down[c % 2][:, j, :]
                        pe.matmul(out, hid_hi[c][:, tokens], w_hi[m][:, 2, :], start=True, stop=False)
                        pe.matmul(out, hid_hi[c][:, tokens], w_lo[m][:, 2, :], start=False, stop=False)
                        ins = pe.matmul(out, hid_lo[c][:, tokens], w_hi[m][:, 2, :], start=False, stop=True)
                    ins.then_inc(down_full, 1)

                def expert(e, m, ahead):
                    pe.wait_ge(w_lo_ready, e + 1)
                    for c in range(NCH):
                        n = e * NCH + c
                        cols = slice(c * CH, (c + 1) * CH)
                        if known(n, BIAS_AT + 1) and n == BIAS_AT:
                            output_biases()
                        if not known(n, 2):
                            pe.wait_ge(hid_ready, n - 1)
                        for j, out in ((0, up[c % 2]), (1, gate[c % 2])):
                            pe.matmul(out[:], w_hi[m][:, j, :], xn_hi[:, cols], start=True, stop=False)
                            pe.matmul(out[:], w_hi[m][:, j, :], xn_lo[:, cols], start=False, stop=False)
                            ins = pe.matmul(out[:], w_lo[m][:, j, :], xn_hi[:, cols], start=False, stop=True)
                        ins.then_inc(up_full, 1)
                        if not known(n, DOWN_LAG):
                            before = (c - DOWN_LAG) % NCH
                            put_down(n - DOWN_LAG, before, m if c >= DOWN_LAG else (m - 1) % RING0)

                pe.wait_ge(xn_lo_ready, NCH)
                every_expert(pe, expert)
                for c in range(NCH - DOWN_LAG, NCH):
                    put_down((E0 - 1) * NCH + c, c, RING0 - 1)


KW = CKV + ROPE1
QW = 2 * ROPE1 + CKV
NQ = H1 * ROPE1
GROUP = 16
NG = P // GROUP
HALF = NG // 2
WIN = 2 * P
SC = WIN + P


SPIN = 2
SOFT = 4

def index_width(t):
    return KTS if t == 0 else t * P + P - LW


def rotate(eng, own, dst, mu, cos, sin, turned, swapped):
    own.mark(eng.tensor_tensor(turned, mu, cos, ALU.mult))
    lo, hi = slice(0, HALF1), slice(HALF1, ROPE1)
    last = lambda ap, cols: ap[(slice(None),) * (ap.ndim - 1) + (cols,)]
    own.mark(eng.tensor_tensor(last(swapped, lo), last(mu, hi), last(sin, lo), ALU.mult))
    own.mark(eng.tensor_tensor(last(swapped, hi), last(mu, lo), last(sin, hi), ALU.mult))
    own.wait()
    return eng.tensor_tensor(dst, turned, swapped, ALU.add)


def projections1(nc, dram, x, ident, keep):
    with ExitStack() as ctx:
        sb, ps, sem = allocators(nc, ctx)
        xnT = sb("a1_xnT", [P, T], F32)
        wkvr = sb("wkvr", [P, KW], F32)
        wdq = sb("a1_wdq", [P, CQ], F32)
        wuq = sb("wuq", [DH1, H1, CQ], F32)
        wuk = sb("wuk", [DH1, H1, CKV], F32)
        wuv = sb("wuv", [DH1, H1, CKV], F32)
        wo = sb("a1_wo", [DH1, H1, D], F32)
        wqq = sb("wqq", [CQ, H1 * CKV + NQ], F32)
        widxq = sb("widxq", [P, NIDX * P], F32)
        widxk = sb("widxk", [P, P], F32)
        mu_k = sb("mu_k", [P, NT, ROPE1], F32)
        e = sb("softplus_e", [P, NT, H1 + 1, ROPE1], F32)
        u = sb("softplus_u", [P, NT, H1 + 1, ROPE1], F32)
        cos_k = sb("cos_k", [P, NT, ROPE1], F32)
        sin_k = sb("sin_k", [P, NT, ROPE1], F32)
        xn = u[:].rearrange("p t h r -> p t (h r)")[:, :, 0:D]
        spare = sb("a1_spare", [P, T], F32)
        cqT = spare[0:CQ, :]
        near_key = spare[:, 0:NT * KW].rearrange("p (t k) -> p t k", k=KW)
        work = norm_work(sb, "2")
        bank = [ps(f"a1_bank{i}", [P, CH], F32) for i in range(4)]
        (w_in, turned, added, var, std, own_sem, normed, full, free, act_own, abs_ready, e_ready, u_ready, ln_ready,
         near_ready, hi_ready, low_free, mu_ready) = (sem("a1_" + n) for n in (
             "w_in", "turned", "added", "var", "std", "own", "normed", "full", "free", "act_own", "abs_ready", "e_ready",
             "u_ready", "ln_ready", "near_ready", "hi_ready", "low_free", "mu_ready"))
        rows, QN, near, nout, qi, ki_hi, ki_lo = (
            keep[n] for n in ("rows", "queries", "near_keys", "nout", "qi", "ki_hi", "ki_lo"))
        loads = [(wkvr, "wkvr"), (wdq, "a1_wdq"), (wuq, "wuq"), (wuk, "wuk"), (wqq[:, H1 * CKV:], "wqr"),
                 (wuv, "wuv"), (wo, "a1_wo"), (widxq, "widxq"), (widxk, "widxk"), (keep["idx_w"], "idx_w"),
                 (keep["cap0"], "cap0"), (keep["cap"], "cap"), (keep["mask"], "mask_first"), (keep["unit"], "unit"), (keep["cos_far"], "cos_far"),
                 (keep["sin_far"], "sin_far"), (cos_k, "cos_k"), (sin_k, "sin_k")]

        jobs = [("xnT", c) for c in range(NCH)] + [("kv", i) for i in range(2)]
        jobs += [("cq", c) for c in range(NCH)] + [("wqq", 0)] + [("q", t) for t in range(NT)]
        jobs += [("ki", c) for c in range(NCH)] + [("qi", i) for i in range(NIDX * NCH)]
        jobs += [("nout", i) for i in range(2)] + [("near", c) for c in range(NCH)]
        by_vector = lambda kind, i: kind in ("ki", "qi") or (kind == "q" and i % 2 == 1)
        free_no = {j: n + 1 for n, j in enumerate(j for j in jobs if not by_vector(*j))}
        hi_no = {j: n + 1 for n, j in enumerate(j for j in jobs if j[0] in ("ki", "qi"))}
        low_no = {j: n + 1 for n, j in enumerate(j for j in jobs if by_vector(*j))}

        PARTS = 1 + NT // SOFT
        begin = {("kv", 1): [0], ("ki", 1): [PARTS - 1],
                 **{("q", SOFT * k + 1): [k] for k in range(1, PARTS - 1)}}
        finish = {("ki", 3): [0], **{("qi", 3 * k): [k] for k in range(1, PARTS)}}
        soft = lambda buffer, k: buffer[:, :, H1, :] if k == 0 else buffer[:, SOFT * (k - 1):SOFT * k, 0:H1, :]
        pre = lambda k: mu_k[:] if k == 0 else QN[:, SOFT * (k - 1):SOFT * k, :, 0:ROPE1]

        with nc.Block() as block:
            @block.sync
            def _(sp):
                for dst, src in loads:
                    sp.dma_start(dst if isinstance(dst, bass.AP) else dst[:], dram[src]).then_inc(w_in, 16)
                sp.wait_ge(keep["rows_ready"], 1)
                sp.dma_start(keep["table"].rearrange("(t p) d -> p t d", p=P), rows[:]).then_inc(keep["table_out"], 16)
                sp.wait_ge(keep["table_out"], 16)

            @block.scalar
            def _(act):
                act.wait_ge(var, 1)
                act.activation(work[3][:], work[2][:], ACT.Sqrt).then_inc(std, 1)

                def drain(n):
                    kind, i = jobs[n]
                    src = bank[n % 4]
                    copies = {
                        "xnT": lambda: [(xnT[:, i * CH:(i + 1) * CH], src[:])],
                        "kv": lambda: [(rows[:, 8 * i:8 * i + 8, 0:CKV], kv[:, :, 0:CKV]),
                                       (mu_k[:, 8 * i:8 * i + 8, :], kv[:, :, CKV:])],
                        "cq": lambda: [(cqT[:, i * CH:(i + 1) * CH], src[0:CQ, :])],
                        "wqq": lambda: [(wqq[:, 0:H1 * CKV], src[0:CQ, 0:H1 * CKV])],
                        "q": lambda: [(QN[:, i, :, ROPE1:ROPE1 + CKV],
                                       src[:, 0:H1 * CKV].rearrange("p (h c) -> p h c", h=H1)),
                                      (QN[:, i, :, 0:ROPE1],
                                       src[:, H1 * CKV:].rearrange("p (h r) -> p h r", h=H1))],
                        "ki": lambda: [(ki_hi[:, i * CH:(i + 1) * CH], src[:])],
                        "qi": lambda: [(qi[:, i // NCH, (i % NCH) * CH:(i % NCH + 1) * CH], src[:])],
                        "nout": lambda: [(nout[:, 4 * i:4 * i + 4, :],
                                          src[0:CKV, :].rearrange("c (h n) -> c h n", h=4))],
                        "near": lambda: [(near[:, P + i * CH:P + (i + 1) * CH], src[0:KW, :])],
                    }
                    kv = src[:].rearrange("p (t k) -> p t k", k=KW)
                    act.wait_ge(full, n + 1)
                    for out, in_ in copies[kind]():
                        ins = act.activation(out, in_, ACT.Copy, scale=SCALE1 if kind == "wqq" else 1.0)
                    ins.then_inc(hi_ready if kind in ("ki", "qi") else free, 1)

                for n, job in enumerate(jobs):
                    if job[0] in ("ki", "qi") or job in free_no:
                        drain(n)
                    for k in begin.get(job, []):
                        act.wait_ge(free, free_no[("q", SOFT * k - 2) if k else ("kv", 1)])
                        if k:
                            act.wait_ge(low_free, low_no["q", SOFT * k - 1])
                        act.activation(soft(e, k), pre(k), ACT.Abs).then_inc(abs_ready, 1)
                        act.wait_ge(abs_ready, k + 1)
                        act.activation(soft(e, k), soft(e, k), ACT.Exp, scale=-1.0).then_inc(e_ready, 1)
                    for k in finish.get(job, []):
                        act.wait_ge(u_ready, k + 1)
                        act.activation(soft(u, k), soft(u, k), ACT.Ln).then_inc(ln_ready, 1)

            @block.vector
            def _(dve):
                own = Order(dve, own_sem)
                layer_norm(dve, own, x, xn, work, var, std, 0, normed)
                dve.memset(near[:, 0:P], 0.0).then_inc(near_ready, 1)

                def new_keys():
                    dve.wait_ge(mu_ready, 1)
                    dve.tensor_copy(rows[:, :, CKV:], mu_k[:]).then_inc(keep["rows_ready"], 1)
                    dve.wait_ge(w_in, len(loads) * 16)
                    own.mark(dve.tensor_copy(near_key[:, :, ROPE1:], rows[:, :, 0:CKV]))
                    rotate(dve, own, near_key[:, :, 0:ROPE1], mu_k[:], cos_k[:], sin_k[:], soft(e, 0), soft(u, 0)
                           ).then_inc(near_ready, 1)

                for n, (kind, i) in enumerate(jobs):
                    src = bank[n % 4]
                    if kind == "ki":
                        cols = slice(i * CH, (i + 1) * CH)
                        dve.wait_ge(hi_ready, hi_no[kind, i])
                        dve.tensor_tensor(ki_lo[:, cols], src[0:DH1, :], ki_hi[0:DH1, cols], ALU.subtract
                                          ).then_inc(low_free, 1)
                    elif kind == "qi":
                        low = qi[DH1:, i // NCH, (i % NCH) * CH:(i % NCH + 1) * CH]
                        dve.wait_ge(hi_ready, hi_no[kind, i])
                        dve.tensor_tensor(low, src[DH1:, :], low, ALU.subtract).then_inc(low_free, 1)
                    elif kind == "q" and i % 2:
                        dve.wait_ge(full, n + 1)
                        dve.tensor_copy(QN[:, i, :, ROPE1:ROPE1 + CKV],
                                        src[:, 0:H1 * CKV].rearrange("p (h c) -> p h c", h=H1))
                        dve.tensor_copy(QN[:, i, :, 0:ROPE1], src[:, H1 * CKV:].rearrange("p (h r) -> p h r", h=H1)
                                        ).then_inc(low_free, 1)
                    for k in begin.get((kind, i), []):
                        dve.wait_ge(e_ready, k + 1)
                        own.link(dve.tensor_scalar(soft(u, k), soft(e, k), 1.0, None, ALU.add))
                        dve.scalar_tensor_tensor(soft(e, k), soft(u, k), -1.0, soft(e, k), ALU.add, ALU.subtract
                                                 ).then_inc(u_ready, 1)
                    for k in finish.get((kind, i), []):
                        dve.wait_ge(ln_ready, k + 1)
                        own.link(dve.tensor_tensor(soft(u, k), soft(u, k), soft(e, k), ALU.subtract))
                        dve.scalar_tensor_tensor(pre(k), pre(k), 0.0, soft(u, k), ALU.max, ALU.add
                                                 ).then_inc(mu_ready, 1)
                        if k == 0:
                            new_keys()

            @block.tensor
            def _(pe):
                def fill(n):
                    kind, i = jobs[n]
                    b = bank[n % 4]
                    before = jobs[n - 4] if n >= 4 else None
                    if before in free_no:
                        pe.wait_ge(free, free_no[before])
                    if before in low_no:
                        pe.wait_ge(low_free, low_no[before])
                    mm = lambda out, lhsT, rhs: pe.matmul(out, lhsT, rhs, start=True, stop=True)
                    cols = slice(i * CH, (i + 1) * CH)
                    if kind == "xnT":
                        for j in range(4):
                            ins = pe.transpose(b[:, j * P:(j + 1) * P], xn[:, 4 * i + j, :], ident[:])
                    elif kind == "kv":
                        for j in range(8):
                            t = 8 * i + j
                            ins = mm(b[:, j * KW:(j + 1) * KW], xnT[:, t * P:(t + 1) * P], wkvr[:])
                    elif kind == "cq":
                        ins = mm(b[0:CQ, :], wdq[:], xnT[:, cols])
                    elif kind == "wqq":
                        for h in range(H1):
                            ins = mm(b[0:CQ, h * CKV:(h + 1) * CKV], wuq[:, h, :], wuk[:, h, :])
                    elif kind == "q":
                        ins = mm(b[:], cqT[:, i * P:(i + 1) * P], wqq[:])
                    elif kind == "ki":
                        ins = mm(b[:], widxk[:], xnT[:, cols])
                    elif kind == "qi":
                        c = i % NCH
                        ins = mm(b[:], widxq[:, (i // NCH) * P:(i // NCH + 1) * P], xnT[:, c * CH:(c + 1) * CH])
                    elif kind == "nout":
                        for h in range(4):
                            ins = mm(b[0:CKV, h * D:(h + 1) * D], wuv[:, 4 * i + h, :], wo[:, 4 * i + h, :])
                    else:
                        for j in range(4):
                            ins = pe.transpose(b[0:KW, j * P:(j + 1) * P], near_key[:, 4 * i + j, :], ident[:])
                    ins.then_inc(full, 1)

                for n, (kind, i) in enumerate(jobs):
                    if n < NCH:
                        pe.wait_ge(normed, n + 1)
                    if n == NCH:
                        pe.wait_ge(w_in, len(loads) * 16)
                        pe.wait_ge(free, NCH)
                    if (kind, i) == ("q", 0):
                        pe.wait_ge(free, free_no["wqq", 0])
                    if (kind, i) == ("near", 0):
                        pe.wait_ge(near_ready, 2)
                    fill(n)


RING = 3
PLACES = 6
A_SLOT = 24
EARLY = 3
EARLY_SLOTS = A_SLOT - 2
RANK_SLOTS = NT * NG + NG
RANK_OPS = 1 + 3 * (FAR // 8)
RANK_FIXED = 64


def index_schedule():
    slots = {}
    steps = []
    for n in range(NT + 1):
        idx = [("idx", n, i) for i in range(len(index_chunks(n)) * NIDX)] if n < NT else []
        rank = [("rank", n - 1, i) for i in range(RANK_OPS)] if n else []
        work = [w for i in range(len(idx) + len(rank)) for w in (idx[i:i + 1] + rank[i:i + 1])]
        if n < EARLY:
            for i, w in enumerate(work):
                slots.setdefault((n * len(work) + i) * EARLY_SLOTS // (EARLY * len(work)), []).append(w)
        else:
            steps += work
    cost = lambda w: (index_width(w[1]) if w[0] == "rank" else 0 if w[2] % NIDX == 0 else
                      min(CH, index_width(w[1]) - w[2] // NIDX * CH)) + RANK_FIXED
    total, done, shares = sum(map(cost, steps)), 0, RANK_SLOTS - EARLY_SLOTS
    slot, scored = 0, {}
    for w in steps:
        slot = max(slot, done * shares // total)
        if w[0] == "idx":
            scored[w[1]] = slot
        else:
            slot = max(slot, scored.get(w[1], -1) + 1)
        slots.setdefault(EARLY_SLOTS + slot, []).append(w)
        done += cost(w)
    return slots


def selected_schedule(slot, ranking):
    j = slot - A_SLOT
    group = lambda kind, j: [(kind, j // NG, j % NG)] if 0 <= j < NT * NG else []
    before = [w[1:] for w in ranking.get(slot - 1, []) if w[0] == "idx"]
    t, c, y = j // NG, (j + 1) // NG - 1, (j + 1) // NG - 2
    sums = {2: [("p", c, 0)], 3: [("p", c, 2), ("p", c, 4)], 4: [("ctx", c, 0)], 6: [("p", c, 1), ("p", c, 3)],
            7: [("p", c, 5), ("ctx", c, 1)]}
    work = [("relu", *w) for w in before]
    work += group("score", j - 1)
    work += [("q", t, i) for i in range(4)] if j % NG == 0 and 0 <= t < NT else []
    work += [("y", y, 0)] if (j + 1) % NG == 0 and 0 <= y < NT else []
    work += group("far", j) + group("max", j - 2) + group("exp", j - 3)
    work += group("den", j - 4) + group("norm", j - 5)
    work += sums.get((j + 1) % NG, []) if 0 <= c < NT else []
    work += [("sum", *w) for w in before]
    work += ranking.get(slot, [])
    work += [("spin", k, 0) for k in range(NT // SPIN)] if j == -2 else []
    ahead = j + 2
    work += [("keys", ahead // NG, ahead % NG // HALF)] if ahead % HALF == 0 and 0 <= ahead < NT * NG else []
    return work


def index_chunks(t):
    return [(lo, min(lo + CH, index_width(t))) for lo in range(0, index_width(t), CH)]


def selected_attention(nc, dram, x, ident, keep):
    with ExitStack() as ctx:
        sb, ps, sem = allocators(nc, ctx)
        rows, QN, near, nout, qi, ki_hi, ki_lo, mask = (
            keep[n] for n in ("rows", "queries", "near_keys", "nout", "qi", "ki_hi", "ki_lo", "mask"))
        index = [sb(f"index{i}", [P, T], F32) for i in range(2)]
        relu = [sb(f"relu{i}", [P, CH], F32) for i in range(1, NIDX)]
        top = sb("a1_top", [P, 8], F32)
        place = sb("place", [P, FAR], U32)
        placeT = [sb(f"placeT{i}", [P, FAR], U32) for i in range(PLACES)]
        far = [sb(f"far{i}", [P, 32, KW], F32) for i in range(RING)]
        turned = sb("far_turned", [P, 16, ROPE1], F32)
        swapped = sb("far_swapped", [P, 16, ROPE1], F32)
        angle = far[RING - 1][:].rearrange("p i k -> p (i k)").rearrange("p (a t r) -> p a t r", a=4, t=NT)
        qT = sb("qT", [KW, 2, 32, 4, H1], F32)
        farT = sb("farT", [KW, 2, 4, P], F32)
        probs = [sb(f"a1_probs{i}", [P, NG, SC], F32) for i in range(2)]
        probsT = sb("a1_probsT", [P, 3, NG, P], F32)
        biggest = sb("biggest", [P, NG], F32)
        den = sb("a1_den", [P, NG], F32)
        ctxT = sb("ctxT", [CKV, H1, P], F32)
        score = [ps(f"a1_score{i}", [P, CH], F32) for i in range(3)]
        turn = [ps(f"a1_turn{i}", [P, CH], F32) for i in range(2)]
        idx = [ps(f"a1_idx{i}", [P, CH], F32) for i in range(2)]
        ctxp = ps("a1_ctx", [CKV, CH], F32)
        (idx_full, relu_ready, summed, own_sem, place_ready, keys_ready, turn_full, turn_free, score_full, first_ready,
         shift_ready, exp_ready, den_ready, normed, ctx_full, ctx_copied) = (sem("a1_" + n) for n in (
             "idx_full", "relu_ready", "summed", "own2", "place_ready", "keys_ready", "turn_full", "turn_free",
             "score_full", "first_ready", "shift_ready", "exp_ready", "den_ready", "normed_p", "ctx_full", "ctx_copied"))
        far_in = [[sem(f"far_in{i}{half}") for half in range(2)] for i in range(RING)]
        mask_in, y_added, angles_in, queries_ready = (sem(n) for n in ("mask_in", "y_added", "angles_in",
                                                                       "queries_ready"))
        sums_done = lambda n: n - (n + NIDX - 1) // NIDX

        ranking = index_schedule()
        schedule = [w for slot in range(A_SLOT + (NT + 1) * NG) for w in selected_schedule(slot, ranking)]
        TURNS = ("q", "far", "p", "y")
        order = [w for w in schedule if w[0] in TURNS]
        turn_no = {w: n + 1 for n, w in enumerate(order)}
        free_no = {w: n + 1 for n, w in enumerate(w for w in order if w[0] != "y")}
        idx_no = {w: n + 1 for n, w in enumerate(w for w in schedule if w[0] == "idx")}

        with nc.Block() as block:
            @block.sync
            def _(sp):
                for j, n in enumerate(("cos_q", "sin_q", "cos_near", "sin_near")):
                    sp.dma_start(angle[:, j], dram[n]).then_inc(angles_in, 16)
                sp.wait_ge(score_full, NG)
                sp.dma_start(mask[:], dram["mask"]).then_inc(mask_in, 16)

            @block.gpsimd
            def _(pool):
                pool.wait_ge(keep["table_out"], 16)
                for t in range(NT):
                    m = t % RING
                    pool.wait_ge(place_ready, t + 1)
                    if t == RING - 1:
                        pool.wait_ge(queries_ready, 2 * NT // SPIN)
                    if t >= RING:
                        pool.wait_ge(ctx_full, 2 * (t - RING + 1))
                    for i in range(32):
                        pool.indirect_dma_start(far[m][:, i, :], None, keep["table"],
                                                bass.IndirectOffsetOnAxis(ap=placeT[t % PLACES][:, i:i + 1], axis=0)
                                                ).then_inc(far_in[m][i // 16], 16)

            @block.scalar
            def _(act):
                def empty_turn(kind, t, i):
                    n = turn_no[kind, t, i]
                    src = turn[n % 2]
                    act.wait_ge(turn_full, n)
                    if kind == "q":
                        if t >= 1:
                            act.wait_ge(score_full, t * NG)
                        heads = slice(4 * (i % 2), 4 * (i % 2) + 4)
                        ins = act.activation(qT[:, i // 2, :, :, heads].rearrange("k i a h -> k h a i"),
                                             src[0:KW, :].rearrange("k (h a i) -> k h a i", h=4, a=4), ACT.Copy)
                    elif kind == "far":
                        if NG * t + i >= 2:
                            act.wait_ge(score_full, NG * t + i - 1)
                        ins = act.activation(farT[:, i % 2, :, :], src[0:KW, :].rearrange("k (i l) -> k i l", i=4),
                                             ACT.Copy)
                    elif kind == "p":
                        if t >= 1:
                            act.wait_ge(ctx_full, 2 * (t - 1) + i % 2 + 1)
                        ins = act.activation(probsT[:, i // 2, HALF * (i % 2):HALF * (i % 2) + HALF, :],
                                             src[:].rearrange("p (g l) -> p g l", g=HALF), ACT.Copy)
                    ins.then_inc(turn_free, 1)

                for kind, t, i in schedule:
                    if kind in TURNS and kind != "y":
                        empty_turn(kind, t, i)
                    elif kind == "relu":
                        n = idx_no["idx", t, i]
                        lo, hi = index_chunks(t)[i // NIDX]
                        act.wait_ge(idx_full, n)
                        h, values = i % NIDX, index[t % 2][:, lo:hi]
                        if h and n > NIDX:
                            act.wait_ge(summed, sums_done(n - NIDX))
                        elif h == 0 and t >= 2 and i == 0:
                            act.wait_ge(place_ready, t - 1)
                        act.activation(relu[h - 1][:, 0:hi - lo] if h else values, idx[n % 2][:, 0:hi - lo], ACT.Relu
                                       ).then_inc(relu_ready, 1)
                        if h == 0:
                            act.wait_ge(relu_ready, n)
                            act.activation(values, values, ACT.Copy, scale=keep["idx_w"][:, 0:1]
                                           ).then_inc(first_ready, 1)
                    elif kind == "exp":
                        n = t * NG + i
                        act.wait_ge(shift_ready, n + 1)
                        if t >= 2 and i == 0:
                            act.wait_ge(turn_full, turn_no["p", t - 2, 5])
                        act.activation(probs[t % 2][:, i, :], score[n % 3][:, 0:SC], ACT.Exp, bias=biggest[:, i:i + 1],
                                       accum_out=den[:, i:i + 1]).then_inc(exp_ready, 1)
                    elif kind == "norm":
                        row = probs[t % 2][:, i, :]
                        act.wait_ge(den_ready, t * NG + i + 1)
                        act.activation(row, row, ACT.Copy, scale=den[:, i:i + 1]).then_inc(normed, 1)
                    elif kind == "ctx":
                        act.wait_ge(ctx_full, 2 * t + i + 1)
                        if t >= 1:
                            act.wait_ge(turn_full, turn_no["y", t - 1, 0])
                        half = ctxT[:].rearrange("c h (a i) -> c i a h", a=4)[:, 16 * i:16 * i + 16]
                        sums = ctxp[:].rearrange("c (i a h) -> c i a h", a=4, h=H1)
                        for a in range(4):
                            ins = act.activation(half[:, :, a], sums[:, :, a], ACT.Copy)
                        ins.then_inc(ctx_copied, 1)

            @block.vector
            def _(dve):
                own = Order(dve, own_sem)

                def rank(t, i):
                    w = index_width(t)
                    values = index[t % 2][:, 0:w]
                    r = 8 * ((i - 1) // 3)
                    if i == 0:
                        dve.wait_ge(summed, sums_done(idx_no["idx", t, len(index_chunks(t)) * NIDX - 1]))
                        cols, cap = (slice(0, w), keep["cap0"]) if t == 0 else (slice(w - P, w), keep["cap"])
                        own.mark(dve.tensor_tensor(values[:, cols], values[:, cols], cap[:], ALU.min))
                    elif i % 3 == 1:
                        own.wait()
                        own.mark(dve.max(top[:], values))
                    elif i % 3 == 2:
                        own.wait()
                        own.mark(dve.max_index(place[:, r:r + 8], top[:], values))
                    elif r + 8 < FAR:
                        own.wait()
                        own.mark(dve.match_replace(values, top[:], values, -3.4e38))
                    else:
                        own.wait()
                        if t >= PLACES:
                            before = t - PLACES
                            for half in far_in[before % RING]:
                                dve.wait_ge(half, (before // RING + 1) * 256)
                        dve.transpose(placeT[t % PLACES][:], place[:]).then_inc(place_ready, 1)

                for kind, t, i in schedule:
                    if kind == "rank":
                        rank(t, i)
                    elif kind == "sum":
                        n = idx_no["idx", t, i]
                        h = i % NIDX
                        lo, hi = index_chunks(t)[i // NIDX]
                        values = index[t % 2][:, lo:hi]
                        if h == 0:
                            continue
                        dve.wait_ge(relu_ready, n)
                        if h == 1:
                            dve.wait_ge(first_ready, (n - 1) // NIDX + 1)
                        else:
                            dve.wait_ge(summed, sums_done(n - 1))
                        dve.scalar_tensor_tensor(values, relu[h - 1][:, 0:hi - lo], keep["idx_w"][:, h:h + 1], values,
                                                 ALU.mult, ALU.add).then_inc(summed, 1)
                    elif kind == "keys":
                        m = t % RING
                        dve.wait_ge(far_in[m][i], (t // RING + 1) * 256)
                        every = lambda ap: ap[:].unsqueeze(1).broadcast_to([P, 16, ROPE1])
                        part = far[m][:, 16 * i:16 * i + 16, CKV:]
                        if t or i:
                            dve.wait_ge(keys_ready, 2 * t + i)
                        else:
                            dve.wait_ge(queries_ready, 2 * NT // SPIN)
                        rotate(dve, own, part, part, every(keep["cos_far"]), every(keep["sin_far"]), turned[:],
                               swapped[:]).then_inc(keys_ready, 1)
                    elif kind == "spin":
                        tiles = slice(SPIN * t, SPIN * t + SPIN)
                        dve.wait_ge(angles_in, 4 * 16)
                        mu_q = QN[:, tiles, :, 0:ROPE1]
                        buffers = [ap[:].rearrange("p (t h) r -> p t h r", t=SPIN) for ap in (turned, swapped)]
                        for i, first in enumerate((ROPE1 + CKV, 0)):
                            cos, sin = (angle[:, 2 * i + j, tiles].unsqueeze(2).broadcast_to([P, SPIN, H1, ROPE1])
                                        for j in range(2))
                            if t or i:
                                dve.wait_ge(queries_ready, 2 * t + i)
                            rotate(dve, own, QN[:, tiles, :, first:first + ROPE1], mu_q, cos, sin, *buffers
                                   ).then_inc(queries_ready, 1)
                    elif kind == "max":
                        n = t * NG + i
                        dve.wait_ge(score_full, n + 1)
                        if t >= 1:
                            dve.wait_ge(exp_ready, n - NG + 1)
                        dve.tensor_reduce(biggest[:, i:i + 1], score[n % 3][:, 0:SC], AX.X, ALU.max, negate=True
                                          ).then_inc(shift_ready, 1)
                    elif kind == "y":
                        n = turn_no[kind, t, i]
                        dve.wait_ge(turn_full, n)
                        dve.tensor_tensor(x[:, t, :], x[:, t, :], turn[n % 2][:, 0:P], ALU.add).then_inc(y_added, 1)
                    elif kind == "den":
                        dve.wait_ge(exp_ready, t * NG + i + 1)
                        dve.reciprocal(den[:, i:i + 1], den[:, i:i + 1]).then_inc(den_ready, 1)

            @block.tensor
            def _(pe):
                def fill_turn(kind, t, i):
                    n = turn_no[kind, t, i]
                    b = turn[n % 2]
                    before = order[n - 3] if n > 2 else None
                    if before and before[0] == "y":
                        pe.wait_ge(y_added, before[1] + 1)
                    elif before:
                        pe.wait_ge(turn_free, free_no[before])
                    if kind == "q" and i == 0:
                        pe.wait_ge(queries_ready, 2 * (t // SPIN) + 2)
                    if kind == "far" and i % HALF == 0:
                        pe.wait_ge(keys_ready, 2 * t + i // HALF + 1)
                    if kind == "p":
                        pe.wait_ge(normed, t * NG + HALF * (i % 2 + 1))
                    if kind == "y":
                        pe.wait_ge(ctx_copied, 2 * t + 2)
                    for j in range(4):
                        out = b[:, j * P:(j + 1) * P]
                        if kind == "q":
                            first = (i // 2) * ROPE1
                            ins = pe.transpose(out[0:KW, :], QN[:, t, 4 * (i % 2) + j, first:first + KW], ident[:])
                        elif kind == "far":
                            ins = pe.transpose(out[0:KW, :], far[t % RING][:, 4 * i + j, :], ident[:])
                        elif kind == "p":
                            g = HALF * (i % 2) + j
                            ins = pe.transpose(out, probs[t % 2][:, g, (i // 2) * P:(i // 2 + 1) * P], ident[:])
                    if kind == "y":
                        for h in range(H1):
                            ins = pe.matmul(b[:, 0:P], ctxT[:, h, :], nout[:, h, :], start=(h == 0),
                                            stop=(h == H1 - 1))
                    ins.then_inc(turn_full, 1)

                def scores(t, g):
                    n = t * NG + g
                    b = score[n % 3]
                    pe.wait_ge(turn_free, max(free_no["q", t, 3], free_no["far", t, g]))
                    if n >= 3:
                        pe.wait_ge(exp_ready, n - 2)
                    if t == 1 and g == 0:
                        pe.wait_ge(mask_in, 16)
                    pe.matmul(b[:, 0:SC], keep["unit"][:].bitcast(BF16), mask[:, g, :].bitcast(BF16), start=True,
                              stop=False, skip_group_check=True)
                    pe.matmul(b[:, 0:WIN], qT[:, 0, 4 * g:4 * g + 4].rearrange("k i a h -> k (i a h)"),
                              near[:, t * P:t * P + WIN], start=False, stop=False, skip_group_check=True)
                    for j in range(4):
                        ins = pe.matmul(b[32 * j:32 * j + 32, WIN:SC], qT[:, 1, 4 * g + j].rearrange("k a h -> k (a h)"),
                                        farT[:, g % 2, j, :], start=False, stop=(j == 3), skip_group_check=True)
                    ins.then_inc(score_full, 1)

                def sums(t, c):
                    pe.wait_ge(turn_free, free_no["p", t, 4 + c])
                    if t >= 1 or c:
                        pe.wait_ge(ctx_copied, 2 * t + c)
                    out = ctxp[:]
                    parts = [1] if t == 0 else [0, 1]
                    for part in parts:
                        pe.matmul(out, rows[:, t - 1 + part, 0:CKV],
                                  probsT[:, part, HALF * c:HALF * c + HALF, :].rearrange("p g l -> p (g l)"),
                                  start=(part == parts[0]), stop=False, skip_group_check=True)
                    for i in range(16 * c, 16 * c + 16):
                        cols = slice((i % 4) * 32, (i % 4 + 1) * 32)
                        ins = pe.matmul(ctxp[:, (i % 16) * 32:(i % 16 + 1) * 32], far[t % RING][:, i, 0:CKV],
                                        probsT[:, 2, i // 4, cols], start=False, stop=(i % 16 == 15),
                                        skip_group_check=True)
                    ins.then_inc(ctx_full, 1)

                for kind, t, i in schedule:
                    if kind in TURNS:
                        fill_turn(kind, t, i)
                    elif kind == "score":
                        scores(t, i)
                    elif kind == "ctx":
                        sums(t, i)
                    elif kind == "idx":
                        n = idx_no[kind, t, i]
                        h = i % NIDX
                        lo, hi = index_chunks(t)[i // NIDX]
                        out = idx[n % 2][:, 0:hi - lo]
                        queries = slice(t * P, (t + 1) * P)
                        if n > 2:
                            pe.wait_ge(relu_ready, n - 2)
                        pe.matmul(out, qi[:, h, queries], ki_hi[:, lo:hi], start=True, stop=False)
                        pe.matmul(out, qi[0:DH1, h, queries], ki_lo[:, lo:hi], start=False, stop=True
                                  ).then_inc(idx_full, 1)


def layer1_attention(nc, dram, x, ident):
    with ExitStack() as ctx:
        sb, _, sem = allocators(nc, ctx)
        keep = {
            "rows": sb("rows", [P, NT, KW], F32),
            "queries": sb("queries", [P, NT, H1, QW], F32),
            "near_keys": sb("near_keys", [KW, P + T], F32),
            "nout": sb("nout", [CKV, H1, D], F32),
            "qi": sb("qi", [P, NIDX, T], F16),
            "ki_hi": sb("ki_hi", [P, T], F16),
            "ki_lo": sb("ki_lo", [DH1, T], F16),
            "idx_w": sb("idx_w", [P, NIDX], F32),
            "cap0": sb("cap0", [P, KTS], F32),
            "cap": sb("cap", [P, P], F32),
            "mask": sb("mask", [P, NG, SC], U16),
            "unit": sb("unit", [P, P], U16),
            "cos_far": sb("cos_far", [P, ROPE1], F32),
            "sin_far": sb("sin_far", [P, ROPE1], F32),
            "rows_ready": sem("rows_ready"),
            "table_out": sem("table_out"),
            "table": dram["key_table"],
        }
        projections1(nc, dram, x, ident, keep)
        selected_attention(nc, dram, x, ident, keep)


TOPK1 = 2
PRIME = 11
HASH_OFF = 7919
CLASS = T // E1
KS = HS // P
CLASS_EXPERTS = [[(r * PRIME + k * HASH_OFF) % E1 for k in range(TOPK1)] for r in range(E1)]


def layer1_experts(nc, dram, x, ident):
    with ExitStack() as ctx:
        sb, ps, sem = allocators(nc, ctx)
        xn = sb("e1_xn", [P, NT, D], F32)
        xnT = sb("e1_xnT", [P, T], F32)
        yT = sb("yT", [P, T], F32)
        sw1 = sb("sw1", [P, HS], F32)
        sw3 = sb("sw3", [P, HS], F32)
        sw2 = sb("sw2", [P, KS, D], F32)
        w1 = sb("e1_w1", [P, E1, HR], F32)
        w2 = sb("e1_w2", [HR, E1, D], F32)
        sb13 = sb("sb13", [P, 2, KS], F32)
        sb2 = sb("sb2", [P, 1], F32)
        b1 = sb("e1_b1", [HR, E1], F32)
        b2 = sb("e1_b2", [P, TOPK1, E1], F32)
        b2_sum = sb("e1_b2_sum", [P, E1], F32)
        silu = [sb(f"e1_silu{i}", [P, CH], F32) for i in range(2)]
        hid = [sb(f"e1_hid{i}", [P, CH], F32) for i in range(2)]
        part = [sb(f"e1_part{i}", [P, CLASS], F32) for i in range(2)]
        work = norm_work(sb, "3")
        bank = [ps(f"e1_bank{i}", [P, CH], F32) for i in range(2)]
        up = [ps(f"e1_up{i}", [P, CH], F32) for i in range(2)]
        gate = [ps(f"e1_gate{i}", [P, CH], F32) for i in range(2)]
        down = [ps(f"e1_down{i}", [P, CH], F32) for i in range(2)]
        (w_in, var, std, own_sem, normed, xnT_full, xnT_ready, up_full, act_ready, hid_ready, hid_used,
         down_read, y_ready, y_turned, out_ready, out_done) = (
             sem("e1_" + n) for n in (
                 "w_in", "var", "std", "own", "normed", "xnT_full", "xnT_ready", "up_full",
                 "act_ready", "hid_ready", "hid_used", "down_read", "y_ready", "y_turned", "out_ready",
                 "out_done"))
        loads = [(sw1, "sw1"), (sw3, "sw3"), (sw2, "sw2"), (sb13, "sb13"), (sb2, "sb2"), (w1, "e1_w1"), (w2, "e1_w2"),
                 (b1, "e1_b1"), (b2, "e1_b2")]
        SHARED = NCH * KS
        ROUTED = E1 * TOPK1

        with nc.Block() as block:
            @block.sync
            def _(sp):
                for dst, src in loads:
                    sp.dma_start(dst[:], dram[src]).then_inc(w_in, 16)
                rows = dram["out"].rearrange("(t p) d -> p t d", p=P)
                for c in range(NCH):
                    sp.wait_ge(out_ready, c + 1)
                    sp.dma_start(rows[:, 4 * c:4 * c + 4, :], x[:, 4 * c:4 * c + 4, :]).then_inc(out_done, 16)
                sp.wait_ge(out_done, NCH * 16)

            @block.scalar
            def _(act):
                act.wait_ge(var, 1)
                act.activation(work[3][:], work[2][:], ACT.Sqrt).then_inc(std, 1)
                for c in range(NCH):
                    act.wait_ge(xnT_full, c + 1)
                    act.activation(xnT[:, c * CH:(c + 1) * CH], bank[c % 2][:], ACT.Copy).then_inc(xnT_ready, 1)
                act.wait_ge(w_in, len(loads) * 16)
                for n in range(SHARED):
                    act.wait_ge(up_full, n + 1)
                    if n >= 2:
                        act.wait_ge(hid_ready, n - 1)
                    act.activation(silu[n % 2][:], up[n % 2][:], ACT.Silu, bias=sb13[:, 0, n % KS:n % KS + 1]
                                   ).then_inc(act_ready, 1)
                for i in range(ROUTED):
                    n = SHARED + i
                    e = CLASS_EXPERTS[i // TOPK1][i % TOPK1]
                    act.wait_ge(up_full, n + 1)
                    act.wait_ge(hid_used, n - 1)
                    act.activation(hid[n % 2][:, 0:CLASS], up[n % 2][:, 0:CLASS], ACT.Gelu, bias=b1[:, e:e + 1]
                                   ).then_inc(act_ready, 1)

            @block.vector
            def _(dve):
                own = Order(dve, own_sem)
                layer_norm(dve, own, x, xn, work, var, std, 0, normed)
                dve.wait_ge(w_in, len(loads) * 16)
                own.link(dve.tensor_tensor(b2_sum[:], b2[:, 0, :], b2[:, 1, :], ALU.add))

                def shared_out(c):
                    dve.wait_ge(hid_used, (c + 1) * KS)
                    dve.tensor_scalar(yT[:, c * CH:(c + 1) * CH], down[c % 2][:], sb2[:], 0.5, ALU.add, ALU.mult
                                      ).then_inc(down_read, 1)

                for n in range(SHARED):
                    dve.wait_ge(act_ready, n + 1)
                    if n >= 2:
                        dve.wait_ge(hid_used, n - 1)
                    dve.scalar_tensor_tensor(hid[n % 2][:], gate[n % 2][:], sb13[:, 1, n % KS:n % KS + 1],
                                             silu[n % 2][:], ALU.add, ALU.mult).then_inc(hid_ready, 1)
                    if n >= KS and n % KS == 0:
                        shared_out(n // KS - 1)
                shared_out(NCH - 1)
                dve.wait_ge(down_read, NCH)
                for r in range(E1):
                    n = NCH + r
                    dve.wait_ge(hid_used, SHARED + (r + 1) * TOPK1)
                    own.link(dve.tensor_scalar(part[r % 2][:], down[n % 2][:, 0:CLASS], b2_sum[:, r:r + 1],
                                               0.5 / TOPK1, ALU.add, ALU.mult))
                    dve.tensor_tensor(yT[:, r:T:E1], yT[:, r:T:E1], part[r % 2][:], ALU.add).then_inc(down_read, 1)
                add_transposed(dve, None, x, yT, ident, bank, y_turned, out_ready)()

            @block.tensor
            def _(pe):
                for c in range(NCH):
                    pe.wait_ge(normed, c + 1)
                    if c >= 2:
                        pe.wait_ge(xnT_ready, c - 1)
                    for j in range(4):
                        ins = pe.transpose(bank[c % 2][:, j * P:(j + 1) * P], xn[:, 4 * c + j, :], ident[:])
                    ins.then_inc(xnT_full, 1)
                pe.wait_ge(w_in, len(loads) * 16)
                pe.wait_ge(xnT_ready, NCH)

                def rise(n):
                    if n >= 2:
                        pe.wait_ge(act_ready, n - 1)
                    if n < SHARED:
                        if n >= 2:
                            pe.wait_ge(hid_ready, n - 1)
                        c, k = n // KS, n % KS
                        cols, half = slice(c * CH, (c + 1) * CH), slice(k * P, (k + 1) * P)
                        pe.matmul(up[n % 2][:], sw1[:, half], xnT[:, cols], start=True, stop=True)
                        ins = pe.matmul(gate[n % 2][:], sw3[:, half], xnT[:, cols], start=True, stop=True)
                    else:
                        r, k = (n - SHARED) // TOPK1, (n - SHARED) % TOPK1
                        ins = pe.matmul(up[n % 2][:, 0:CLASS], w1[:, CLASS_EXPERTS[r][k], :], xnT[:, r:T:E1],
                                        start=True, stop=True)
                    ins.then_inc(up_full, 1)

                def fall(n):
                    if n < SHARED:
                        out, k, last = n // KS, n % KS, KS - 1
                        pe.wait_ge(hid_ready, n + 1)
                        w, width = sw2[:, k, :], CH
                    else:
                        r, k = (n - SHARED) // TOPK1, (n - SHARED) % TOPK1
                        out, last = NCH + r, TOPK1 - 1
                        pe.wait_ge(act_ready, n + 1)
                        w, width = w2[:, CLASS_EXPERTS[r][k], :], CLASS
                    if k == 0 and out >= 2:
                        pe.wait_ge(down_read, out - 1)
                    ins = pe.matmul(down[out % 2][:, 0:width], w, hid[n % 2][:, 0:width], start=(k == 0),
                                    stop=(k == last))
                    ins.then_inc(hid_used, 1)

                for n in range(SHARED + ROUTED):
                    rise(n)
                    if n:
                        fall(n - 1)
                fall(SHARED + ROUTED - 1)
                pe.wait_ge(down_read, NCH + E1)
                add_transposed(None, pe, x, yT, ident, bank, y_turned, out_ready)()


def build(nc, dram):
    with ExitStack() as ctx:
        sb, _, _ = allocators(nc, ctx)
        x = sb("x", [P, NT, D], F32)
        ident = sb("ident", [P, P], F32)
        layer0_attention(nc, dram, x, ident)
        layer0_experts(nc, dram, x, ident)
        layer1_attention(nc, dram, x, ident)
        layer1_experts(nc, dram, x, ident)


def tables():
    f32 = np.float32
    bfloat16 = lambda v: (np.ascontiguousarray(v, f32).view(np.uint32) >> 16).astype(np.uint16)
    t = {"ident": np.eye(P, dtype=f32)}
    inv = 1.0 / 10000.0 ** (np.arange(0, DH0, 2, dtype=f32) / DH0)
    angle = np.outer(np.arange(T, dtype=f32), inv)
    cos = np.concatenate([np.cos(angle), np.cos(angle)], -1)[:, ::2].T.astype(f32)
    sin = np.concatenate([np.sin(angle), np.sin(angle)], -1)[:, ::2].T.astype(f32)
    t["cos0"] = np.ascontiguousarray(np.tile(cos, (4, 1)))
    t["sin0"] = np.ascontiguousarray(np.tile(np.concatenate([-sin, sin], 0), (2, 1)))
    theta = (1.0 / 10000.0 ** (2.0 * np.arange(HALF1, dtype=f32) / f32(ROPE1))).astype(np.float64)
    place = np.arange(T)

    def turn(steps, scale=1.0):
        c, s = scale * np.cos(np.outer(steps, theta)), scale * np.sin(np.outer(steps, theta))
        return np.concatenate([c, c], 1).astype(f32), np.concatenate([-s, s], 1).astype(f32)

    near = np.where(place < LW, place, 2 * place - LW + 1)
    for name, steps, scale in (("k", place, 1.0), ("near", near, SCALE1), ("q", place, SCALE1)):
        for part, table in zip(("cos_", "sin_"), turn(steps, scale)):
            t[part + name] = table.reshape(NT, P, ROPE1).transpose(1, 0, 2)
    t["cos_far"], t["sin_far"] = (np.tile(v, (4, 1)) for v in turn(LW + np.arange(FAR)))
    l, k = np.arange(P)[:, None], np.arange(P)[None, :]
    t["cap"] = np.where(k <= l, 3.4e38, -3.3e38).astype(f32)
    k = np.arange(KTS)[None, :]
    t["cap0"] = np.where(k <= l - LW, 3.4e38, np.where(k <= l, -3.3e38, -1e36 * (k + 1))).astype(f32)
    row = np.arange(P)
    i4, quarter = row // 32, row % 32 // H1
    l = (32 * quarter + i4)[:, None, None] + 4 * np.arange(NG)[None, :, None]
    s = np.arange(WIN)[None, None, :] - P
    gathered = np.broadcast_to(np.arange(P)[None, None, :] // FAR == quarter[:, None, None], (P, NG, P))
    first = np.where(l < LW, (s >= 0) & (s < KTS), (s > l - LW) & (s <= l))
    rest = (s > l - LW) & (s <= l)
    for name, keep in (("mask_first", [first, gathered & (l >= LW)]), ("mask", [rest, gathered])):
        t[name] = bfloat16(np.where(np.concatenate(keep, 2), 0.0, -1e30))
    t["unit"] = bfloat16(np.eye(P))
    t["iota"] = np.tile(np.arange(E0, dtype=f32), (P, 1))
    return t


def layouts(a):
    even_odd = np.concatenate([np.arange(0, DH0, 2), np.arange(1, DH0, 2)])
    odd_even = np.concatenate([np.arange(1, DH0, 2), np.arange(0, DH0, 2)])
    twice = lambda w, axis: np.concatenate([w, w], axis)

    def up(w, order):
        w = w.reshape(H0, DH0, LAT0)[:, order, :].transpose(2, 0, 1)
        return twice(twice(w, 2).reshape(LAT0, H0 * P), 0)

    m = {
        "x": a["L0_attn_x"].reshape(T, D),
        "ln_scale": a["L0_attn_ln_scale"].reshape(D, 1),
        "ln_bias": a["L0_attn_ln_bias"].reshape(D, 1),
        "wdq": twice(a["L0_attn_w_down_q"].T, 1),
        "wdkv": twice(a["L0_attn_w_down_kv"].T, 1),
        "wq": up(a["L0_attn_w_up_q"], even_odd),
        "wq_sw": up(a["L0_attn_w_up_q"], odd_even),
        "wk": up(a["L0_attn_w_up_k"], even_odd),
        "wk_sw": up(a["L0_attn_w_up_k"], odd_even),
        "wv": twice(a["L0_attn_w_up_v"].T, 0),
        "wg": a["L0_ffn_Wg"].T,
        "e0_w1": a["L0_ffn_W1"].transpose(0, 2, 1),
        "e0_w3": a["L0_ffn_W3"].transpose(0, 2, 1),
        "e0_w2": a["L0_ffn_W2"].transpose(0, 2, 1),
        "e0_b13": np.stack([a["L0_ffn_b1"], a["L0_ffn_b3"]], 2),
        "e0_b2": a["L0_ffn_b2"],
        "wkvr": np.concatenate([a["L1_attn_W_dkv"], a["L1_attn_W_kr"]], 1),
        "a1_wdq": a["L1_attn_W_dq"],
        "wuq": a["L1_attn_W_uq"].reshape(CQ, H1, DH1).transpose(2, 1, 0),
        "wuk": a["L1_attn_W_uk"].reshape(CKV, H1, DH1).transpose(2, 1, 0),
        "wuv": a["L1_attn_W_uv"].reshape(CKV, H1, DH1).transpose(2, 1, 0),
        "wqr": a["L1_attn_W_qr"],
        "a1_wo": a["L1_attn_W_out"].reshape(H1, DH1, D).transpose(1, 0, 2),
        "widxq": twice(a["L1_attn_idx_wq"].reshape(D, NIDX, DH1), 2).reshape(D, NIDX * P),
        "widxk": twice(a["L1_attn_idx_wk"], 1),
        "idx_w": np.tile(a["L1_attn_idx_w"], (P, 1)),
        "sw1": a["L1_ffn_sw1"],
        "sw3": a["L1_ffn_sw3"],
        "sw2": a["L1_ffn_sw2"].reshape(KS, P, D).transpose(1, 0, 2),
        "sb13": np.stack([a["L1_ffn_sb1"].reshape(KS, P).T, a["L1_ffn_sb3"].reshape(KS, P).T], 1),
        "sb2": a["L1_ffn_sb2"].reshape(D, 1),
        "e1_w1": a["L1_ffn_w1"].transpose(1, 0, 2),
        "e1_b1": a["L1_ffn_b1"].T,
        "e1_w2": a["L1_ffn_w2"].transpose(1, 0, 2),
        "e1_b2": a["L1_ffn_b2"][CLASS_EXPERTS].transpose(2, 1, 0),
        "w_out": a["L0_attn_w_out"].reshape(D, H0 // 2, P).transpose(2, 1, 0).reshape(P, H0 // 2 * D),
    }
    return m


def kernel(**inputs):
    import concourse.bacc as bacc
    from concourse.bass_utils import run_bass_kernel_spmd as run

    nc = bacc.Bacc("TRN2", target_bir_lowering=False, num_devices=1)
    arrays, dram = {}, {}
    host = layouts({k: np.asarray(v) for k, v in inputs.items()})
    host.update(tables())
    for name, a in host.items():
        a = np.ascontiguousarray(a)
        arrays["in_" + name] = a
        dram[name] = nc.dram_tensor("in_" + name, a.shape, mybir.dt.from_np(a.dtype), kind="ExternalInput").ap()
    dram["out"] = nc.dram_tensor("out_0", (T, D), F32, kind="ExternalOutput").ap()
    dram["key_table"] = nc.dram_tensor("key_table", (T, KW), F32, kind="Internal").ap()
    build(nc, dram)
    r = run(nc, [arrays], core_ids=[0])
    return r.results[0]["out_0"].reshape(1, T, D)
```
